# Optimizing a Trainium2 kernel written in Bass

```python
import numpy as np
import jax
import jax.numpy as jnp

def _softmax(x, axis=-1):
    return jax.nn.softmax(x, axis=axis)

def _gelu(x):
    return jax.nn.gelu(x, approximate=True)

def _silu(x):
    return jax.nn.silu(x)

def _sigmoid(x):
    return jax.nn.sigmoid(x)

def _layernorm(x, axis=-1, eps=1e-05):
    m = jnp.mean(x, axis=axis, keepdims=True)
    v = jnp.var(x, axis=axis, keepdims=True)
    return (x - m) / jnp.sqrt(v + eps)

def _scatter_add(tgt, idx, src, axis=0):
    return tgt.at[idx].add(src)

def _segment_sum(src, seg, n):
    return jax.ops.segment_sum(src, seg, n)
kernel_name = 'mk_gps_d1_gnn_r64_491ace'

def setup_inputs(seed: int=0):
    np.random.seed(seed)
    _w = jnp.asarray

    def _rec_inputs():
        import jax
        import jax.numpy as jnp
        _gk = jax.random.key(seed)
        x = -0.0003713 + 1 * jax.random.normal(jax.random.fold_in(_gk, 1), (50000, 256), jnp.float32)
        src = jax.random.randint(jax.random.fold_in(_gk, 2), (12500,), 0, 50000, jnp.int32)
        dst = jnp.minimum((50000 * jax.random.uniform(jax.random.fold_in(_gk, 3), (12500,)) ** 2.0).astype(jnp.int32), 49999)
        _o = jnp.argsort(dst, stable=True)
        src = src[_o]
        dst = dst[_o]
        return (x, src, dst)
    x, src, dst = _rec_inputs()

    def _L0_gnn_setup():
        import jax, jax.numpy as jnp
        import numpy as np
        N_NODES = 50000
        N_EDGES = 25000
        IN_DIM, OUT_DIM, N_HEADS = (256, 64, 4)
        EPS = 1e-12
        key = jax.random.key(seed)
        k1, k2, k3, k4, k5 = jax.random.split(key, 5)
        h = jax.random.normal(k1, (N_NODES, IN_DIM), dtype=jnp.float32)
        edge_index = jax.random.randint(k2, (2, N_EDGES), 0, N_NODES, dtype=jnp.int32)
        W = jax.random.normal(k3, (IN_DIM, OUT_DIM), dtype=jnp.float32) * 0.05
        Wl = jax.random.normal(k4, (N_HEADS, OUT_DIM), dtype=jnp.float32) * 0.05
        Wr = jax.random.normal(k5, (N_HEADS, OUT_DIM), dtype=jnp.float32) * 0.05
        b = jnp.zeros((OUT_DIM,), dtype=jnp.float32)
        return {'h': h, 'W': W, 'Wl': Wl, 'Wr': Wr, 'b': b, 'edge_index': edge_index}
    _L0_gnn_all = _L0_gnn_setup()
    _L0_gnn_in = {k: v for k, v in _L0_gnn_all.items() if k in ('W', 'Wl', 'Wr', 'b')}
    del _L0_gnn_all

    def _L0_mix_setup():
        import jax, jax.numpy as jnp
        import numpy as np
        EPS_NORM = 1e-06
        EPS_ATTN = 1e-06
        HEADS = 8

        def rmsnorm(x, w):
            ms = jnp.mean(x * x, axis=-1, keepdims=True)
            return w * (x * jax.lax.rsqrt(ms + EPS_NORM))

        def linear_attention(x, w_qkv, w_out, b_out):
            B, N, D = x.shape
            hd = D // HEADS
            qkv = (x @ w_qkv).reshape(B, N, 3, HEADS, hd)
            q, k, v = (qkv[:, :, 0], qkv[:, :, 1], qkv[:, :, 2])
            q = jax.nn.elu(q) + 1.0
            k = jax.nn.elu(k) + 1.0
            kv = jnp.einsum('bnhd,bnhm->bhdm', k, v)
            z = 1.0 / (jnp.einsum('bnhd,bhd->bnh', q, k.sum(axis=1)) + EPS_ATTN)
            out = jnp.einsum('bnhd,bhdm,bnh->bnhm', q, kv, z)
            out = out.reshape(B, N, D)
            return out @ w_out + b_out
        key = jax.random.key(seed)
        ks = jax.random.split(key, 4)
        B, N, D = (16, 128, 256)
        x = jax.random.normal(ks[0], (B, N, D), dtype=jnp.float32)
        w_norm1 = jnp.ones((D,), dtype=jnp.float32)
        w_qkv = jax.random.normal(ks[1], (D, 3 * D), dtype=jnp.float32) * 0.02
        w_out = jax.random.normal(ks[2], (D, D), dtype=jnp.float32) * 0.02
        b_out = jnp.zeros((D,), dtype=jnp.float32)
        w_norm2 = jnp.ones((D,), dtype=jnp.float32)
        return {'x': x, 'w_norm1': w_norm1, 'w_qkv': w_qkv, 'w_out': w_out, 'b_out': b_out, 'w_norm2': w_norm2}
    _L0_mix_all = _L0_mix_setup()
    _L0_mix_in = {k: v for k, v in _L0_mix_all.items() if k in ('w_norm1', 'w_qkv', 'w_out', 'b_out', 'w_norm2')}
    del _L0_mix_all

    def _L0_ffn_setup():
        import jax, jax.numpy as jnp
        import numpy as np
        B, S, D = (8, 64, 256)
        H = 4 * D
        CAPACITY = 0.5
        key = jax.random.key(seed)
        ks = jax.random.split(key, 6)
        x = jax.random.normal(ks[0], (B, S, D), dtype=jnp.float32)
        attention_mask = jnp.zeros((B, 1, 1, S), dtype=jnp.float32)
        wr = jax.random.normal(ks[1], (D, 1), dtype=jnp.float32) * 0.02
        br = jnp.zeros((1,), dtype=jnp.float32)
        w1 = jax.random.normal(ks[2], (D, H), dtype=jnp.float32) * 0.02
        b1 = jnp.zeros((H,), dtype=jnp.float32)
        w2 = jax.random.normal(ks[3], (H, D), dtype=jnp.float32) * 0.02
        b2 = jnp.zeros((D,), dtype=jnp.float32)
        return {'x': x, 'attention_mask': attention_mask, 'wr': wr, 'br': br, 'w1': w1, 'b1': b1, 'w2': w2, 'b2': b2}
    _L0_ffn_all = _L0_ffn_setup()
    _L0_ffn_in = {k: v for k, v in _L0_ffn_all.items() if k in ('attention_mask', 'wr', 'br', 'w1', 'b1', 'w2', 'b2')}
    del _L0_ffn_all
    return {'x': x, 'src': src, 'dst': dst, 'L0_gnn_W': _L0_gnn_in['W'], 'L0_gnn_Wl': _L0_gnn_in['Wl'], 'L0_gnn_Wr': _L0_gnn_in['Wr'], 'L0_gnn_b': _L0_gnn_in['b'], 'L0_mix_w_norm1': _L0_mix_in['w_norm1'], 'L0_mix_w_qkv': _L0_mix_in['w_qkv'], 'L0_mix_w_out': _L0_mix_in['w_out'], 'L0_mix_b_out': _L0_mix_in['b_out'], 'L0_mix_w_norm2': _L0_mix_in['w_norm2'], 'L0_ffn_attention_mask': _L0_ffn_in['attention_mask'], 'L0_ffn_wr': _L0_ffn_in['wr'], 'L0_ffn_br': _L0_ffn_in['br'], 'L0_ffn_w1': _L0_ffn_in['w1'], 'L0_ffn_b1': _L0_ffn_in['b1'], 'L0_ffn_w2': _L0_ffn_in['w2'], 'L0_ffn_b2': _L0_ffn_in['b2']}

def reference(x, src, dst, L0_gnn_W, L0_gnn_Wl, L0_gnn_Wr, L0_gnn_b, L0_mix_w_norm1, L0_mix_w_qkv, L0_mix_w_out, L0_mix_b_out, L0_mix_w_norm2, L0_ffn_attention_mask, L0_ffn_wr, L0_ffn_br, L0_ffn_w1, L0_ffn_b1, L0_ffn_w2, L0_ffn_b2):
    import jax
    import jax.numpy as jnp

    def _L0_gnn_ref(h, W, Wl, Wr, b, edge_index):
        import jax, jax.numpy as jnp
        import numpy as np
        N_NODES = 50000
        N_EDGES = 25000
        IN_DIM, OUT_DIM, N_HEADS = (256, 64, 4)
        EPS = 1e-12
        N = h.shape[0]
        H = Wl.shape[0]
        x = h @ W
        el = x @ Wl.T
        er = x @ Wr.T
        src, dst = (edge_index[0], edge_index[1])
        e = el[src] + er[dst]
        e = jnp.exp(jax.nn.leaky_relu(e, negative_slope=0.2))
        rowsum = jax.ops.segment_sum(e, src, num_segments=N)
        w = e / jnp.maximum(rowsum, EPS)[src]
        heads = [jax.ops.segment_sum(w[:, hd:hd + 1] * x[dst], src, num_segments=N) for hd in range(H)]
        out = jnp.stack(heads, axis=1)
        out = jax.nn.elu(out + b)
        return out.reshape(N, H * x.shape[1])

    def _L0_mix_ref(x, w_norm1, w_qkv, w_out, b_out, w_norm2):
        import jax, jax.numpy as jnp
        import numpy as np
        EPS_NORM = 1e-06
        EPS_ATTN = 1e-06
        HEADS = 8

        def rmsnorm(x, w):
            ms = jnp.mean(x * x, axis=-1, keepdims=True)
            return w * (x * jax.lax.rsqrt(ms + EPS_NORM))

        def linear_attention(x, w_qkv, w_out, b_out):
            B, N, D = x.shape
            hd = D // HEADS
            qkv = (x @ w_qkv).reshape(B, N, 3, HEADS, hd)
            q, k, v = (qkv[:, :, 0], qkv[:, :, 1], qkv[:, :, 2])
            q = jax.nn.elu(q) + 1.0
            k = jax.nn.elu(k) + 1.0
            kv = jnp.einsum('bnhd,bnhm->bhdm', k, v)
            z = 1.0 / (jnp.einsum('bnhd,bhd->bnh', q, k.sum(axis=1)) + EPS_ATTN)
            out = jnp.einsum('bnhd,bhdm,bnh->bnhm', q, kv, z)
            out = out.reshape(B, N, D)
            return out @ w_out + b_out
        h = x + linear_attention(rmsnorm(x, w_norm1), w_qkv, w_out, b_out)
        return h + rmsnorm(h, w_norm2)

    def _L0_ffn_ref(x, attention_mask, wr, br, w1, b1, w2, b2):
        import jax, jax.numpy as jnp
        import numpy as np
        B, S, D = (8, 64, 256)
        H = 4 * D
        CAPACITY = 0.5
        b, s, d = x.shape
        weights = (jnp.einsum('bsd,do->bso', x, wr) + br)[..., 0]
        k = max(1, int(CAPACITY * s))
        kk = k - 1 if k > 1 else 1
        _, idx = jax.lax.top_k(weights, k)
        sel_idx = idx[:, :kk]
        sel = jnp.take_along_axis(x, sel_idx[:, :, None], axis=1)
        h = jax.nn.gelu(jnp.einsum('bkd,dh->bkh', sel, w1) + b1)
        y = jnp.einsum('bkh,hd->bkd', h, w2) + b2
        w_sel = jnp.take_along_axis(weights, sel_idx, axis=1)
        y = y * w_sel[..., None]
        batch_idx = jnp.arange(b)[:, None]
        processed = jnp.zeros_like(x).at[batch_idx, sel_idx].set(y)
        return processed + x
    edge_index = jnp.stack([src, dst])
    xn = _layernorm(x, axis=-1)
    x = x + _L0_gnn_ref(xn, L0_gnn_W, L0_gnn_Wl, L0_gnn_Wr, L0_gnn_b, edge_index) + _L0_mix_ref(xn[None], L0_mix_w_norm1, L0_mix_w_qkv, L0_mix_w_out, L0_mix_b_out, L0_mix_w_norm2)[0]
    x = x + _L0_ffn_ref(_layernorm(x, axis=-1)[None], L0_ffn_attention_mask, L0_ffn_wr, L0_ffn_br, L0_ffn_w1, L0_ffn_b1, L0_ffn_w2, L0_ffn_b2)[0]
    return x

_drawn_inputs = setup_inputs


def setup_inputs(seed=0):
    import zlib

    import numpy as np

    out = dict(_drawn_inputs(seed))
    spreads = {'L0_gnn_b': (0.0, 0.1),
     'L0_mix_w_norm1': (1.0, 0.6),
     'L0_mix_b_out': (0.0, 0.1),
     'L0_mix_w_norm2': (1.0, 0.2),
     'L0_ffn_b1': (0.0, 0.8),
     'L0_ffn_b2': (0.0, 0.8)}
    factors = {'L0_gnn_Wl': 8.0,
     'L0_gnn_Wr': 8.0,
     'L0_mix_w_qkv': 8.0,
     'L0_mix_w_out': 8.0,
     'L0_ffn_wr': 7.822,
     'L0_ffn_w1': 8.0,
     'L0_ffn_w2': 8.0}
    for name, (base, spread) in spreads.items():
        noise = np.random.default_rng([zlib.crc32(name.encode()), seed]).standard_normal(out[name].shape)
        drawn = base * np.exp(spread * noise) if base else spread * noise
        out[name] = jnp.asarray(drawn.astype(out[name].dtype))
    for name, factor in factors.items():
        out[name] = (out[name] * factor).astype(out[name].dtype)
    return out
```

```python
from contextlib import ExitStack, contextmanager

import concourse.bass as bass
from concourse import mybir

ALU = mybir.AluOpType
ACT = mybir.ActivationFunctionType
AX = mybir.AxisListType
F32 = mybir.dt.float32
F16 = mybir.dt.float16
I32 = mybir.dt.int32

P = 128
LN_EPS = 1e-5
RMS_EPS = 1e-6
ATTN_EPS = 1e-6
GNN_EPS = 1e-12
ATTN_HEADS = 8


class At:

    def __init__(self, n, buf, turn):
        self.n, self.buf, self.turn = n, buf, turn

    def __add__(self, k):
        return At(self.n + k, (self.buf + k) % 2, self.turn + (self.buf + k) // 2)

    def inside(self, lo, hi):
        return not isinstance(self.n, int) or lo <= self.n < hi


def run_steps(eng, body, peeled, loop_end, end):
    for n in range(peeled):
        body(At(n, n % 2, n // 2))
    if loop_end > peeled:
        with eng.Fori(peeled // 2, loop_end // 2) as i:
            body(At(2 * i, 0, i))
            body(At(2 * i + 1, 1, i))
    for n in range(loop_end, end):
        body(At(n, n % 2, n // 2))


def gps_layer(nc, x, src, dst, gnn_W, gnn_Wl, gnn_Wr, gnn_b, w_norm1, w_qkv, w_out, b_out, w_norm2,
              wr, br, w1, b1, w2, b2, out):
    N, D = x.shape
    E = src.shape[0]
    OD = gnn_W.shape[1]
    GH = gnn_Wl.shape[0]
    H = w1.shape[1]
    KB = D // P
    FB = H // P
    T = 4
    ROWS = T * P
    NG = -(-N // ROWS)
    LAST0 = N - ROWS
    SEEN = (NG - 1) * ROWS - LAST0
    SEEN_P = SEEN // T
    EP, EC = 125, 100
    assert EP * EC == E and SEEN_P * T == SEEN and NG % 2 == 0
    PADN = 392 * P
    MSG = GH * OD + GH
    TP, TC = 125, 400
    assert TP * TC == N
    CAP = N // 2 - 1
    NF = -(-CAP // ROWS)
    SKIP = 100000.0

    xg_v = x[0:(NG - 1) * ROWS, :].rearrange("(g p j) d -> g p (j d)", p=P, j=T)
    x_last = x[LAST0:N, :].rearrange("(p j) d -> p (j d)", j=T)

    def group_rows(table, at, d):
        if isinstance(at.n, int) and at.n == NG - 1:
            return table[LAST0:N, :].rearrange("(p j) d -> p (j d)", j=T)
        return table[0:(NG - 1) * ROWS, :].rearrange("(g p j) d -> g p (j d)", p=P, j=T)[at.n]

    acc_d = nc.dram_tensor("gnn_acc", (PADN, MSG), F32, kind="Internal").ap()
    gnn_d = nc.dram_tensor("gnn_rows", (PADN, D), F32, kind="Internal").ap()
    aux_d = nc.dram_tensor("aux_rows", (N, 4), F32, kind="Internal").ap()
    wt_d = nc.dram_tensor("router_rows", (N, 1), F32, kind="Internal").ap()

    with ExitStack() as whole:
        def keep(name, shape, dt=F32):
            return whole.enter_context(nc.sbuf_tensor(name, shape, dt))

        held = []

        def sem(name):
            held.append(nc.alloc_semaphore(name=name))
            return held[-1]

        def wait_apart(eng, signal, value):
            eng.wait_ge(signal, value)
            if not isinstance(value, int):
                eng.sem_inc(passed[0], 1)

        passed, phases = [], []

        @contextmanager
        def phase():
            phases.append(1)
            passed[:] = [sem(f"waits_passed{len(phases)}")]
            with ExitStack() as stack:
                yield stack
            nc.clear_and_free_semaphores(held)
            held.clear()
            nc.all_engine_barrier()

        ident = keep("ident", [P, P])
        before = keep("before", [P, P])
        after = keep("after", [P, P])
        ones = keep("ones", [P, P])
        headmask = keep("headmask", [P, P])
        mask8 = keep("mask8", [P, KB, ATTN_HEADS])
        spread8 = keep("spread8", [ATTN_HEADS, KB, P])
        wqkv = keep("wqkv", [P, KB, 3 * D])
        wout = keep("wout", [P, KB, D])
        mix = keep("mix", [P, KB, D])
        ks8 = keep("ks8", [P, KB, ATTN_HEADS])
        bout_b = keep("bout_b", [P, D])
        wn2_b = keep("wn2_b", [P, D])
        wr_b = keep("wr_b", [P, D])
        br_b = keep("br_b", [P, 1])
        b2_b = keep("b2_b", [P, D])
        gb_b = keep("gb_b", [P, OD])
        b1c = keep("b1c", [P, FB])
        mean_a = keep("mean_a", [P, NG * T])
        scale_a = keep("scale_a", [P, NG * T])
        back_a = keep("back_a", [P, NG * T])
        rw_a = keep("rw_a", [P, 4])
        wD = keep("wD", [P, KB, OD + GH])
        wS = keep("wS", [P, KB, GH])
        halfneg = keep("halfneg", [P, 8])

        with phase() as ph:
            def sb(name, shape, dt=F32):
                return ph.enter_context(nc.sbuf_tensor(name, shape, dt))
            gw = sb("gw", [P, KB, OD])
            wlr = sb("wlr", [2 * GH, OD])
            wlrT = sb("wlrT", [OD, 2 * GH])
            gwT = sb("gwT", [OD, KB, P])
            wn1c = sb("wn1c", [P, KB])
            wrsum = sb("wrsum", [P, 1])
            wr_raw = sb("wr_raw", [P, D])
            zero = sb("zero", [P, 2080])
            eb = sb("eb", [P, OD])
            eb1 = sb("eb1", [P, OD])
            ebrow = sb("ebrow", [P, 8 * GH, OD])
            pT = ph.enter_context(nc.psum_tensor("pT", [P, 512], F32))
            pW = ph.enter_context(nc.psum_tensor("pW", [P, 512], F32))
            loaded = sem("weights_loaded")
            made = sem("pool_masks_made")
            blank = sem("blank_masks_ready")
            dve_masks = sem("dve_masks_made")
            scaled = sem("weights_scaled")
            wrmean = sem("router_sum_ready")
            eb_exp = sem("bias_exp_ready")
            eb_min = sem("bias_min_ready")
            eb_elu = sem("bias_elu_ready")
            eb_rows = sem("bias_rows_ready")
            zero_ready = sem("zero_ready")
            fold_t = sem("fold_transposed")
            fold_c = sem("fold_copied")
            fold_m = sem("fold_product_ready")
            fold_d = sem("fold_done")
            table_init = sem("tables_written")
            with nc.Block() as block:
                @block.sync
                def _(sp):
                    loads = 0
                    with nc.allow_non_contiguous_dma(reason="a few small weight columns"):
                        for dst_ap, src_ap in (
                            (gw[:], gnn_W.rearrange("(k p) n -> p k n", p=P)),
                            (wlr[0:GH, :], gnn_Wl), (wlr[GH:2 * GH, :], gnn_Wr),
                            (gb_b[:], gnn_b.partition_broadcast(P)),
                            (wn1c[:], w_norm1.rearrange("(k p) -> p k", p=P)),
                            (wqkv[:], w_qkv.rearrange("(k p) n -> p k n", p=P)),
                            (wout[:], w_out.rearrange("(k p) n -> p k n", p=P)),
                            (bout_b[:], b_out.partition_broadcast(P)),
                            (wn2_b[:], w_norm2.partition_broadcast(P)),
                            (wr_raw[:], wr.rearrange("d o -> (d o)").partition_broadcast(P)),
                            (br_b[:], br.partition_broadcast(P)),
                            (b2_b[:], b2.partition_broadcast(P)),
                            (b1c[:], b1.rearrange("(k p) -> p k", p=P)),
                        ):
                            sp.dma_start(dst_ap, src_ap).then_inc(loaded, 16)
                            loads += 1
                    assert loads == 13
                    sp.wait_ge(eb_rows, 1)
                    gi = gnn_d.rearrange("(g p j) d -> g p (j d)", p=P, j=8)
                    with sp.Fori(0, PADN // (8 * P)) as i:
                        sp.dma_start(gi[i], ebrow[:].rearrange("p a b -> p (a b)")).then_inc(table_init, 16)
                    sp.wait_ge(table_init, 2 * 16 * (PADN // (8 * P)))

                @block.gpsimd
                def _(pool):
                    pool.wait_ge(blank, 5)
                    pool.affine_select(out=ident[:], in_=ident[:], compare_op=ALU.not_equal, fill=1.0, base=0,
                                       pattern=[[-1, P]], channel_multiplier=1).then_inc(made, 1)
                    pool.affine_select(out=before[:], in_=ones[:], compare_op=ALU.is_gt, fill=0.0, base=0,
                                       pattern=[[-1, P]], channel_multiplier=1).then_inc(made, 1)
                    pool.affine_select(out=after[:], in_=ones[:], compare_op=ALU.is_gt, fill=0.0, base=0,
                                       pattern=[[1, P]], channel_multiplier=-1).then_inc(made, 1)
                    pool.affine_select(out=spread8[:].rearrange("h k (q e) -> h k q e", e=32),
                                       in_=spread8[:].rearrange("h k (q e) -> h k q e", e=32),
                                       compare_op=ALU.not_equal, fill=1.0, base=0,
                                       pattern=[[-4, KB], [-1, 4], [0, 32]], channel_multiplier=1).then_inc(made, 1)

                @block.vector
                def _(dve):
                    dve.memset(ident[:], 0.0).then_inc(blank, 1)
                    dve.memset(ones[:], 1.0).then_inc(blank, 1)
                    dve.memset(spread8[:], 0.0).then_inc(blank, 1)
                    dve.memset(headmask[:], 0.0).then_inc(blank, 1)
                    dve.memset(mask8[:], 0.0).then_inc(blank, 1)
                    dve.memset(halfneg[:], -0.5)
                    dve.memset(zero[:], 0.0).then_inc(zero_ready, 1)
                    dve.wait_ge(blank, 5)
                    for q in range(4):
                        dve.memset(headmask[32 * q:32 * q + 32, 32 * q:32 * q + 32], 1.0)
                        for k in range(KB):
                            last = dve.memset(mask8[32 * q:32 * q + 32, k, 4 * k + q:4 * k + q + 1], 1.0)
                    last.then_inc(dve_masks, 1)
                    dve.wait_ge(loaded, 13 * 16)
                    for k in range(KB):
                        dve.tensor_scalar(wqkv[:, k, :], wqkv[:, k, :], wn1c[:, k:k + 1], None, ALU.mult)\
                           .then_inc(scaled, 1)
                    dve.tensor_reduce(wrsum[:], wr_raw[:], AX.X, ALU.add).then_inc(wrmean, 1)
                    dve.wait_ge(wrmean, 1)
                    dve.tensor_scalar(wrsum[:], wrsum[:], 1.0 / D, None, ALU.mult).then_inc(wrmean, 1)
                    dve.wait_ge(wrmean, 2)
                    dve.tensor_scalar(wr_b[:], wr_raw[:], wrsum[:, 0:1], None, ALU.subtract).then_inc(wrmean, 1)
                    dve.wait_ge(eb_exp, 1)
                    dve.tensor_scalar(eb1[:], eb[:], 1.0, -1.0, ALU.min, ALU.add).then_inc(eb_min, 1)
                    dve.wait_ge(eb_min, 1)
                    dve.tensor_tensor(eb[:], eb1[:], gb_b[:], ALU.max).then_inc(eb_elu, 1)
                    dve.wait_ge(eb_elu, 1)
                    dve.tensor_copy(ebrow[:], eb[:].unsqueeze(1).to_broadcast([P, 8 * GH, OD])).then_inc(eb_rows, 1)
                    dve.wait_ge(fold_t, 1)
                    dve.tensor_copy(gwT[:], pT[0:OD, 0:KB * P].rearrange("p (k n) -> p k n", k=KB)).then_inc(fold_c, 1)
                    dve.tensor_copy(wlrT[:], pT[0:OD, KB * P:KB * P + 2 * GH]).then_inc(fold_c, 1)
                    dve.tensor_copy(wD[:, :, 0:OD], gw[:]).then_inc(fold_d, 1)
                    dve.wait_ge(fold_m, 1)
                    pv = pW[:, 0:KB * 2 * GH].rearrange("p (k n) -> p k n", k=KB)
                    dve.tensor_copy(wS[:], pv[:, :, 0:GH]).then_inc(fold_d, 1)
                    dve.tensor_copy(wD[:, :, OD:OD + GH], pv[:, :, GH:2 * GH]).then_inc(fold_d, 1)

                @block.scalar
                def _(act):
                    act.wait_ge(loaded, 13 * 16)
                    act.activation(eb[:], gb_b[:], ACT.Exp).then_inc(eb_exp, 1)
                    act.wait_ge(zero_ready, 1)
                    per = PADN * MSG // P // 2080
                    za = acc_d.rearrange("r c -> (r c)").rearrange("(g p c) -> g p c", p=P, c=2080)
                    assert per == PADN // (8 * P)
                    with act.Fori(0, per) as i:
                        act.dma_start(za[i], zero[:]).then_inc(table_init, 16)

                @block.tensor
                def _(pe):
                    pe.wait_ge(loaded, 13 * 16)
                    pe.wait_ge(made, 4)
                    for k in range(KB):
                        pe.transpose(pT[0:OD, k * P:(k + 1) * P], gw[:, k, :], ident[:])
                    pe.transpose(pT[0:OD, KB * P:KB * P + 2 * GH], wlr[:], ident[0:2 * GH, 0:2 * GH]).then_inc(fold_t, 1)
                    pe.wait_ge(fold_c, 2)
                    for k in range(KB):
                        last = pe.matmul(pW[:, 2 * GH * k:2 * GH * (k + 1)], gwT[:, k, :], wlrT[:], start=True, stop=True)
                    last.then_inc(fold_m, 1)

        with phase() as ph:
            def sb(name, shape, dt=F32):
                return ph.enter_context(nc.sbuf_tensor(name, shape, dt))
            i_dst = sb("i_dst", [P, EC], I32)
            i_src = sb("i_src", [P, EC], I32)
            i_own = sb("i_own", [P, EC], I32)
            i_acc = sb("i_acc", [P, EC], I32)
            pair = [sb(f"pair{u}", [P, 2], I32) for u in range(2)]
            goal = [sb(f"goal{u}", [P, 1], I32) for u in range(2)]
            ix_col = sem("edge_columns_ready")
            ix_col2 = sem("target_columns_ready")
            i_dump = sb("i_dump", [P, 1], I32)
            dump = sb("dump", [P, 1])
            own = sb("own", [P, EC])
            ends = [sb(f"ends{u}", [P, 2, D]) for u in range(2)]
            st = [sb(f"st{u}", [P, 2, 6]) for u in range(2)]
            mv = [sb(f"mv{u}", [P, 2, 2]) for u in range(2)]
            rs = [sb(f"rs{u}", [P, 2]) for u in range(2)]
            norm = [sb(f"norm{u}", [P, 2, D]) for u in range(2)]
            normT = [sb(f"normT{u}", [P, 2 * KB, P]) for u in range(2)]
            ownb = [sb(f"ownb{u}", [P, P]) for u in range(2)]
            same = [sb(f"same{u}", [P, P]) for u in range(2)]
            junk = sb("junk", [P, P])
            cnt = [sb(f"cnt{u}", [P, 4]) for u in range(2)]
            ev = [sb(f"ev{u}", [P, 2 * GH]) for u in range(2)]
            msg = [sb(f"msg{u}", [P, MSG]) for u in range(2)]
            tot = [sb(f"tot{u}", [P, MSG]) for u in range(2)]
            pG = ph.enter_context(nc.psum_tensor("pG", [P, 2 * KB * P], F32))
            pX = ph.enter_context(nc.psum_tensor("pX", [P, 512], F32))
            pS = ph.enter_context(nc.psum_tensor("pS", [P, 512], F32))
            pM = ph.enter_context(nc.psum_tensor("pM", [P, 512], F32))
            idx_init = sem("index_blank")
            idx_load = sem("index_loaded")
            idx_float = sem("index_float")
            got = [sem(f"ends_gathered{u}") for u in range(2)]
            stat = sem("ends_stats")
            aggr = sem("ends_aggregated")
            veps = sem("ends_var_eps")
            rstd = sem("ends_rstd")
            normed = sem("ends_normed")
            turned = sem("ends_turned")
            copied = sem("ends_copied")
            projected = sem("ends_projected")
            spread = sem("own_spread")
            row = sem("own_row_ready")
            eq = sem("same_ready")
            counted = sem("earlier_counted")
            clipped = sem("earlier_clipped")
            gap = sem("dump_gap")
            target = sem("target_float")
            target_i = sem("target_ready")
            sc_copy = sem("score_copied")
            sc_lrelu = sem("score_lrelu")
            sc_exp = sem("score_exp")
            msgs = sem("messages_ready")
            summed = sem("messages_summed")
            tot_ready = sem("sums_copied")
            added = sem("sums_added")

            with nc.Block() as block:
                @block.sync
                def _(sp):
                    sp.wait_ge(idx_init, 3)
                    for t, a in ((i_dst, dst), (i_src, src), (i_own, src)):
                        sp.dma_start(t[0:EP, :], a.rearrange("(p c) -> p c", c=EC)).then_inc(idx_load, 16)

                @block.gpsimd
                def _(pool):
                    pool.iota(i_own[:], pattern=[[0, EC]], base=N, channel_multiplier=1).then_inc(idx_init, 1)
                    pool.iota(i_dst[:], pattern=[[0, EC]], base=0, channel_multiplier=0).then_inc(idx_init, 1)
                    pool.iota(i_src[:], pattern=[[0, EC]], base=0, channel_multiplier=0).then_inc(idx_init, 1)
                    pool.iota(i_dump[:], pattern=[[0, 1]], base=N, channel_multiplier=1).then_inc(idx_init, 1)
                    pool.wait_ge(idx_load, 48)

                    def gather(c):
                        if not (isinstance(c.n, int) and c.n < 2):
                            wait_apart(pool, normed, 2 * (c.n - 1))
                        for side, idx in enumerate((i_dst, i_src)):
                            pool.tensor_copy(pair[c.buf][:, side:side + 1], idx[:, bass.ds(c.n, 1)]).then_inc(ix_col, 1)
                        wait_apart(pool, ix_col, 2 * (c.n + 1))
                        for side in range(2):
                            pool.indirect_dma_start(
                                out=ends[c.buf][:, side, :], out_offset=None, in_=x,
                                in_offset=bass.IndirectOffsetOnAxis(ap=pair[c.buf][:, side:side + 1], axis=0)
                            ).then_inc(got[c.buf], 16)

                    def scatter(c):
                        pool.wait_ge(tot_ready, c.n + 1)
                        wait_apart(pool, target_i, c.n + 1)
                        if not (isinstance(c.n, int) and c.n == 0):
                            wait_apart(pool, added, 16 * c.n)
                        pool.indirect_dma_start(
                            out=acc_d, out_offset=bass.IndirectOffsetOnAxis(ap=goal[c.buf][:], axis=0),
                            in_=tot[c.buf][:], in_offset=None, compute_op=ALU.add).then_inc(added, 16)

                    def step(c):
                        if c.inside(0, EC):
                            gather(c)
                            wait_apart(pool, aggr, 2 * (c.n + 1))
                            if not (isinstance(c.n, int) and c.n < 2):
                                wait_apart(pool, normed, 2 * (c.n - 1))
                            pool.tensor_scalar(rs[c.buf][:], mv[c.buf][:, :, 1], LN_EPS, 1.0, ALU.add, ALU.mult)\
                                .then_inc(veps, 1)
                            wait_apart(pool, veps, c.n + 1)
                            pool.tensor_tensor(rs[c.buf][:], rs[c.buf][:], halfneg[:, 0:2], ALU.pow).then_inc(rstd, 1)
                        if (c + -1).inside(0, EC):
                            scatter(c + -1)
                    run_steps(pool, step, 2, EC, EC + 1)
                    pool.wait_ge(added, 16 * EC)

                @block.vector
                def _(dve):
                    dve.wait_ge(idx_init, 4)
                    dve.wait_ge(idx_load, 48)
                    dve.tensor_copy(own[:], i_own[:]).then_inc(idx_float, 1)
                    dve.tensor_copy(dump[:], i_dump[:]).then_inc(idx_float, 1)
                    dve.wait_ge(idx_float, 2)

                    def step(c):
                        u = c.buf
                        old = not (isinstance(c.n, int) and c.n < 2)
                        dve.wait_ge(got[u], 32 * (c.turn + 1))
                        for s in range(2):
                            dve.bn_stats(st[u][:, s, :], ends[u][:, s, :]).then_inc(stat, 1)
                        wait_apart(dve, stat, 2 * (c.n + 1))
                        for s in range(2):
                            dve.bn_aggr(mv[u][:, s, :], st[u][:, s, :]).then_inc(aggr, 1)
                        if old:
                            dve.wait_ge(row, c.n - 1)
                            dve.wait_ge(eq, c.n - 1)
                        dve.tensor_copy(ownb[u][:], own[:, bass.ds(c.n, 1)].to_broadcast([P, P])).then_inc(spread, 1)
                        dve.wait_ge(rstd, c.n + 1)
                        dve.wait_ge(aggr, 2 * (c.n + 1))
                        if old:
                            dve.wait_ge(turned, c.n - 1)
                        for s in range(2):
                            dve.tensor_scalar(norm[u][:, s, :], ends[u][:, s, :], mv[u][:, s, 0:1], rs[u][:, s:s + 1],
                                              ALU.subtract, ALU.mult).then_inc(normed, 1)
                        dve.wait_ge(row, c.n + 1)
                        if old:
                            dve.wait_ge(summed, c.n - 1)
                        dve.wait_ge(spread, c.n + 1)
                        dve.tensor_scalar(same[u][:], pS[:, 0:P], ownb[u][:, 0:1], None, ALU.is_equal).then_inc(eq, 1)
                        dve.wait_ge(eq, c.n + 1)
                        dve.tensor_tensor_reduce(junk[:], same[u][:], before[:], 1.0, 0.0, ALU.mult, ALU.add,
                                                 cnt[u][:, 0:1]).then_inc(counted, 1)
                        dve.tensor_scalar(cnt[u][:, 2:3], dump[:], ownb[u][:, 0:1], None, ALU.subtract).then_inc(gap, 1)
                        dve.wait_ge(counted, c.n + 1)
                        dve.tensor_scalar(cnt[u][:, 1:2], cnt[u][:, 0:1], 1.0, None, ALU.min).then_inc(clipped, 1)
                        dve.wait_ge(clipped, c.n + 1)
                        dve.wait_ge(gap, c.n + 1)
                        dve.scalar_tensor_tensor(out=cnt[u][:, 3:4], in0=cnt[u][:, 1:2], scalar=cnt[u][:, 2:3],
                                                 in1=ownb[u][:, 0:1], op0=ALU.mult, op1=ALU.add).then_inc(target, 1)
                        dve.wait_ge(target, c.n + 1)
                        if old:
                            dve.wait_ge(added, 16 * (c.n - 1))
                        dve.tensor_copy(goal[u][:], cnt[u][:, 3:4]).then_inc(target_i, 1)
                        dve.tensor_copy(i_acc[:, bass.ds(c.n, 1)], cnt[u][:, 3:4])
                        dve.wait_ge(projected, c.n + 1)
                        dve.tensor_copy(ev[u][:, 0:GH], pX[:, OD:OD + GH]).then_inc(sc_copy, 1)
                        dve.wait_ge(sc_copy, c.n + 1)
                        dve.scalar_tensor_tensor(out=ev[u][:, GH:2 * GH], in0=pX[:, OD:OD + GH], scalar=0.2,
                                                 in1=ev[u][:, 0:GH], op0=ALU.mult, op1=ALU.max).then_inc(sc_lrelu, 1)
                        dve.wait_ge(sc_exp, c.n + 1)
                        dve.tensor_tensor(msg[u][:, 0:GH * OD].rearrange("p (h d) -> p h d", h=GH),
                                          pX[:, 0:OD].unsqueeze(1).to_broadcast([P, GH, OD]),
                                          msg[u][:, GH * OD:MSG].unsqueeze(2).to_broadcast([P, GH, OD]), ALU.mult)\
                           .then_inc(msgs, 1)
                    run_steps(dve, step, 2, EC, EC)

                @block.scalar
                def _(act):
                    def step(c):
                        u = c.buf
                        old = not (isinstance(c.n, int) and c.n < 2)
                        act.wait_ge(turned, c.n + 1)
                        if old:
                            act.wait_ge(projected, c.n - 1)
                        act.activation(normT[u][:].rearrange("p a b -> p (a b)"), pG[:], ACT.Copy).then_inc(copied, 1)
                        act.wait_ge(sc_lrelu, c.n + 1)
                        if old:
                            act.wait_ge(summed, c.n - 1)
                        act.activation(msg[u][:, GH * OD:MSG], ev[u][:, GH:2 * GH], ACT.Exp).then_inc(sc_exp, 1)
                        act.wait_ge(summed, c.n + 1)
                        if old:
                            act.wait_ge(added, 16 * (c.n - 1))
                        act.activation(tot[u][:], pM[:, 0:MSG], ACT.Copy).then_inc(tot_ready, 1)
                    run_steps(act, step, 2, EC, EC)

                @block.tensor
                def _(pe):
                    def step(c):
                        u = c.buf
                        first = isinstance(c.n, int) and c.n == 0
                        pe.wait_ge(spread, c.n + 1)
                        if not first:
                            pe.wait_ge(eq, c.n)
                        pe.transpose(pS[:, 0:P], ownb[u][:], ident[:]).then_inc(row, 1)
                        pe.wait_ge(normed, 2 * (c.n + 1))
                        if not first:
                            pe.wait_ge(copied, c.n)
                        for s in range(2):
                            for k in range(KB):
                                last = pe.transpose(pG[:, (KB * s + k) * P:(KB * s + k + 1) * P],
                                                    norm[u][:, s, k * P:(k + 1) * P], ident[:])
                        last.then_inc(turned, 1)
                        pe.wait_ge(copied, c.n + 1)
                        if not first:
                            pe.wait_ge(msgs, c.n)
                        for k in range(KB):
                            pe.matmul(pX[:, 0:OD + GH], normT[u][:, k, :], wD[:, k, :], start=(k == 0),
                                      stop=(k == KB - 1), skip_group_check=True)
                        for k in range(KB):
                            last = pe.matmul(pX[:, OD:OD + GH], normT[u][:, KB + k, :], wS[:, k, :], start=False,
                                             stop=(k == KB - 1), skip_group_check=True)
                        last.then_inc(projected, 1)
                        pe.wait_ge(msgs, c.n + 1)
                        pe.wait_ge(eq, c.n + 1)
                        if not first:
                            pe.wait_ge(tot_ready, c.n)
                        pe.matmul(pM[:, 0:MSG], same[u][:], msg[u][:], start=True, stop=True).then_inc(summed, 1)
                    run_steps(pe, step, 2, EC, EC)

            ag = [sb(f"ag{u}", [P, MSG]) for u in range(2)]
            rr = [sb(f"rr{u}", [P, 2 * GH]) for u in range(2)]
            gv = [sb(f"gv{u}", [P, D]) for u in range(2)]
            ge = [sb(f"ge{u}", [P, D]) for u in range(2)]
            fetched = [sem(f"sums_fetched{u}") for u in range(2)]
            guard = sem("rowsum_guarded")
            recip = sem("rowsum_reciprocal")
            mean_r = sem("rows_normalised")
            biased = sem("rows_biased")
            expd = sem("rows_exp")
            mined = sem("rows_min")
            elud = sem("rows_elu")
            placed = sem("rows_placed")
            with nc.Block() as block:
                @block.gpsimd
                def _(pool):
                    def step(c):
                        if c.inside(0, EC):
                            if not (isinstance(c.n, int) and c.n < 2):
                                pool.wait_ge(mean_r, c.n - 1)
                                wait_apart(pool, placed, 16 * (c.n - 1))
                            pool.tensor_copy(goal[c.buf][:], i_acc[:, bass.ds(c.n, 1)]).then_inc(ix_col2, 1)
                            wait_apart(pool, ix_col2, c.n + 1)
                            pool.indirect_dma_start(
                                out=ag[c.buf][:], out_offset=None, in_=acc_d,
                                in_offset=bass.IndirectOffsetOnAxis(ap=goal[c.buf][:], axis=0)
                            ).then_inc(fetched[c.buf], 16)
                        m = c + -1
                        if m.inside(0, EC):
                            wait_apart(pool, elud, m.n + 1)
                            if not (isinstance(m.n, int) and m.n == 0):
                                wait_apart(pool, placed, 16 * m.n)
                            pool.indirect_dma_start(
                                out=gnn_d, out_offset=bass.IndirectOffsetOnAxis(ap=goal[m.buf][:], axis=0),
                                in_=gv[m.buf][:], in_offset=None).then_inc(placed, 16)
                    run_steps(pool, step, 2, EC, EC + 1)
                    pool.wait_ge(placed, 16 * EC)

                @block.vector
                def _(dve):
                    def step(c):
                        u = c.buf
                        dve.wait_ge(fetched[u], 16 * (c.turn + 1))
                        dve.tensor_scalar(rr[u][:, 0:GH], ag[u][:, GH * OD:MSG], GNN_EPS, None, ALU.max).then_inc(guard, 1)
                        dve.wait_ge(guard, c.n + 1)
                        dve.reciprocal(rr[u][:, GH:2 * GH], rr[u][:, 0:GH]).then_inc(recip, 1)
                        dve.wait_ge(recip, c.n + 1)
                        if not (isinstance(c.n, int) and c.n < 2):
                            dve.wait_ge(placed, 16 * (c.n - 1))
                        v3 = gv[u][:].rearrange("p (h d) -> p h d", h=GH)
                        dve.tensor_tensor(v3, ag[u][:, 0:GH * OD].rearrange("p (h d) -> p h d", h=GH),
                                          rr[u][:, GH:2 * GH].unsqueeze(2).to_broadcast([P, GH, OD]), ALU.mult)\
                           .then_inc(mean_r, 1)
                        dve.wait_ge(mean_r, c.n + 1)
                        dve.tensor_tensor(v3, v3, gb_b[:].unsqueeze(1).to_broadcast([P, GH, OD]), ALU.add)\
                           .then_inc(biased, 1)
                        dve.wait_ge(expd, c.n + 1)
                        dve.tensor_scalar(ge[u][:], ge[u][:], 1.0, -1.0, ALU.min, ALU.add).then_inc(mined, 1)
                        dve.wait_ge(mined, c.n + 1)
                        dve.tensor_tensor(gv[u][:], gv[u][:], ge[u][:], ALU.max).then_inc(elud, 1)
                    run_steps(dve, step, 2, EC, EC)

                @block.scalar
                def _(act):
                    def step(c):
                        act.wait_ge(biased, c.n + 1)
                        if not (isinstance(c.n, int) and c.n < 2):
                            act.wait_ge(elud, c.n - 1)
                        act.activation(ge[c.buf][:], gv[c.buf][:], ACT.Exp).then_inc(expd, 1)
                    run_steps(act, step, 2, EC, EC)

        with phase() as ph:
            def sb(name, shape, dt=F32):
                return ph.enter_context(nc.sbuf_tensor(name, shape, dt))
            xin = [sb(f"xin{u}", [P, T, D]) for u in range(2)]
            st = [sb(f"pst{u}", [P, T, 6]) for u in range(2)]
            mv = [sb(f"pmv{u}", [P, T, 2]) for u in range(2)]
            sc = [sb(f"psc{u}", [P, T]) for u in range(2)]
            sv = [sb(f"psv{u}", [P, T]) for u in range(2)]
            rq = [sb(f"prq{u}", [P, T]) for u in range(2)]
            xs = [sb(f"xs{u}", [P, T, D + 1]) for u in range(2)]
            xT = [sb(f"xT{u}", [P, KB, ROWS]) for u in range(2)]
            ke = [sb(f"ke{u}", [P, T, D]) for u in range(2)]
            kk = [sb(f"kk{u}", [P, T, D]) for u in range(2)]
            gsb = sb("gsb", [P, KB, D + 1])
            gT = sb("gT", [P, KB, D])
            kvT = sb("kvT", [P, KB, P])
            pT = ph.enter_context(nc.psum_tensor("p1T", [P, KB, ROWS], F32))
            pK = ph.enter_context(nc.psum_tensor("p1K", [P, T, D], F32))
            pGm = [ph.enter_context(nc.psum_tensor(f"p1G{m}", [P, 512], F32)) for m in range(KB)]
            x_in = [sem(f"x_loaded{u}") for u in range(2)]
            stat = sem("x_stats")
            aggr = sem("x_aggregated")
            vs = sem("x_scale_var")
            s_rdy = sem("x_scale_ready")
            v_e = sem("x_var_eps")
            r_rdy = sem("x_rstd_ready")
            iv = sem("x_root_ready")
            bk = sem("x_back_ready")
            s_copy = sem("x_stats_kept")
            one_col = sem("one_column_ready")
            scaled_x = sem("xs_ready")
            turned = sem("xs_turned")
            copied = sem("xT_copied")
            k_rdy = sem("k_ready")
            k_exp = sem("k_exp_ready")
            k_min = sem("k_min_ready")
            k_elu = sem("k_elu_ready")
            k_mask = sem("k_seen_rows_cleared")
            gram = sem("gram_added")
            g_copy = sem("gram_copied")
            g_turn = sem("gram_turned")
            gT_rdy = sem("gramT_copied")
            kv_rdy = sem("kvT_ready")
            kv_m = sem("kvT_masked")
            m_rdy = sem("mix_ready")
            m_copy = sem("mix_copied")
            HALF = T // 2
            with nc.Block() as block:
                @block.sync
                def _(sp):
                    def step(g):
                        if not (isinstance(g.n, int) and g.n < 2):
                            wait_apart(sp, scaled_x, T * (g.n - 1))
                        sp.dma_start(xin[g.buf][:].rearrange("p j d -> p (j d)"), group_rows(x, g, D))\
                          .then_inc(x_in[g.buf], 16)
                    run_steps(sp, step, 2, NG - 2, NG)

                @block.gpsimd
                def _(pool):
                    def step(g):
                        u = g.buf
                        if not (isinstance(g.n, int) and g.n < 2):
                            pool.wait_ge(scaled_x, T * (g.n - 1))
                            pool.wait_ge(s_copy, 3 * (g.n - 1))
                        wait_apart(pool, aggr, T * (g.n + 1))
                        pool.tensor_scalar(sv[u][:], mv[u][:, :, 1], 1.0 + RMS_EPS, LN_EPS * RMS_EPS, ALU.mult, ALU.add)\
                            .then_inc(vs, 1)
                        wait_apart(pool, vs, g.n + 1)
                        pool.tensor_tensor(sc[u][:], sv[u][:], halfneg[:, 0:T], ALU.pow).then_inc(s_rdy, 1)
                        pool.tensor_scalar(rq[u][:], mv[u][:, :, 1], LN_EPS, 1.0, ALU.add, ALU.mult).then_inc(v_e, 1)
                        wait_apart(pool, v_e, g.n + 1)
                        pool.tensor_tensor(rq[u][:], rq[u][:], halfneg[:, 0:T], ALU.pow).then_inc(r_rdy, 1)
                        wait_apart(pool, s_rdy, g.n + 1)
                        pool.tensor_tensor(sv[u][:], sv[u][:], sc[u][:], ALU.mult).then_inc(iv, 1)
                        pool.wait_ge(iv, g.n + 1)
                        wait_apart(pool, r_rdy, g.n + 1)
                        pool.tensor_tensor(rq[u][:], rq[u][:], sv[u][:], ALU.mult).then_inc(bk, 1)
                    run_steps(pool, step, 2, NG - 2, NG)

                @block.vector
                def _(dve):
                    for u in range(2):
                        dve.memset(xs[u][:, :, D:D + 1], 1.0).then_inc(one_col, 1)

                    def stats(g):
                        u = g.buf
                        dve.wait_ge(x_in[u], 16 * (g.turn + 1))
                        if not (isinstance(g.n, int) and g.n < 2):
                            dve.wait_ge(bk, g.n - 1)
                            dve.wait_ge(s_copy, 3 * (g.n - 1))
                        for j in range(T):
                            dve.bn_stats(st[u][:, j, :], xin[u][:, j, :]).then_inc(stat, 1)
                        for j in range(T):
                            wait_apart(dve, stat, T * g.n + j + 1)
                            dve.bn_aggr(mv[u][:, j, :], st[u][:, j, :]).then_inc(aggr, 1)

                    def scale_x(g):
                        u = g.buf
                        dve.wait_ge(s_rdy, g.n + 1)
                        if not (isinstance(g.n, int) and g.n < 2):
                            dve.wait_ge(gram, g.n - 1)
                        for j in range(T):
                            dve.tensor_scalar(xs[u][:, j, 0:D], xin[u][:, j, :], mv[u][:, j, 0:1], sc[u][:, j:j + 1],
                                              ALU.subtract, ALU.mult).then_inc(scaled_x, 1)
                        dve.wait_ge(bk, g.n + 1)
                        for whole_t, part in ((mean_a, mv[u][:, :, 0]), (scale_a, sc[u][:]), (back_a, rq[u][:])):
                            dve.tensor_copy(whole_t[:, bass.ds(g.n * T, T)], part).then_inc(s_copy, 1)

                    def elu_k(g):
                        u = g.buf
                        if not (isinstance(g.n, int) and g.n < 2):
                            dve.wait_ge(gram, g.n - 1)
                        for h in range(2):
                            part = slice(HALF * h, HALF * h + HALF)
                            dve.wait_ge(k_exp, 2 * g.n + h + 1)
                            dve.tensor_scalar(ke[u][:, part, :], ke[u][:, part, :], 1.0, None, ALU.min).then_inc(k_min, 1)
                            dve.wait_ge(k_min, 2 * g.n + h + 1)
                            dve.scalar_tensor_tensor(out=kk[u][:, part, :], in0=pK[:, part, :], scalar=1.0,
                                                     in1=ke[u][:, part, :], op0=ALU.add, op1=ALU.max).then_inc(k_elu, 1)
                        if isinstance(g.n, int) and g.n == NG - 1:
                            dve.wait_ge(k_elu, 2 * NG)
                            dve.memset(kk[u][0:SEEN_P, :, :], 0.0).then_inc(k_mask, 1)

                    stats(At(0, 0, 0))
                    scale_x(At(0, 0, 0))
                    stats(At(1, 1, 0))

                    def step(g):
                        if (g + 1).inside(0, NG):
                            scale_x(g + 1)
                        elu_k(g)
                        if (g + 2).inside(0, NG):
                            stats(g + 2)
                    run_steps(dve, step, 2, NG - 4, NG)

                    for m in range(KB):
                        dve.wait_ge(gram, NG)
                        dve.tensor_copy(gsb[:, m, :], pGm[m][:, 0:D + 1]).then_inc(g_copy, 1)
                    dve.wait_ge(g_turn, 1)
                    dve.tensor_copy(gT[:], pT[:, :, 0:D]).then_inc(gT_rdy, 1)
                    dve.wait_ge(kv_rdy, 1)
                    for m in range(KB):
                        dve.tensor_tensor(kvT[:, m, :], pK[:, m, 0:P], headmask[:], ALU.mult).then_inc(kv_m, 1)
                    dve.wait_ge(g_copy, KB)
                    for m in range(KB):
                        dve.tensor_scalar(ks8[:, m, :], mask8[:, m, :], gsb[:, m, D:D + 1], None, ALU.mult)
                    dve.wait_ge(m_rdy, 1)
                    dve.tensor_copy(mix[:], pT[:, :, 0:D]).then_inc(m_copy, 1)

                @block.scalar
                def _(act):
                    def copy_x(g):
                        act.wait_ge(turned, g.n + 1)
                        if not (isinstance(g.n, int) and g.n < 2):
                            act.wait_ge(k_rdy, 2 * (g.n - 1))
                        act.activation(xT[g.buf][:], pT[:], ACT.Copy).then_inc(copied, 1)

                    def exp_k(g):
                        u = g.buf
                        if not (isinstance(g.n, int) and g.n < 2):
                            act.wait_ge(k_elu, 2 * (g.n - 1))
                        for h in range(2):
                            part = slice(HALF * h, HALF * h + HALF)
                            act.wait_ge(k_rdy, 2 * g.n + h + 1)
                            act.activation(ke[u][:, part, :], pK[:, part, :], ACT.Exp).then_inc(k_exp, 1)
                    copy_x(At(0, 0, 0))

                    def step(g):
                        exp_k(g)
                        if (g + 1).inside(0, NG):
                            copy_x(g + 1)
                    run_steps(act, step, 2, NG - 4, NG)

                @block.tensor
                def _(pe):
                    def turn(g):
                        pe.wait_ge(scaled_x, T * (g.n + 1))
                        if not (isinstance(g.n, int) and g.n == 0):
                            pe.wait_ge(copied, g.n)
                        for j in range(T):
                            for k in range(KB):
                                last = pe.transpose(pT[:, k, j * P:(j + 1) * P], xs[g.buf][:, j, k * P:(k + 1) * P], ident[:])
                        last.then_inc(turned, 1)

                    def project(g):
                        pe.wait_ge(copied, g.n + 1)
                        for h in range(2):
                            if not (isinstance(g.n, int) and g.n == 0):
                                pe.wait_ge(k_elu, 2 * (g.n - 1) + h + 1)
                            for j in range(HALF * h, HALF * h + HALF):
                                for k in range(KB):
                                    last = pe.matmul(pK[:, j, :], xT[g.buf][:, k, j * P:(j + 1) * P],
                                                     wqkv[:, k, D:2 * D], start=(k == 0), stop=(k == KB - 1))
                            last.then_inc(k_rdy, 1)

                    def add_gram(g):
                        first = isinstance(g.n, int) and g.n == 0
                        final = isinstance(g.n, int) and g.n == NG - 1
                        if final:
                            pe.wait_ge(k_mask, 1)
                        for j in range(T):
                            if j % HALF == 0:
                                pe.wait_ge(k_elu, 2 * g.n + j // HALF + 1)
                            for m in range(KB):
                                last = pe.matmul(pGm[m][:, 0:D + 1], kk[g.buf][:, j, m * P:(m + 1) * P], xs[g.buf][:, j, :],
                                                 start=(first and j == 0), stop=(final and j == T - 1),
                                                 skip_group_check=True)
                        last.then_inc(gram, 1)

                    pe.wait_ge(one_col, 2)
                    turn(At(0, 0, 0))

                    def step(g):
                        if (g + -1).inside(0, NG):
                            add_gram(g + -1)
                        if g.inside(0, NG):
                            project(g)
                        if (g + 1).inside(0, NG):
                            turn(g + 1)
                    run_steps(pe, step, 2, NG - 4, NG + 1)

                    pe.wait_ge(g_copy, KB)
                    for m in range(KB):
                        for k in range(KB):
                            last = pe.transpose(pT[:, k, m * P:(m + 1) * P], gsb[:, m, k * P:(k + 1) * P], ident[:])
                    last.then_inc(g_turn, 1)
                    pe.wait_ge(gT_rdy, 1)
                    for m in range(KB):
                        for k in range(KB):
                            last = pe.matmul(pK[:, m, 0:P], wqkv[:, k, 2 * D + m * P:2 * D + (m + 1) * P],
                                             gT[:, k, m * P:(m + 1) * P], start=(k == 0), stop=(k == KB - 1))
                    last.then_inc(kv_rdy, 1)
                    pe.wait_ge(kv_m, KB)
                    for m in range(KB):
                        last = pe.matmul(pT[:, m, 0:D], kvT[:, m, :], wout[:, m, :], start=True, stop=True)
                    last.then_inc(m_rdy, 1)

        with phase() as ph:
            def sb(name, shape, dt=F32):
                return ph.enter_context(nc.sbuf_tensor(name, shape, dt))

            def two(name, shape, dt=F32):
                return [sb(f"{name}{u}", shape, dt) for u in range(2)]
            xin, gin = two("x2in", [P, T, D]), two("g2in", [P, T, D])
            xg, xs, xb = two("xg", [P, T, D]), two("xs2", [P, T, D]), sb("xb", [P, T, D])
            xT = two("xT2", [P, KB, ROWS])
            qe, qq, qz = sb("qe", [P, KB, ROWS]), two("qq", [P, KB, ROWS]), sb("qz", [P, KB, ROWS])
            den, z = sb("den", [P, T * ATTN_HEADS]), two("z", [P, T * ATTN_HEADS])
            zT = sb("zT", [ATTN_HEADS, ROWS])
            hh = two("hh", [P, T, D])
            junk, junk2 = sb("junk2", [P, T, D]), sb("junk3", [P, T, D])
            ssq, r1, r2 = two("ssq", [P, T]), two("r1", [P, T]), two("r2", [P, T])
            t1, x2, base = sb("t1", [P, T, D]), two("x2_", [P, T, D]), two("base", [P, T, D])
            st, mv = sb("st2", [P, T, 6]), two("mv2", [P, T, 2])
            dots = two("dots", [P, T])
            a1, nb = two("a1", [P, T]), two("nb", [P, T])
            fa = two("fa", [P, T])
            aux = two("aux", [P, T, 4])
            wv = two("wv", [P, T])
            pT = ph.enter_context(nc.psum_tensor("p2T", [P, KB, ROWS], F32))
            pQ = ph.enter_context(nc.psum_tensor("p2Q", [P, KB, ROWS], F32))
            pZ = ph.enter_context(nc.psum_tensor("p2Z", [P, KB, ROWS], F32))
            pA = ph.enter_context(nc.psum_tensor("p2A", [P, T, D], F32))
            x_in = [sem(f"x2_loaded{u}") for u in range(2)]
            g_in = [sem(f"gnn_loaded{u}") for u in range(2)]
            xg_s, xs_s, xb_s = sem("x_plus_gnn"), sem("xs2_ready"), sem("xn_bias_ready")
            turned, copied = sem("xs2_turned"), sem("xT2_copied")
            q_rdy, q_exp, q_min, q_elu = sem("q_ready"), sem("q_exp"), sem("q_min"), sem("q_elu")
            den_rdy, den_c, z_rdy = sem("den_ready"), sem("den_copied"), sem("z_ready")
            zt_rdy, zt_c, zb_rdy, qz_s = sem("zT_ready"), sem("zT_copied"), sem("z_spread"), sem("q_normalised")
            at_rdy, h_s, sq_s = sem("attention_ready"), sem("h_ready"), sem("h_squares")
            ms_s, r_s = sem("h_mean_square"), sem("h_rms_ready")
            t1_s, t2_s, x2_s = sem("h_rms_normed"), sem("h_sum"), sem("x2_ready")
            st_s, ag_s, dt_s = sem("x2_stats"), sem("x2_aggregated"), sem("x2_router_dot")
            ve_s, rr_s, a1_s, nb_s = sem("x2_var_eps"), sem("x2_rstd"), sem("x2_plus_one"), sem("x2_shift")
            f_s, w_s, aux_s, wv_s = sem("x2_undo"), sem("router_scaled"), sem("aux_ready"), sem("router_ready")
            base_s = sem("base_ready")
            o_out = [sem(f"base_stored{u}") for u in range(2)]
            a_out = [sem(f"aux_stored{u}") for u in range(2)]
            auxz = sem("aux_blank")

            def fresh(g, k=2):
                return isinstance(g.n, int) and g.n < k

            with nc.Block() as block:
                @block.sync
                def _(sp):
                    def load(g):
                        if not fresh(g):
                            wait_apart(sp, xg_s, g.n - 1)
                            wait_apart(sp, xs_s, T * (g.n - 1))
                        sp.dma_start(xin[g.buf][:].rearrange("p j d -> p (j d)"), group_rows(x, g, D)).then_inc(x_in[g.buf], 16)
                        sp.dma_start(gin[g.buf][:].rearrange("p j d -> p (j d)"), group_rows(gnn_d, g, D)).then_inc(g_in[g.buf], 16)

                    def store(g):
                        wait_apart(sp, base_s, T * (g.n + 1))
                        if isinstance(g.n, int) and g.n == NG - 1:
                            sp.wait_ge(o_out[1 - g.buf], 16 * (NG // 2))
                            sp.wait_ge(a_out[1 - g.buf], 32 * (NG // 2))
                        sp.dma_start(group_rows(out, g, D), base[g.buf][:].rearrange("p j d -> p (j d)")).then_inc(o_out[g.buf], 16)
                        wait_apart(sp, aux_s, g.n + 1)
                        wait_apart(sp, wv_s, g.n + 1)
                        sp.dma_start(group_rows(aux_d, g, 4), aux[g.buf][:].rearrange("p j d -> p (j d)")).then_inc(a_out[g.buf], 16)
                        sp.dma_start(group_rows(wt_d, g, 1), wv[g.buf][:]).then_inc(a_out[g.buf], 16)
                    load(At(0, 0, 0))
                    load(At(1, 1, 0))

                    def step(g):
                        if (g + -3).inside(0, NG):
                            store(g + -3)
                        if (g + 2).inside(0, NG):
                            load(g + 2)
                    run_steps(sp, step, 4, NG - 4, NG + 3)
                    for u in range(2):
                        sp.wait_ge(o_out[u], 16 * (NG // 2))
                        sp.wait_ge(a_out[u], 32 * (NG // 2))

                @block.gpsimd
                def _(pool):
                    for u in range(2):
                        pool.memset(aux[u][:], 0.0).then_inc(auxz, 1)
                    pool.wait_ge(auxz, 2)

                    def add_gnn(g):
                        pool.wait_ge(x_in[g.buf], 16 * (g.turn + 1))
                        wait_apart(pool, g_in[g.buf], 16 * (g.turn + 1))
                        if not fresh(g):
                            wait_apart(pool, x2_s, g.n - 1)
                        pool.tensor_tensor(xg[g.buf][:], xin[g.buf][:], gin[g.buf][:], ALU.add).then_inc(xg_s, 1)

                    def rms(g):
                        u = g.buf
                        wait_apart(pool, sq_s, T * (g.n + 1))
                        if not fresh(g):
                            wait_apart(pool, t1_s, T * (g.n - 1))
                        pool.tensor_scalar(r1[u][:], ssq[u][:], 1.0 / D, RMS_EPS, ALU.mult, ALU.add).then_inc(ms_s, 1)
                        wait_apart(pool, ms_s, g.n + 1)
                        pool.tensor_tensor(r1[u][:], r1[u][:], halfneg[:, 0:T], ALU.pow).then_inc(r_s, 1)

                    def second_norm(g):
                        u = g.buf
                        wait_apart(pool, ag_s, T * (g.n + 1))
                        if not fresh(g):
                            pool.wait_ge(base_s, T * (g.n - 1))
                            pool.wait_ge(f_s, g.n - 1)
                            wait_apart(pool, a_out[u], 32 * g.turn)
                        pool.tensor_scalar(r2[u][:], mv[u][:, :, 1], LN_EPS, 1.0, ALU.add, ALU.mult).then_inc(ve_s, 1)
                        wait_apart(pool, ve_s, g.n + 1)
                        pool.tensor_tensor(r2[u][:], r2[u][:], halfneg[:, 0:T], ALU.pow).then_inc(rr_s, 1)
                        wait_apart(pool, rr_s, g.n + 1)
                        pool.tensor_scalar(a1[u][:], r2[u][:], 1.0, 1.0, ALU.add, ALU.mult).then_inc(a1_s, 1)
                        pool.tensor_tensor(nb[u][:], mv[u][:, :, 0], r2[u][:], ALU.mult).then_inc(nb_s, 1)
                        wait_apart(pool, nb_s, 2 * g.n + 1)
                        pool.tensor_scalar(nb[u][:], nb[u][:], -1.0, 1.0, ALU.mult, ALU.mult).then_inc(nb_s, 1)
                        wait_apart(pool, dt_s, T * (g.n + 1))
                        pool.tensor_tensor(dots[u][:], dots[u][:], r2[u][:], ALU.mult).then_inc(w_s, 1)
                        wait_apart(pool, w_s, g.n + 1)
                        pool.tensor_scalar(wv[u][:], dots[u][:], br_b[:, 0:1], 1.0, ALU.add, ALU.mult).then_inc(wv_s, 1)

                    def step(g):
                        if (g + -1).inside(0, NG):
                            rms(g + -1)
                        if g.inside(0, NG):
                            add_gnn(g)
                        if (g + -2).inside(0, NG):
                            second_norm(g + -2)
                    run_steps(pool, step, 4, NG - 4, NG + 2)

                @block.vector
                def _(dve):
                    def elu_q(g):
                        dve.wait_ge(q_exp, g.n + 1)
                        dve.tensor_scalar(qe[:], qe[:], 1.0, None, ALU.min).then_inc(q_min, 1)
                        dve.wait_ge(q_min, g.n + 1)
                        if not fresh(g):
                            dve.wait_ge(qz_s, g.n - 1)
                        dve.scalar_tensor_tensor(out=qq[g.buf][:], in0=pQ[:], scalar=1.0, in1=qe[:],
                                                 op0=ALU.add, op1=ALU.max).then_inc(q_elu, 1)

                    def norm_q(g):
                        dve.wait_ge(zb_rdy, g.n + 1)
                        if not fresh(g, 1):
                            dve.wait_ge(at_rdy, g.n)
                        dve.tensor_tensor(qz[:], pZ[:], qq[g.buf][:], ALU.mult).then_inc(qz_s, 1)

                    def bias_x(g):
                        if not fresh(g, 1):
                            dve.wait_ge(h_s, g.n)
                        for j in range(T):
                            dve.scalar_tensor_tensor(out=xb[:, j, :], in0=xs[g.buf][:, j, :],
                                                     scalar=back_a[:, bass.ds(T * g.n + j, 1)], in1=bout_b[:],
                                                     op0=ALU.mult, op1=ALU.add).then_inc(xb_s, 1)

                    def scale_x(g):
                        dve.wait_ge(x_in[g.buf], 16 * (g.turn + 1))
                        if not fresh(g):
                            dve.wait_ge(turned, g.n - 1)
                            dve.wait_ge(xb_s, T * (g.n - 1))
                        for j in range(T):
                            dve.tensor_scalar(xs[g.buf][:, j, :], xin[g.buf][:, j, :],
                                              mean_a[:, bass.ds(T * g.n + j, 1)], scale_a[:, bass.ds(T * g.n + j, 1)],
                                              ALU.subtract, ALU.mult).then_inc(xs_s, 1)

                    def residual(g):
                        dve.wait_ge(at_rdy, g.n + 1)
                        dve.wait_ge(xb_s, T * (g.n + 1))
                        if not fresh(g):
                            dve.wait_ge(t2_s, g.n - 1)
                        dve.tensor_tensor(hh[g.buf][:], pA[:], xb[:], ALU.add).then_inc(h_s, 1)

                    def recip_den(g):
                        dve.wait_ge(den_rdy, g.n + 1)
                        dve.tensor_scalar(den[:], pZ[:, 1, 0:T * ATTN_HEADS], ATTN_EPS, None, ALU.add).then_inc(den_c, 1)
                        dve.wait_ge(den_c, g.n + 1)
                        if not fresh(g):
                            dve.wait_ge(zt_rdy, g.n - 1)
                        dve.reciprocal(z[g.buf][:], den[:]).then_inc(z_rdy, 1)

                    def finish_x2(g):
                        u = g.buf
                        dve.wait_ge(r_s, g.n + 1)
                        for j in range(T):
                            dve.scalar_tensor_tensor(out=t1[:, j, :], in0=hh[u][:, j, :], scalar=r1[u][:, j:j + 1],
                                                     in1=wn2_b[:], op0=ALU.mult, op1=ALU.mult).then_inc(t1_s, 1)
                        dve.wait_ge(t1_s, T * (g.n + 1))
                        dve.tensor_tensor(t1[:], t1[:], hh[u][:], ALU.add).then_inc(t2_s, 1)
                        dve.wait_ge(t2_s, g.n + 1)
                        dve.wait_ge(xg_s, g.n + 1)
                        if not fresh(g):
                            dve.wait_ge(base_s, T * (g.n - 1))
                            dve.wait_ge(nb_s, 2 * (g.n - 1))
                        dve.tensor_tensor(x2[u][:], t1[:], xg[u][:], ALU.add).then_inc(x2_s, 1)
                        dve.wait_ge(x2_s, g.n + 1)
                        for j in range(T):
                            dve.bn_stats(st[:, j, :], x2[u][:, j, :]).then_inc(st_s, 1)
                        dve.wait_ge(st_s, T * (g.n + 1))
                        if not fresh(g):
                            wait_apart(dve, aux_s, g.n - 1)
                        for j in range(T):
                            dve.bn_aggr(mv[u][:, j, :], st[:, j, :]).then_inc(ag_s, 1)
                        if not fresh(g):
                            dve.wait_ge(wv_s, g.n - 1)
                        if not fresh(g, 1):
                            dve.wait_ge(dt_s, T * g.n)
                        for j in range(T):
                            dve.tensor_tensor_reduce(junk[:, j, :], x2[u][:, j, :], wr_b[:], 1.0, 0.0, ALU.mult, ALU.add,
                                                     dots[u][:, j:j + 1]).then_inc(dt_s, 1)

                    def make_aux(g):
                        u = g.buf
                        dve.wait_ge(a1_s, g.n + 1)
                        dve.wait_ge(wv_s, g.n + 1)
                        dve.reciprocal(fa[u][:], a1[u][:]).then_inc(f_s, 1)
                        dve.wait_ge(f_s, g.n + 1)
                        if not fresh(g):
                            dve.wait_ge(a_out[u], 32 * g.turn)
                        dve.tensor_copy(aux[u][:, :, 0], mv[u][:, :, 0])
                        dve.tensor_tensor(aux[u][:, :, 1], fa[u][:], r2[u][:], ALU.mult)
                        dve.tensor_copy(aux[u][:, :, 2], wv[u][:]).then_inc(aux_s, 1)

                    dve.wait_ge(auxz, 2)
                    scale_x(At(0, 0, 0))

                    def step(g):
                        if g.inside(0, NG):
                            elu_q(g)
                        if (g + -1).inside(0, NG):
                            norm_q(g + -1)
                            bias_x(g + -1)
                        if (g + 1).inside(0, NG):
                            scale_x(g + 1)
                        if (g + -1).inside(0, NG):
                            residual(g + -1)
                        if g.inside(0, NG):
                            recip_den(g)
                        if (g + -3).inside(0, NG):
                            make_aux(g + -3)
                        if (g + -2).inside(0, NG):
                            finish_x2(g + -2)
                    run_steps(dve, step, 4, NG - 4, NG + 3)

                @block.scalar
                def _(act):
                    def exp_q(g):
                        act.wait_ge(q_rdy, g.n + 1)
                        if not fresh(g, 1):
                            act.wait_ge(q_elu, g.n)
                        act.activation(qe[:], pQ[:], ACT.Exp).then_inc(q_exp, 1)

                    def copy_z(g):
                        act.wait_ge(zt_rdy, g.n + 1)
                        if not fresh(g, 1):
                            act.wait_ge(zb_rdy, g.n)
                        act.activation(zT[:], pZ[0:ATTN_HEADS, 0, :], ACT.Copy).then_inc(zt_c, 1)

                    def make_base(g):
                        u = g.buf
                        act.wait_ge(a1_s, g.n + 1)
                        act.wait_ge(nb_s, 2 * (g.n + 1))
                        act.wait_ge(x2_s, g.n + 1)
                        if not fresh(g):
                            act.wait_ge(o_out[u], 16 * g.turn)
                        for j in range(T):
                            act.activation(base[u][:, j, :], x2[u][:, j, :], ACT.Identity, bias=nb[u][:, j:j + 1],
                                           scale=a1[u][:, j:j + 1]).then_inc(base_s, 1)

                    def copy_x(g):
                        act.wait_ge(turned, g.n + 1)
                        if not fresh(g):
                            act.wait_ge(q_rdy, g.n - 1)
                        act.activation(xT[g.buf][:], pT[:], ACT.Copy).then_inc(copied, 1)

                    def squares(g):
                        act.wait_ge(h_s, g.n + 1)
                        if not fresh(g):
                            act.wait_ge(ms_s, g.n - 1)
                        if not fresh(g, 1):
                            act.wait_ge(sq_s, T * g.n)
                        for j in range(T):
                            act.activation(junk2[:, j, :], hh[g.buf][:, j, :], ACT.Square, accum_out=ssq[g.buf][:, j:j + 1])\
                               .then_inc(sq_s, 1)
                    copy_x(At(0, 0, 0))

                    def step(g):
                        if g.inside(0, NG):
                            exp_q(g)
                        if (g + -1).inside(0, NG):
                            copy_z(g + -1)
                        if (g + -3).inside(0, NG):
                            make_base(g + -3)
                        if (g + 1).inside(0, NG):
                            copy_x(g + 1)
                        if (g + -1).inside(0, NG):
                            squares(g + -1)
                    run_steps(act, step, 4, NG - 4, NG + 3)

                @block.tensor
                def _(pe):
                    def turn(g):
                        pe.wait_ge(xs_s, T * (g.n + 1))
                        if not fresh(g, 1):
                            pe.wait_ge(copied, g.n)
                        for j in range(T):
                            for k in range(KB):
                                last = pe.transpose(pT[:, k, j * P:(j + 1) * P], xs[g.buf][:, j, k * P:(k + 1) * P], ident[:])
                        last.then_inc(turned, 1)

                    def project(g):
                        pe.wait_ge(copied, g.n + 1)
                        if not fresh(g, 1):
                            pe.wait_ge(q_elu, g.n)
                        for m in range(KB):
                            for k in range(KB):
                                last = pe.matmul(pQ[:, m, :], wqkv[:, k, m * P:(m + 1) * P], xT[g.buf][:, k, :],
                                                 start=(k == 0), stop=(k == KB - 1))
                        last.then_inc(q_rdy, 1)

                    def turn_z(g):
                        pe.wait_ge(z_rdy, g.n + 1)
                        for j in range(T):
                            last = pe.transpose(pZ[0:ATTN_HEADS, 0, j * P:(j + 1) * P],
                                                z[g.buf][:, ATTN_HEADS * j:ATTN_HEADS * (j + 1)], ident[:])
                        last.then_inc(zt_rdy, 1)

                    def spread_z(g):
                        pe.wait_ge(zt_c, g.n + 1)
                        for m in range(KB):
                            last = pe.matmul(pZ[:, m, :], spread8[:, m, :], zT[:], start=True, stop=True)
                        last.then_inc(zb_rdy, 1)

                    def attend(g):
                        pe.wait_ge(qz_s, g.n + 1)
                        if not fresh(g, 1):
                            pe.wait_ge(h_s, g.n)
                        for j in range(T):
                            for k in range(KB):
                                last = pe.matmul(pA[:, j, :], qz[:, k, j * P:(j + 1) * P], mix[:, k, :],
                                                 start=(k == 0), stop=(k == KB - 1))
                        last.then_inc(at_rdy, 1)

                    def denominators(g):
                        pe.wait_ge(q_elu, g.n + 1)
                        if not fresh(g, 1):
                            pe.wait_ge(qz_s, g.n)
                        for j in range(T):
                            for k in range(KB):
                                last = pe.matmul(pZ[:, 1, ATTN_HEADS * j:ATTN_HEADS * (j + 1)],
                                                 qq[g.buf][:, k, j * P:(j + 1) * P], ks8[:, k, :],
                                                 start=(k == 0), stop=(k == KB - 1))
                        last.then_inc(den_rdy, 1)

                    turn(At(0, 0, 0))

                    def step(g):
                        if g.inside(0, NG):
                            project(g)
                        if (g + -1).inside(0, NG):
                            turn_z(g + -1)
                            spread_z(g + -1)
                            attend(g + -1)
                        if (g + 1).inside(0, NG):
                            turn(g + 1)
                        if g.inside(0, NG):
                            denominators(g)
                    run_steps(pe, step, 4, NG - 4, NG + 1)

        w1s = keep("w1s", [P, KB, H])
        w2s = keep("w2s", [P, FB, D])
        ctab = keep("ctab", [TP, TC + 3], F16)
        bounds = keep("bounds", [TP, 2])
        with phase() as ph:
            def sb(name, shape, dt=F32):
                return ph.enter_context(nc.sbuf_tensor(name, shape, dt))
            w = sb("w", [TP, TC])
            sgn = sb("sgn", [TP, TC], I32)
            key = sb("key", [TP, TC], I32)
            half_i = sb("half_i", [TP, 2, TC], I32)
            hi = sb("hi", [TP, TC])
            lo = sb("lo", [TP, TC])
            m1 = sb("m1", [TP, TC])
            m2 = sb("m2", [TP, TC])
            m3 = sb("m3", [TP, TC])
            fill1 = sb("fill1", [TP, TC])
            scr = sb("scr", [TP, TC])
            thr = sb("thr", [TP, 2])
            bit = sb("bit", [TP, 2])
            cand = sb("cand", [TP, 1])
            cnt = sb("cntp", [TP, 1])
            hit = sb("hit", [TP, 1])
            tot = sb("totp", [TP, 2])
            need = sb("need", [TP, 1])
            offi = sb("offi", [TP, 3], I32)
            pC = ph.enter_context(nc.psum_tensor("pC", [P, 512], F32))
            pc = sem("selection_loaded")
            c_ = sem("selection_chain")
            total = sem("count_total")
            cnts = sem("count_ready")
            pid = sem("partition_ids")
            with nc.Block() as block:
                @block.sync
                def _(sp):
                    sp.dma_start(w[:], wt_d.rearrange("(p c) o -> p (c o)", c=TC)).then_inc(pc, 16)
                    sp.dma_start(w1s[:], w1.rearrange("(k p) n -> p k n", p=P)).then_inc(pc, 16)
                    sp.dma_start(w2s[:], w2.rearrange("(k p) n -> p k n", p=P)).then_inc(pc, 16)
                    sp.wait_ge(pc, 48)

                @block.gpsimd
                def _(pool):
                    pool.iota(offi[:, 2:3], pattern=[[0, 1]], base=0, channel_multiplier=1).then_inc(pid, 1)

                @block.tensor
                def _(pe):
                    with pe.Fori(0, 32) as i:
                        pe.wait_ge(cnts, i + 1)
                        pe.matmul(pC[0:TP, 0:1], ones[0:TP, 0:TP], cnt[:], start=True, stop=True).then_inc(total, 1)
                    pe.wait_ge(cnts, 33)
                    pe.matmul(pC[0:TP, 0:1], ones[0:TP, 0:TP], cnt[:], start=True, stop=True).then_inc(total, 1)
                    for i in range(2):
                        pe.wait_ge(cnts, 34 + i)
                        pe.matmul(pC[0:TP, 0:1], after[0:TP, 0:TP], tot[:, i:i + 1], start=True, stop=True).then_inc(total, 1)

                @block.vector
                def _(dve):
                    done = [0]

                    def link(ins):
                        done[0] += 1
                        ins.then_inc(c_, 1)
                        dve.wait_ge(c_, done[0])
                    dve.memset(fill1[:], 1.0)
                    dve.memset(thr[:], 0.0)
                    link(dve.memset(bit[:], 32768.0))
                    dve.wait_ge(pc, 48)
                    wi = w[:].bitcast(I32)
                    link(dve.tensor_scalar(sgn[:], wi, 31, None, ALU.arith_shift_right))
                    link(dve.tensor_scalar(sgn[:], sgn[:], -2147483648, None, ALU.bitwise_or))
                    link(dve.tensor_tensor(key[:], sgn[:], wi, ALU.bitwise_xor))
                    link(dve.tensor_scalar(half_i[:, 0, :], key[:], 16, None, ALU.logical_shift_right))
                    link(dve.tensor_scalar(half_i[:, 1, :], key[:], 65535, None, ALU.bitwise_and))
                    link(dve.tensor_copy(hi[:], half_i[:, 0, :]))
                    link(dve.tensor_copy(lo[:], half_i[:, 1, :]))

                    def search(vals, col, base_n):
                        per = 5
                        c0 = done[0]
                        with dve.Fori(0, 16) as i:
                            dve.tensor_tensor(cand[:], thr[:, col:col + 1], bit[:, col:col + 1], ALU.add).then_inc(c_, 1)
                            dve.wait_ge(c_, c0 + per * i + 1)
                            dve.tensor_scalar(scr[:], vals[:], cand[:, 0:1], None, ALU.is_ge, ALU.add,
                                              accum_out=cnt[:]).then_inc(cnts, 1)
                            dve.wait_ge(total, base_n + i + 1)
                            dve.tensor_scalar(hit[:], pC[0:TP, 0:1], float(CAP), None, ALU.is_ge).then_inc(c_, 1)
                            dve.wait_ge(c_, c0 + per * i + 2)
                            dve.tensor_tensor(hit[:], hit[:], bit[:, col:col + 1], ALU.mult).then_inc(c_, 1)
                            dve.wait_ge(c_, c0 + per * i + 3)
                            dve.tensor_tensor(thr[:, col:col + 1], thr[:, col:col + 1], hit[:], ALU.add).then_inc(c_, 1)
                            dve.tensor_scalar(bit[:, col:col + 1], bit[:, col:col + 1], 0.5, None, ALU.mult).then_inc(c_, 1)
                            dve.wait_ge(c_, c0 + per * i + 5)
                        done[0] += per * 16
                    search(hi, 0, 0)
                    link(dve.tensor_scalar(m1[:], hi[:], thr[:, 0:1], 70000.0, ALU.is_gt, ALU.mult))
                    link(dve.tensor_scalar(m2[:], hi[:], thr[:, 0:1], None, ALU.is_equal))
                    link(dve.scalar_tensor_tensor(out=m2[:], in0=lo[:], scalar=1.0, in1=m2[:], op0=ALU.add, op1=ALU.mult))
                    link(dve.scalar_tensor_tensor(out=lo[:], in0=m2[:], scalar=-1.0, in1=m1[:], op0=ALU.add, op1=ALU.add))
                    search(lo, 1, 16)
                    dve.tensor_scalar(m1[:], lo[:], thr[:, 1:2], None, ALU.is_gt, ALU.add, accum_out=cnt[:]).then_inc(cnts, 1)
                    link(dve.tensor_scalar(m2[:], lo[:], thr[:, 1:2], None, ALU.is_equal))
                    dve.wait_ge(total, 33)
                    link(dve.tensor_scalar(need[:], pC[0:TP, 0:1], -1.0, float(CAP), ALU.mult, ALU.add))
                    link(dve.tensor_tensor_scan(m3[:], fill1[:], m2[:], 0.0, ALU.mult, ALU.add))
                    dve.tensor_copy(tot[:, 0:1], m3[:, TC - 1:TC]).then_inc(cnts, 1)
                    dve.wait_ge(total, 34)
                    link(dve.tensor_scalar(m3[:], m3[:], pC[0:TP, 0:1], need[:, 0:1], ALU.add, ALU.is_le))
                    link(dve.tensor_tensor(m2[:], m2[:], m3[:], ALU.mult))
                    link(dve.tensor_tensor(m1[:], m1[:], m2[:], ALU.add))
                    link(dve.tensor_tensor_scan(m3[:], fill1[:], m1[:], 0.0, ALU.mult, ALU.add))
                    dve.tensor_copy(tot[:, 1:2], m3[:, TC - 1:TC]).then_inc(cnts, 1)
                    dve.wait_ge(total, 35)
                    link(dve.tensor_copy(bounds[:, 0:1], pC[0:TP, 0:1]))
                    link(dve.tensor_tensor(bounds[:, 1:2], bounds[:, 0:1], tot[:, 1:2], ALU.add))
                    link(dve.tensor_copy(offi[:, 0:1], bounds[:, 0:1]))
                    link(dve.tensor_scalar(offi[:, 1:2], offi[:, 0:1], 63, None, ALU.bitwise_and))
                    link(dve.tensor_copy(cand[:], offi[:, 1:2]))
                    dve.wait_ge(pid, 1)
                    link(dve.tensor_copy(ctab[:, 0:TC], m3[:]))
                    link(dve.tensor_tensor(ctab[:, TC:TC + 1], bounds[:, 0:1], cand[:], ALU.subtract))
                    link(dve.tensor_copy(ctab[:, TC + 1:TC + 2], cand[:]))
                    link(dve.tensor_copy(ctab[:, TC + 2:TC + 3], offi[:, 2:3]))

        with phase() as ph:
            def sb(name, shape, dt=F32):
                return ph.enter_context(nc.sbuf_tensor(name, shape, dt))

            def two(name, shape, dt=F32):
                return [sb(f"{name}{u}", shape, dt) for u in range(2)]
            rank0 = sb("rank0", [TP, ROWS])
            rank0i = sb("rank0i", [TP, ROWS], I32)
            slot_i = sb("slot_i", [P, T], I32)
            slot = sb("slot", [P, T])
            below = sb("below", [TP, ROWS], F16)
            pick = sb("pick", [TP, ROWS], F16)
            rk = sb("rk", [P, 2 * T])
            cntj = sb("cntj", [P, 3 * T])
            past = sb("past", [P, T])
            scr = sb("scr2", [P, TC])
            tok = two("tok", [P, T], I32)
            brow = two("brow", [P, T, D])
            axr = two("axr", [P, T, 4])
            yn = sb("yn", [P, T, D])
            yT = two("yT", [P, KB, ROWS])
            hT = two("hT", [P, FB, ROWS])
            res = two("res", [P, T, D])
            o1 = sb("o1", [P, T, D])
            pC = [ph.enter_context(nc.psum_tensor(f"pC{u}", [P, 512], F32)) for u in range(2)]
            pT = ph.enter_context(nc.psum_tensor("p3T", [P, KB, ROWS], F32))
            pH = [ph.enter_context(nc.psum_tensor(f"p3H{u}", [P, 512], F32)) for u in range(2)]
            pY = ph.enter_context(nc.psum_tensor("p3Y", [P, T, D], F32))
            ini, ini_f, blank2 = sem("ranks_made"), sem("ranks_float"), sem("row_buffers_blank")
            bl_s, pk_s, bd_s, pa_s, sl_s = sem("below_ready"), sem("pick_ready"), sem("bounds_moved"), sem("past_end"), sem("slots_moved")
            ct_s, rk_s, cj_s = sem("rows_looked_up"), sem("ranks_ready"), sem("tokens_counted")
            tk_s, tf_s = sem("token_parts"), sem("token_ready")
            fetch = [sem(f"rows_fetched{u}") for u in range(2)]
            yn_s, yt_s, yc_s = sem("yn_ready"), sem("yn_turned"), sem("yT_copied")
            h_s, g_s, y_s = sem("hidden_ready"), sem("gelu_ready"), sem("y_ready")
            o_s, r_s = sem("y_biased"), sem("result_ready")
            put = [sem(f"rows_put{u}") for u in range(2)]

            def fresh(g, k=2):
                return isinstance(g.n, int) and g.n < k

            with nc.Block() as block:
                @block.gpsimd
                def _(pool):
                    pool.iota(rank0i[:], pattern=[[1, ROWS]], base=0, channel_multiplier=0).then_inc(ini, 1)
                    pool.iota(slot_i[:], pattern=[[P, T]], base=0, channel_multiplier=1).then_inc(ini, 1)
                    pool.wait_ge(blank2, 4)

                    def fetch_rows(g):
                        wait_apart(pool, tf_s, g.n + 1)
                        if not fresh(g):
                            pool.wait_ge(yn_s, T * (g.n - 1))
                            wait_apart(pool, r_s, T * (g.n - 1))
                        for j in range(T):
                            for t, table in ((brow, out), (axr, aux_d)):
                                pool.indirect_dma_start(
                                    out=t[g.buf][:, j, :], out_offset=None, in_=table,
                                    in_offset=bass.IndirectOffsetOnAxis(ap=tok[g.buf][:, j:j + 1], axis=0),
                                    bounds_check=N - 1, oob_is_err=False).then_inc(fetch[g.buf], 16)

                    def put_rows(g):
                        for j in range(T):
                            wait_apart(pool, r_s, T * g.n + j + 1)
                            pool.indirect_dma_start(
                                out=out, out_offset=bass.IndirectOffsetOnAxis(ap=tok[g.buf][:, j:j + 1], axis=0),
                                in_=res[g.buf][:, j, :], in_offset=None,
                                bounds_check=N - 1, oob_is_err=False).then_inc(put[g.buf], 16)
                    fetch_rows(At(0, 0, 0))

                    def step(g):
                        if (g + -1).inside(0, NF):
                            put_rows(g + -1)
                        if (g + 1).inside(0, NF):
                            fetch_rows(g + 1)
                    run_steps(pool, step, 2, NF - 3, NF + 1)
                    for u in range(2):
                        pool.wait_ge(put[u], 16 * T * ((NF + 1 - u) // 2))

                @block.vector
                def _(dve):
                    for u in range(2):
                        dve.memset(brow[u][:], 0.0).then_inc(blank2, 1)
                        dve.memset(axr[u][:], 0.0).then_inc(blank2, 1)
                    dve.wait_ge(ini, 2)
                    dve.tensor_copy(rank0[:], rank0i[:]).then_inc(ini_f, 1)
                    dve.tensor_copy(slot[:], slot_i[:]).then_inc(ini_f, 1)
                    dve.wait_ge(ini_f, 2)

                    def pick_ranks(g):
                        if not fresh(g, 1):
                            dve.wait_ge(bd_s, g.n)
                            dve.wait_ge(ct_s, T * g.n)
                        dve.tensor_scalar(below[:], rank0[:], bounds[:, 0:1], None, ALU.is_ge).then_inc(bl_s, 1)
                        dve.wait_ge(bl_s, g.n + 1)
                        dve.scalar_tensor_tensor(out=pick[:], in0=rank0[:], scalar=bounds[:, 1:2], in1=below[:],
                                                 op0=ALU.is_lt, op1=ALU.mult).then_inc(pk_s, 1)
                        dve.wait_ge(pk_s, g.n + 1)
                        dve.tensor_scalar(bounds[:], bounds[:], -float(ROWS), None, ALU.add).then_inc(bd_s, 1)

                    def find_tokens(g):
                        u = g.buf
                        if not fresh(g, 1):
                            dve.wait_ge(sl_s, g.n)
                        dve.tensor_scalar(past[:], slot[:], float(CAP), SKIP, ALU.is_ge, ALU.mult).then_inc(pa_s, 1)
                        for j in range(T):
                            c = pC[j % 2]
                            dve.wait_ge(ct_s, T * g.n + j + 1)
                            dve.tensor_tensor(rk[:, j:j + 1], slot[:, j:j + 1], c[:, TC:TC + 1], ALU.subtract).then_inc(rk_s, 1)
                            dve.wait_ge(rk_s, 2 * (T * g.n + j) + 1)
                            dve.tensor_tensor(rk[:, T + j:T + j + 1], rk[:, j:j + 1], c[:, TC + 1:TC + 2], ALU.subtract)\
                               .then_inc(rk_s, 1)
                            dve.wait_ge(rk_s, 2 * (T * g.n + j) + 2)
                            dve.tensor_scalar(cntj[:, T + j:T + j + 1], c[:, TC + 2:TC + 3], float(TC), None, ALU.mult)\
                               .then_inc(tk_s, 1)
                            if not (fresh(g, 1) and j == 0):
                                dve.wait_ge(cj_s, T * g.n + j)
                            dve.tensor_scalar(scr[:], c[:, 0:TC], rk[:, T + j:T + j + 1], None, ALU.is_le, ALU.add,
                                              accum_out=cntj[:, j:j + 1]).then_inc(cj_s, 1)
                        dve.wait_ge(cj_s, T * (g.n + 1))
                        dve.wait_ge(tk_s, T * (g.n + 1) + g.n)
                        dve.wait_ge(pa_s, g.n + 1)
                        dve.tensor_tensor(cntj[:, 2 * T:3 * T], cntj[:, 0:T], cntj[:, T:2 * T], ALU.add).then_inc(tk_s, 1)
                        dve.wait_ge(tk_s, (T + 1) * (g.n + 1))
                        if not fresh(g):
                            dve.wait_ge(put[u], 16 * T * g.turn)
                        dve.tensor_tensor(tok[u][:], cntj[:, 2 * T:3 * T], past[:], ALU.add).then_inc(tf_s, 1)
                        dve.tensor_scalar(slot[:], slot[:], float(ROWS), None, ALU.add).then_inc(sl_s, 1)

                    def norm_rows(g):
                        u = g.buf
                        dve.wait_ge(fetch[u], 32 * T * (g.turn + 1))
                        if not fresh(g, 1):
                            dve.wait_ge(yt_s, g.n)
                        for j in range(T):
                            dve.tensor_scalar(yn[:, j, :], brow[u][:, j, :], axr[u][:, j, 0:1], axr[u][:, j, 1:2],
                                              ALU.subtract, ALU.mult).then_inc(yn_s, 1)

                    def finish_rows(g):
                        u = g.buf
                        for h in range(2):
                            dve.wait_ge(y_s, 2 * g.n + h + 1)
                            if not fresh(g, 1) and h == 0:
                                dve.wait_ge(r_s, T * g.n)
                            dve.tensor_tensor(o1[:, 2 * h:2 * h + 2, :], pY[:, 2 * h:2 * h + 2, :],
                                              b2_b[:].unsqueeze(1).to_broadcast([P, 2, D]), ALU.add).then_inc(o_s, 1)
                        if not fresh(g):
                            dve.wait_ge(put[u], 16 * T * g.turn)
                        dve.wait_ge(o_s, 2 * (g.n + 1))
                        for j in range(T):
                            dve.scalar_tensor_tensor(out=res[u][:, j, :], in0=o1[:, j, :], scalar=axr[u][:, j, 2:3],
                                                     in1=brow[u][:, j, :], op0=ALU.mult, op1=ALU.add).then_inc(r_s, 1)
                    pick_ranks(At(0, 0, 0))
                    find_tokens(At(0, 0, 0))
                    norm_rows(At(0, 0, 0))

                    def step(g):
                        if (g + 1).inside(0, NF):
                            pick_ranks(g + 1)
                        if (g + -1).inside(0, NF):
                            finish_rows(g + -1)
                        if (g + 1).inside(0, NF):
                            find_tokens(g + 1)
                            norm_rows(g + 1)
                    run_steps(dve, step, 2, NF - 3, NF + 1)

                @block.scalar
                def _(act):
                    def copy_y(g):
                        act.wait_ge(yt_s, g.n + 1)
                        if not fresh(g):
                            act.wait_ge(h_s, FB * (g.n - 1))
                        act.activation(yT[g.buf][:], pT[:], ACT.Copy).then_inc(yc_s, 1)

                    def gelu(g):
                        if not fresh(g):
                            act.wait_ge(y_s, 2 * (g.n - 1))
                        for f in range(FB):
                            act.wait_ge(h_s, FB * g.n + f + 1)
                            act.activation(hT[g.buf][:, f, :], pH[f % 2][:], ACT.Gelu_apprx_tanh, bias=b1c[:, f:f + 1])\
                               .then_inc(g_s, 1)
                    copy_y(At(0, 0, 0))

                    def step(g):
                        if g.inside(0, NF):
                            gelu(g)
                        if (g + 1).inside(0, NF):
                            copy_y(g + 1)
                    run_steps(act, step, 2, NF - 3, NF)

                @block.tensor
                def _(pe):
                    def look_up(g):
                        pe.wait_ge(pk_s, g.n + 1)
                        for j in range(T):
                            if not (fresh(g, 1) and j < 2):
                                pe.wait_ge(cj_s, T * g.n + j - 1)
                            pe.matmul(pC[j % 2][:, 0:TC + 3], pick[:, j * P:(j + 1) * P], ctab[:], start=True, stop=True)\
                              .then_inc(ct_s, 1)

                    def turn(g):
                        pe.wait_ge(yn_s, T * (g.n + 1))
                        if not fresh(g, 1):
                            pe.wait_ge(yc_s, g.n)
                        for j in range(T):
                            for k in range(KB):
                                last = pe.transpose(pT[:, k, j * P:(j + 1) * P], yn[:, j, k * P:(k + 1) * P], ident[:])
                        last.then_inc(yt_s, 1)

                    def up(g):
                        pe.wait_ge(yc_s, g.n + 1)
                        for f in range(FB):
                            if not (fresh(g, 1) and f < 2):
                                pe.wait_ge(g_s, FB * g.n + f - 1)
                            for k in range(KB):
                                last = pe.matmul(pH[f % 2][:], w1s[:, k, f * P:(f + 1) * P], yT[g.buf][:, k, :],
                                                 start=(k == 0), stop=(k == KB - 1))
                            last.then_inc(h_s, 1)

                    def down(g):
                        pe.wait_ge(g_s, FB * (g.n + 1))
                        for j in range(T):
                            if not fresh(g, 1) and j % 2 == 0:
                                pe.wait_ge(o_s, 2 * (g.n - 1) + j // 2 + 1)
                            for f in range(FB):
                                last = pe.matmul(pY[:, j, :], hT[g.buf][:, f, j * P:(j + 1) * P], w2s[:, f, :],
                                                 start=(f == 0), stop=(f == FB - 1))
                            if j % 2:
                                last.then_inc(y_s, 1)
                    look_up(At(0, 0, 0))
                    turn(At(0, 0, 0))

                    def step(g):
                        if (g + -1).inside(0, NF):
                            down(g + -1)
                        if (g + 1).inside(0, NF):
                            look_up(g + 1)
                        if g.inside(0, NF):
                            up(g)
                        if (g + 1).inside(0, NF):
                            turn(g + 1)
                    run_steps(pe, step, 2, NF - 3, NF + 1)


_INS = ["x", "src", "dst", "L0_gnn_W", "L0_gnn_Wl", "L0_gnn_Wr", "L0_gnn_b", "L0_mix_w_norm1", "L0_mix_w_qkv",
        "L0_mix_w_out", "L0_mix_b_out", "L0_mix_w_norm2", "L0_ffn_wr", "L0_ffn_br", "L0_ffn_w1", "L0_ffn_b1",
        "L0_ffn_w2", "L0_ffn_b2"]


def kernel(**inputs):
    import numpy as np
    import concourse.bacc as bacc
    from concourse.bass_utils import run_bass_kernel_spmd

    nc = bacc.Bacc("TRN2", target_bir_lowering=False, num_devices=1)
    arrays, args = {}, []
    for name in _INS:
        a = np.ascontiguousarray(inputs[name])
        arrays[f"in_{name}"] = a
        args.append(nc.dram_tensor(f"in_{name}", a.shape, mybir.dt.from_np(a.dtype), kind="ExternalInput").ap())
    out = nc.dram_tensor("out_0", inputs["x"].shape, F32, kind="ExternalOutput").ap()
    gps_layer(nc, *args, out)
    r = run_bass_kernel_spmd(nc, [arrays], core_ids=[0])
    return r.results[0]["out_0"]
```

```python
from contextlib import ExitStack, contextmanager

import concourse.bass as bass
from concourse import mybir

ALU = mybir.AluOpType
ACT = mybir.ActivationFunctionType
AX = mybir.AxisListType
F32 = mybir.dt.float32
F16 = mybir.dt.float16
I32 = mybir.dt.int32

P = 128
LN_EPS = 1e-5
RMS_EPS = 1e-6
ATTN_EPS = 1e-6
GNN_EPS = 1e-12
ATTN_HEADS = 8


class At:

    def __init__(self, n, buf, turn):
        self.n, self.buf, self.turn = n, buf, turn

    def __add__(self, k):
        return At(self.n + k, (self.buf + k) % 2, self.turn + (self.buf + k) // 2)

    def inside(self, lo, hi):
        return not isinstance(self.n, int) or lo <= self.n < hi


def run_steps(eng, body, peeled, loop_end, end):
    run_plan(eng, body, ((False, 0, peeled), (True, peeled, loop_end), (False, loop_end, end)))


def run_plan(eng, body, plan):
    for looped, lo, hi in plan:
        if looped:
            with eng.Fori(lo // 2, hi // 2) as i:
                body(At(2 * i, 0, i))
                body(At(2 * i + 1, 1, i))
        else:
            for n in range(lo, hi):
                body(At(n, n % 2, n // 2))


def gps_layer(nc, x, src, dst, gnn_W, gnn_Wl, gnn_Wr, gnn_b, w_norm1, w_qkv, w_out, b_out, w_norm2,
              wr, br, w1, b1, w2, b2, out):
    N, D = x.shape
    E = src.shape[0]
    OD = gnn_W.shape[1]
    GH = gnn_Wl.shape[0]
    H = w1.shape[1]
    KB = D // P
    FB = H // P
    T = 4
    ROWS = T * P
    NG = -(-N // ROWS)
    LAST0 = N - ROWS
    SEEN = (NG - 1) * ROWS - LAST0
    SEEN_P = SEEN // T
    EP, EC = 125, 100
    assert EP * EC == E and SEEN_P * T == SEEN and NG % 2 == 0
    PADN = 400 * P
    MSG = GH * OD + GH
    TP, TC = 125, 400
    assert TP * TC == N
    CAP = N // 2 - 1
    NF = -(-CAP // ROWS)
    SKIP = 100000.0

    xg_v = x[0:(NG - 1) * ROWS, :].rearrange("(g p j) d -> g p (j d)", p=P, j=T)
    x_last = x[LAST0:N, :].rearrange("(p j) d -> p (j d)", j=T)

    def group_rows(table, at, d):
        if isinstance(at.n, int) and at.n == NG - 1:
            return table[LAST0:N, :].rearrange("(p j) d -> p (j d)", j=T)
        return table[0:(NG - 1) * ROWS, :].rearrange("(g p j) d -> g p (j d)", p=P, j=T)[at.n]

    acc_d = nc.dram_tensor("gnn_acc", (PADN, MSG), F32, kind="Internal").ap()
    gnn_d = nc.dram_tensor("gnn_rows", (PADN, D), F32, kind="Internal").ap()
    aux_d = nc.dram_tensor("aux_rows", (N, 4), F32, kind="Internal").ap()
    wt_d = nc.dram_tensor("router_rows", (N, 1), F32, kind="Internal").ap()

    with ExitStack() as whole:
        def keep(name, shape, dt=F32):
            return whole.enter_context(nc.sbuf_tensor(name, shape, dt))

        held = []

        def sem(name):
            held.append(nc.alloc_semaphore(name=name))
            return held[-1]

        def wait_apart(eng, signal, value):
            eng.wait_ge(signal, value)
            if not isinstance(value, int):
                eng.sem_inc(passed[0], 1)

        passed, phases = [], []

        @contextmanager
        def phase():
            phases.append(1)
            passed[:] = [sem(f"waits_passed{len(phases)}")]
            with ExitStack() as stack:
                yield stack
            nc.clear_and_free_semaphores(held)
            held.clear()
            nc.all_engine_barrier()

        ident = keep("ident", [P, P])
        before = keep("before", [P, P])
        after = keep("after", [P, P])
        ones = keep("ones", [P, P])
        headmask = keep("headmask", [P, P])
        mask8 = keep("mask8", [P, KB, ATTN_HEADS])
        spread8 = keep("spread8", [ATTN_HEADS, KB, P])
        wqkv = keep("wqkv", [P, KB, 3 * D])
        wout = keep("wout", [P, KB, D])
        mix = keep("mix", [P, KB, D])
        ks8 = keep("ks8", [P, KB, ATTN_HEADS])
        bout_b = keep("bout_b", [P, D])
        wn2_b = keep("wn2_b", [P, D])
        wr_b = keep("wr_b", [P, D])
        br_b = keep("br_b", [P, 1])
        b2_b = keep("b2_b", [P, D])
        gb_b = keep("gb_b", [P, OD])
        b1c = keep("b1c", [P, FB])
        shift_a = keep("shift_a", [P, NG * T])
        scale_a = keep("scale_a", [P, NG * T])
        back_a = keep("back_a", [P, NG * T])
        rw_a = keep("rw_a", [P, 4])
        wD = keep("wD", [P, KB, OD + GH])
        wS = keep("wS", [P, KB, GH])
        halfneg = keep("halfneg", [P, 8])

        early = whole.enter_context(ExitStack())
        zero = early.enter_context(nc.sbuf_tensor("zero", [P, 8 * MSG], F32))
        ebrow = early.enter_context(nc.sbuf_tensor("ebrow", [P, 8 * GH, OD], F32))

        with phase() as ph:
            def sb(name, shape, dt=F32):
                return ph.enter_context(nc.sbuf_tensor(name, shape, dt))
            gw = sb("gw", [P, KB, OD])
            wlr = sb("wlr", [2 * GH, OD])
            wlrT = sb("wlrT", [OD, 2 * GH])
            gwT = sb("gwT", [OD, KB, P])
            wn1c = sb("wn1c", [P, KB])
            wrsum = sb("wrsum", [P, 1])
            wr_raw = sb("wr_raw", [P, D])
            eb = sb("eb", [P, OD])
            eb1 = sb("eb1", [P, OD])
            pT = ph.enter_context(nc.psum_tensor("pT", [P, 512], F32))
            pW = ph.enter_context(nc.psum_tensor("pW", [P, 512], F32))
            loaded = sem("weights_loaded")
            made = sem("pool_masks_made")
            blank = sem("blank_masks_ready")
            dve_masks = sem("dve_masks_made")
            scaled = sem("weights_scaled")
            wrmean = sem("router_sum_ready")
            eb_exp = sem("bias_exp_ready")
            eb_min = sem("bias_min_ready")
            eb_elu = sem("bias_elu_ready")
            eb_rows = sem("bias_rows_ready")
            zero_ready = sem("zero_ready")
            fold_t = sem("fold_transposed")
            fold_c = sem("fold_copied")
            fold_m = sem("fold_product_ready")
            fold_d = sem("fold_done")
            with nc.Block() as block:
                @block.sync
                def _(sp):
                    loads = 0
                    with nc.allow_non_contiguous_dma(reason="a few small weight columns"):
                        for dst_ap, src_ap in (
                            (gw[:], gnn_W.rearrange("(k p) n -> p k n", p=P)),
                            (wlr[0:GH, :], gnn_Wl), (wlr[GH:2 * GH, :], gnn_Wr),
                            (gb_b[:], gnn_b.partition_broadcast(P)),
                            (wn1c[:], w_norm1.rearrange("(k p) -> p k", p=P)),
                            (wqkv[:], w_qkv.rearrange("(k p) n -> p k n", p=P)),
                            (wout[:], w_out.rearrange("(k p) n -> p k n", p=P)),
                            (bout_b[:], b_out.partition_broadcast(P)),
                            (wn2_b[:], w_norm2.partition_broadcast(P)),
                            (wr_raw[:], wr.rearrange("d o -> (d o)").partition_broadcast(P)),
                            (br_b[:], br.partition_broadcast(P)),
                            (b2_b[:], b2.partition_broadcast(P)),
                            (b1c[:], b1.rearrange("(k p) -> p k", p=P)),
                        ):
                            sp.dma_start(dst_ap, src_ap).then_inc(loaded, 16)
                            loads += 1
                    assert loads == 13
                    sp.wait_ge(eb_rows, 1)

                @block.gpsimd
                def _(pool):
                    pool.wait_ge(blank, 5)
                    pool.affine_select(out=ident[:], in_=ident[:], compare_op=ALU.not_equal, fill=1.0, base=0,
                                       pattern=[[-1, P]], channel_multiplier=1).then_inc(made, 1)
                    pool.affine_select(out=before[:], in_=ones[:], compare_op=ALU.is_gt, fill=0.0, base=0,
                                       pattern=[[-1, P]], channel_multiplier=1).then_inc(made, 1)
                    pool.affine_select(out=after[:], in_=ones[:], compare_op=ALU.is_gt, fill=0.0, base=0,
                                       pattern=[[1, P]], channel_multiplier=-1).then_inc(made, 1)
                    pool.affine_select(out=spread8[:].rearrange("h k (q e) -> h k q e", e=32),
                                       in_=spread8[:].rearrange("h k (q e) -> h k q e", e=32),
                                       compare_op=ALU.not_equal, fill=1.0, base=0,
                                       pattern=[[-4, KB], [-1, 4], [0, 32]], channel_multiplier=1).then_inc(made, 1)

                @block.vector
                def _(dve):
                    dve.memset(ident[:], 0.0).then_inc(blank, 1)
                    dve.memset(ones[:], 1.0).then_inc(blank, 1)
                    dve.memset(spread8[:], 0.0).then_inc(blank, 1)
                    dve.memset(headmask[:], 0.0).then_inc(blank, 1)
                    dve.memset(mask8[:], 0.0).then_inc(blank, 1)
                    dve.memset(halfneg[:], -0.5)
                    dve.memset(zero[:], 0.0).then_inc(zero_ready, 1)
                    dve.wait_ge(blank, 5)
                    for q in range(4):
                        dve.memset(headmask[32 * q:32 * q + 32, 32 * q:32 * q + 32], 1.0)
                        for k in range(KB):
                            last = dve.memset(mask8[32 * q:32 * q + 32, k, 4 * k + q:4 * k + q + 1], 1.0)
                    last.then_inc(dve_masks, 1)
                    dve.wait_ge(loaded, 13 * 16)
                    for k in range(KB):
                        dve.tensor_scalar(wqkv[:, k, :], wqkv[:, k, :], wn1c[:, k:k + 1], None, ALU.mult)\
                           .then_inc(scaled, 1)
                    dve.tensor_reduce(wrsum[:], wr_raw[:], AX.X, ALU.add).then_inc(wrmean, 1)
                    dve.wait_ge(wrmean, 1)
                    dve.tensor_scalar(wrsum[:], wrsum[:], 1.0 / D, None, ALU.mult).then_inc(wrmean, 1)
                    dve.wait_ge(wrmean, 2)
                    dve.tensor_scalar(wr_b[:], wr_raw[:], wrsum[:, 0:1], None, ALU.subtract).then_inc(wrmean, 1)
                    dve.wait_ge(eb_exp, 1)
                    dve.tensor_scalar(eb1[:], eb[:], 1.0, -1.0, ALU.min, ALU.add).then_inc(eb_min, 1)
                    dve.wait_ge(eb_min, 1)
                    dve.tensor_tensor(eb[:], eb1[:], gb_b[:], ALU.max).then_inc(eb_elu, 1)
                    dve.wait_ge(eb_elu, 1)
                    dve.tensor_copy(ebrow[:], eb[:].unsqueeze(1).to_broadcast([P, 8 * GH, OD])).then_inc(eb_rows, 1)
                    dve.wait_ge(fold_t, 1)
                    dve.tensor_copy(gwT[:], pT[0:OD, 0:KB * P].rearrange("p (k n) -> p k n", k=KB)).then_inc(fold_c, 1)
                    dve.tensor_copy(wlrT[:], pT[0:OD, KB * P:KB * P + 2 * GH]).then_inc(fold_c, 1)
                    dve.tensor_copy(wD[:, :, 0:OD], gw[:]).then_inc(fold_d, 1)
                    dve.wait_ge(fold_m, 1)
                    pv = pW[:, 0:KB * 2 * GH].rearrange("p (k n) -> p k n", k=KB)
                    dve.tensor_copy(wS[:], pv[:, :, 0:GH]).then_inc(fold_d, 1)
                    dve.tensor_copy(wD[:, :, OD:OD + GH], pv[:, :, GH:2 * GH]).then_inc(fold_d, 1)

                @block.scalar
                def _(act):
                    act.wait_ge(loaded, 13 * 16)
                    act.activation(eb[:], gb_b[:], ACT.Exp).then_inc(eb_exp, 1)

                @block.tensor
                def _(pe):
                    pe.wait_ge(loaded, 13 * 16)
                    pe.wait_ge(made, 4)
                    for k in range(KB):
                        pe.transpose(pT[0:OD, k * P:(k + 1) * P], gw[:, k, :], ident[:])
                    pe.transpose(pT[0:OD, KB * P:KB * P + 2 * GH], wlr[:], ident[0:2 * GH, 0:2 * GH]).then_inc(fold_t, 1)
                    pe.wait_ge(fold_c, 2)
                    for k in range(KB):
                        last = pe.matmul(pW[:, 2 * GH * k:2 * GH * (k + 1)], gwT[:, k, :], wlrT[:], start=True, stop=True)
                    last.then_inc(fold_m, 1)

        A_STEPS, B_STEPS = (24, 74), (76, 96)
        A_PER, B_PER = 2, 5
        assert (A_STEPS[1] - A_STEPS[0]) * A_PER == EC and (B_STEPS[1] - B_STEPS[0]) * B_PER == EC
        PLAN = ((False, 0, 2), (True, 2, 24), (False, 24, 26), (True, 26, 72), (False, 72, 78), (True, 78, 94),
                (False, 94, NG + 1))

        with phase() as ph:
            def sb(name, shape, dt=F32):
                return ph.enter_context(nc.sbuf_tensor(name, shape, dt))

            def two(name, shape, dt=F32):
                return [sb(f"{name}{u}", shape, dt) for u in range(2)]

            i_dst, i_src, i_own = sb("i_dst", [P, EC], I32), sb("i_src", [P, EC], I32), sb("i_own", [P, EC], I32)
            i_acc, i_dump = sb("i_acc", [P, EC], I32), sb("i_dump", [P, 1], I32)
            pair, goal, put_ix = two("pair", [P, 2], I32), two("goal", [P, 1], I32), two("put_ix", [P, 1], I32)
            dump, own = sb("dump", [P, 1]), sb("own", [P, EC])
            ends = two("ends", [P, 2, D])
            est, emv, ers = two("est", [P, 2, 6]), two("emv", [P, 2, 2]), two("ers", [P, 2])
            norm, normT = two("norm", [P, 2, D]), two("normT", [P, 2 * KB, P])
            ownb, same, junk = two("ownb", [P, P]), two("same", [P, P]), two("junk", [P, P])
            cnt, ev = two("cnt", [P, 4]), two("ev", [P, 2 * GH])
            msg, tot = two("msg", [P, MSG]), two("tot", [P, MSG])
            ag, rr, gv, ge = two("ag", [P, MSG]), two("rr", [P, 2 * GH]), two("gv", [P, D]), two("ge", [P, D])
            xin, xs, xT = two("xin", [P, T, D]), two("xs", [P, T, D + 1]), two("xT", [P, KB, ROWS])
            st, mv = two("pst", [P, T, 6]), two("pmv", [P, T, 2])
            sc, sv, rq, sh = two("psc", [P, T]), two("psv", [P, T]), two("prq", [P, T]), two("psh", [P, T])
            ke, kk = two("ke", [P, T, D]), two("kk", [P, T, D])
            gsb, gT, kvT = sb("gsb", [P, KB, D + 1]), sb("gT", [P, KB, D]), sb("kvT", [P, KB, P])
            pT = ph.enter_context(nc.psum_tensor("p1T", [P, KB, ROWS], F32))
            pK = ph.enter_context(nc.psum_tensor("p1K", [P, T, D], F32))
            pGm = [ph.enter_context(nc.psum_tensor(f"p1G{m}", [P, 512], F32)) for m in range(KB)]
            pE = ph.enter_context(nc.psum_tensor("pE", [P, 2 * KB * P], F32))
            pF = ph.enter_context(nc.psum_tensor("pF", [P, 512], F32))
            pX = pF[:, 0:OD + GH]
            pS = pF[:, OD + GH:OD + GH + P]
            pM = pF[:, OD + GH + P:OD + GH + P + MSG]

            idx_init, idx_load, idx_float = sem("index_blank"), sem("index_loaded"), sem("index_float")
            ix_col, ix_col2, ix_col3 = sem("edge_columns_ready"), sem("sum_columns_ready"), sem("goal_columns_ready")
            got = [sem(f"ends_gathered{u}") for u in range(2)]
            e_stat, e_aggr, e_veps, e_rstd = sem("ends_stats"), sem("ends_aggregated"), sem("ends_var_eps"), sem("ends_rstd")
            normed, e_turned, e_copied = sem("ends_normed"), sem("ends_turned"), sem("ends_copied")
            filled, spread, eq = sem("shared_bank_filled"), sem("own_spread"), sem("same_ready")
            counted, clipped, gap = sem("earlier_counted"), sem("earlier_clipped"), sem("dump_gap")
            target, target_i = sem("target_float"), sem("target_ready")
            sc_copy, sc_lrelu, sc_exp = sem("score_copied"), sem("score_lrelu"), sem("score_exp")
            msgs, tot_ready, added = sem("messages_ready"), sem("sums_copied"), sem("sums_added")
            cleared, prefilled = sem("accumulators_zero"), sem("default_rows_written")
            fetched = [sem(f"sums_fetched{u}") for u in range(2)]
            guard, recip, mean_r, biased = sem("rowsum_guarded"), sem("rowsum_reciprocal"), sem("rows_normalised"), sem("rows_biased")
            expd, mined, elud, placed = sem("rows_exp"), sem("rows_min"), sem("rows_elu"), sem("rows_placed")
            x_in = [sem(f"x_loaded{u}") for u in range(2)]
            stat, aggr, vs, s_rdy = sem("x_stats"), sem("x_aggregated"), sem("x_scale_var"), sem("x_scale_ready")
            v_e, r_rdy, iv, bk = sem("x_var_eps"), sem("x_rstd_ready"), sem("x_root_ready"), sem("x_back_ready")
            mm_s, sh_s, kept = sem("x_mean_scaled"), sem("x_shift_ready"), sem("x_stats_kept")
            one_col, scaled_x = sem("one_column_ready"), sem("xs_ready")
            turned, copied = sem("xs_turned"), sem("xT_copied")
            k_rdy, k_exp, k_min, k_elu, k_mask = sem("k_ready"), sem("k_exp_ready"), sem("k_min_ready"), sem("k_elu_ready"), sem("k_seen_rows_cleared")
            gram, g_copy, g_turn, gT_rdy = sem("gram_added"), sem("gram_copied"), sem("gram_turned"), sem("gramT_copied")
            kv_rdy, kv_m, m_rdy, m_copy = sem("kvT_ready"), sem("kvT_masked"), sem("mix_ready"), sem("mix_copied")
            HALF = T // 2

            def first(c, k=1):
                return isinstance(c.n, int) and c.n < k

            def slots(g, per, lo, hi):
                if isinstance(g.n, int):
                    return [At(c, c % 2, c // 2) for c in range((g.n - lo) * per, (g.n - lo + 1) * per)]
                return [At((g.n - lo) * per + k, (g.buf * per + k) % 2, (g.turn - lo // 2) * per + (g.buf * per + k) // 2)
                        for k in range(per)]

            def a_slots(g, looped):
                if looped not in (None, "A") or (looped is None and not A_STEPS[0] <= g.n <= A_STEPS[1]):
                    return []
                return slots(g, A_PER, *A_STEPS)

            def b_slots(g, looped):
                if looped not in (None, "B") or (looped is None and not B_STEPS[0] <= g.n <= B_STEPS[1]):
                    return []
                return slots(g, B_PER, *B_STEPS)

            def go(eng, body):
                for part, entry in zip((None, "Z", None, "A", None, "B", None), PLAN):
                    run_plan(eng, lambda g: body(g, part), (entry,))

            with nc.Block() as block:
                @block.sync
                def _(sp):
                    wait_apart(sp, idx_init, 3)
                    for t, a in ((i_dst, dst), (i_src, src), (i_own, src)):
                        sp.dma_start(t[0:EP, :], a.rearrange("(p c) -> p c", c=EC)).then_inc(idx_load, 16)
                    za = acc_d.rearrange("r c -> (r c)").rearrange("(g p c) -> g p c", p=P, c=8 * MSG)
                    ga = gnn_d.rearrange("(g p j) d -> g p (j d)", p=P, j=8)

                    def step(g, part):
                        if g.inside(0, NG):
                            if not first(g, 2):
                                wait_apart(sp, scaled_x, T * (g.n - 1))
                            sp.dma_start(xin[g.buf][:].rearrange("p j d -> p (j d)"), group_rows(x, g, D))\
                              .then_inc(x_in[g.buf], 16)
                        if part == "Z" or (part is None and g.n < A_STEPS[0]):
                            if isinstance(g.n, int):
                                blocks = [3 * g.n, 3 * g.n + 1, 3 * g.n + 2]
                            else:
                                blocks = [2 * g.n + 2, 2 * g.n + 3]
                            for b in blocks:
                                sp.dma_start(za[b], zero[:]).then_inc(cleared, 16)
                        elif part == "A" or (part is None and g.n < A_STEPS[1]):
                            sp.dma_start(ga[g.n - A_STEPS[0]], ebrow[:].rearrange("p a b -> p (a b)")).then_inc(prefilled, 16)
                    go(sp, step)

                @block.gpsimd
                def _(pool):
                    pool.iota(i_own[:], pattern=[[0, EC]], base=N, channel_multiplier=1).then_inc(idx_init, 1)
                    pool.iota(i_dst[:], pattern=[[0, EC]], base=0, channel_multiplier=0).then_inc(idx_init, 1)
                    pool.iota(i_src[:], pattern=[[0, EC]], base=0, channel_multiplier=0).then_inc(idx_init, 1)
                    pool.iota(i_dump[:], pattern=[[0, 1]], base=N, channel_multiplier=1).then_inc(idx_init, 1)
                    pool.wait_ge(idx_load, 48)

                    def scales(g):
                        u = g.buf
                        if not first(g, 2):
                            wait_apart(pool, scaled_x, T * (g.n - 1))
                        wait_apart(pool, aggr, T * (g.n + 1))
                        pool.tensor_scalar(sv[u][:], mv[u][:, :, 1], 1.0 + RMS_EPS, LN_EPS * RMS_EPS, ALU.mult, ALU.add)\
                            .then_inc(vs, 1)
                        pool.tensor_scalar(rq[u][:], mv[u][:, :, 1], LN_EPS, 1.0, ALU.add, ALU.mult).then_inc(v_e, 1)
                        pool.tensor_scalar(sh[u][:], mv[u][:, :, 0], -1.0, 1.0, ALU.mult, ALU.mult).then_inc(mm_s, 1)
                        pool.wait_ge(vs, g.n + 1)
                        pool.tensor_tensor(sc[u][:], sv[u][:], halfneg[:, 0:T], ALU.pow).then_inc(s_rdy, 1)
                        pool.wait_ge(v_e, g.n + 1)
                        pool.tensor_tensor(rq[u][:], rq[u][:], halfneg[:, 0:T], ALU.pow).then_inc(r_rdy, 1)
                        pool.wait_ge(s_rdy, g.n + 1)
                        pool.wait_ge(mm_s, g.n + 1)
                        pool.tensor_tensor(sh[u][:], sh[u][:], sc[u][:], ALU.mult).then_inc(sh_s, 1)
                        pool.tensor_tensor(sv[u][:], sv[u][:], sc[u][:], ALU.mult).then_inc(iv, 1)
                        pool.wait_ge(iv, g.n + 1)
                        pool.wait_ge(r_rdy, g.n + 1)
                        pool.tensor_tensor(back_a[:, bass.ds(g.n * T, T)], rq[u][:], sv[u][:], ALU.mult).then_inc(bk, 1)
                        pool.tensor_copy(scale_a[:, bass.ds(g.n * T, T)], sc[u][:]).then_inc(kept, 1)
                        wait_apart(pool, sh_s, g.n + 1)
                        pool.tensor_copy(shift_a[:, bass.ds(g.n * T, T)], sh[u][:]).then_inc(kept, 1)

                    def gather(c):
                        if not first(c, 2):
                            wait_apart(pool, normed, 2 * (c.n - 1))
                        for side, idx in enumerate((i_dst, i_src)):
                            pool.tensor_copy(pair[c.buf][:, side:side + 1], idx[:, bass.ds(c.n, 1)]).then_inc(ix_col, 1)
                        wait_apart(pool, ix_col, 2 * (c.n + 1))
                        for side in range(2):
                            pool.indirect_dma_start(
                                out=ends[c.buf][:, side, :], out_offset=None, in_=x,
                                in_offset=bass.IndirectOffsetOnAxis(ap=pair[c.buf][:, side:side + 1], axis=0)
                            ).then_inc(got[c.buf], 16)

                    def end_scale(c):
                        wait_apart(pool, e_aggr, 2 * (c.n + 1))
                        if not first(c, 2):
                            wait_apart(pool, normed, 2 * (c.n - 1))
                        pool.tensor_scalar(ers[c.buf][:], emv[c.buf][:, :, 1], LN_EPS, 1.0, ALU.add, ALU.mult)\
                            .then_inc(e_veps, 1)
                        pool.wait_ge(e_veps, c.n + 1)
                        pool.tensor_tensor(ers[c.buf][:], ers[c.buf][:], halfneg[:, 0:2], ALU.pow).then_inc(e_rstd, 1)

                    def add_sums(c):
                        pool.wait_ge(tot_ready, c.n + 1)
                        wait_apart(pool, target_i, c.n + 1)
                        if first(c):
                            pool.wait_ge(cleared, 16 * (PADN // (8 * P)))
                        else:
                            wait_apart(pool, added, 16 * c.n)
                        pool.indirect_dma_start(
                            out=acc_d, out_offset=bass.IndirectOffsetOnAxis(ap=goal[c.buf][:], axis=0),
                            in_=tot[c.buf][:], in_offset=None, compute_op=ALU.add).then_inc(added, 16)

                    def fetch_sums(c):
                        if not first(c, 2):
                            wait_apart(pool, mean_r, c.n - 1)
                        if first(c):
                            pool.wait_ge(added, 16 * EC)
                        pool.tensor_copy(goal[c.buf][:], i_acc[:, bass.ds(c.n, 1)]).then_inc(ix_col2, 1)
                        wait_apart(pool, ix_col2, c.n + 1)
                        pool.indirect_dma_start(
                            out=ag[c.buf][:], out_offset=None, in_=acc_d,
                            in_offset=bass.IndirectOffsetOnAxis(ap=goal[c.buf][:], axis=0)).then_inc(fetched[c.buf], 16)

                    def place(c):
                        wait_apart(pool, elud, c.n + 1)
                        if first(c):
                            pool.wait_ge(prefilled, 16 * (PADN // (8 * P)))
                        else:
                            wait_apart(pool, placed, 16 * c.n)
                        pool.tensor_copy(put_ix[c.buf][:], i_acc[:, bass.ds(c.n, 1)]).then_inc(ix_col3, 1)
                        wait_apart(pool, ix_col3, c.n + 1)
                        pool.indirect_dma_start(
                            out=gnn_d, out_offset=bass.IndirectOffsetOnAxis(ap=put_ix[c.buf][:], axis=0),
                            in_=gv[c.buf][:], in_offset=None).then_inc(placed, 16)

                    def node_tile(c):
                        if first(c) and c.n == 0:
                            fetch_sums(At(0, 0, 0))
                            fetch_sums(At(1, 1, 0))
                        if (c + 2).inside(0, EC):
                            fetch_sums(c + 2)
                        if (c + -1).inside(0, EC):
                            place(c + -1)

                    scales(At(0, 0, 0))
                    scales(At(1, 1, 0))

                    def step(g, part):
                        slots_b = b_slots(g, part)
                        for c in a_slots(g, part):
                            if first(c) and c.n == 0:
                                gather(At(0, 0, 0))
                                gather(At(1, 1, 0))
                                end_scale(At(0, 0, 0))
                            if (c + 2).inside(0, EC):
                                gather(c + 2)
                            if (c + 1).inside(0, EC):
                                end_scale(c + 1)
                            if (c + -2).inside(0, EC):
                                add_sums(c + -2)
                        for c in slots_b[0:2]:
                            node_tile(c)
                        if (g + 2).inside(0, NG):
                            scales(g + 2)
                        for c in slots_b[2:]:
                            node_tile(c)
                    go(pool, step)
                    pool.wait_ge(placed, 16 * EC)

                @block.vector
                def _(dve):
                    for u in range(2):
                        dve.memset(xs[u][:, :, D:D + 1], 1.0).then_inc(one_col, 1)
                    dve.wait_ge(idx_init, 4)
                    dve.wait_ge(idx_load, 48)
                    dve.tensor_copy(own[:], i_own[:]).then_inc(idx_float, 1)
                    dve.tensor_copy(dump[:], i_dump[:]).then_inc(idx_float, 1)
                    dve.wait_ge(idx_float, 2)

                    def stats(g):
                        u = g.buf
                        dve.wait_ge(x_in[u], 16 * (g.turn + 1))
                        if not first(g, 2):
                            dve.wait_ge(mm_s, g.n - 1)
                            dve.wait_ge(vs, g.n - 1)
                            dve.wait_ge(v_e, g.n - 1)
                        for j in range(T):
                            dve.bn_stats(st[u][:, j, :], xin[u][:, j, :]).then_inc(stat, 1)
                        for j in range(T):
                            wait_apart(dve, stat, T * g.n + j + 1)
                            dve.bn_aggr(mv[u][:, j, :], st[u][:, j, :]).then_inc(aggr, 1)

                    def elu_k(g):
                        u = g.buf
                        if not first(g, 2):
                            dve.wait_ge(gram, g.n - 1)
                        for h in range(2):
                            part = slice(HALF * h, HALF * h + HALF)
                            dve.wait_ge(k_exp, 2 * g.n + h + 1)
                            dve.tensor_scalar(ke[u][:, part, :], ke[u][:, part, :], 1.0, None, ALU.min).then_inc(k_min, 1)
                            dve.wait_ge(k_min, 2 * g.n + h + 1)
                            dve.scalar_tensor_tensor(out=kk[u][:, part, :], in0=pK[:, part, :], scalar=1.0,
                                                     in1=ke[u][:, part, :], op0=ALU.add, op1=ALU.max).then_inc(k_elu, 1)
                        if isinstance(g.n, int) and g.n == NG - 1:
                            dve.wait_ge(k_elu, 2 * NG)
                            dve.memset(kk[u][0:SEEN_P, :, :], 0.0).then_inc(k_mask, 1)

                    def end_stats(c):
                        u = c.buf
                        dve.wait_ge(got[u], 32 * (c.turn + 1))
                        if not first(c, 2):
                            dve.wait_ge(normed, 2 * (c.n - 1))
                        for s in range(2):
                            dve.bn_stats(est[u][:, s, :], ends[u][:, s, :]).then_inc(e_stat, 1)
                        if not first(c, 2):
                            dve.wait_ge(e_veps, c.n - 1)
                            dve.wait_ge(filled, c.n - 1)
                            dve.wait_ge(target, c.n - 1)
                        dve.tensor_copy(ownb[u][:], own[:, bass.ds(c.n, 1)].to_broadcast([P, P])).then_inc(spread, 1)
                        wait_apart(dve, e_stat, 2 * (c.n + 1))
                        for s in range(2):
                            dve.bn_aggr(emv[u][:, s, :], est[u][:, s, :]).then_inc(e_aggr, 1)

                    def end_norm(c):
                        u = c.buf
                        dve.wait_ge(e_rstd, c.n + 1)
                        if not first(c, 2):
                            dve.wait_ge(e_turned, c.n - 1)
                        for s in range(2):
                            dve.tensor_scalar(norm[u][:, s, :], ends[u][:, s, :], emv[u][:, s, 0:1], ers[u][:, s:s + 1],
                                              ALU.subtract, ALU.mult).then_inc(normed, 1)

                    def scores(c):
                        u = c.buf
                        dve.wait_ge(filled, c.n + 2)
                        dve.tensor_copy(ev[u][:, 0:GH], pX[:, OD:OD + GH]).then_inc(sc_copy, 1)
                        dve.wait_ge(sc_copy, c.n + 1)
                        if not first(c, 2):
                            dve.wait_ge(sc_exp, c.n - 1)
                        dve.scalar_tensor_tensor(out=ev[u][:, GH:2 * GH], in0=pX[:, OD:OD + GH], scalar=0.2,
                                                 in1=ev[u][:, 0:GH], op0=ALU.mult, op1=ALU.max).then_inc(sc_lrelu, 1)

                    def messages(c):
                        u = c.buf
                        dve.wait_ge(sc_exp, c.n + 1)
                        dve.tensor_tensor(msg[u][:, 0:GH * OD].rearrange("p (h d) -> p h d", h=GH),
                                          pX[:, 0:OD].unsqueeze(1).to_broadcast([P, GH, OD]),
                                          msg[u][:, GH * OD:MSG].unsqueeze(2).to_broadcast([P, GH, OD]), ALU.mult)\
                           .then_inc(msgs, 1)

                    def shared_sources(c):
                        u = c.buf
                        dve.wait_ge(filled, c.n + 1)
                        dve.wait_ge(spread, c.n + 1)
                        dve.tensor_scalar(same[u][:], pS, ownb[u][:, 0:1], None, ALU.is_equal).then_inc(eq, 1)
                        dve.tensor_scalar(cnt[u][:, 2:3], dump[:], ownb[u][:, 0:1], None, ALU.subtract).then_inc(gap, 1)
                        dve.wait_ge(eq, c.n + 1)
                        dve.tensor_tensor_reduce(junk[u][:], same[u][:], before[:], 1.0, 0.0, ALU.mult, ALU.add,
                                                 cnt[u][:, 0:1]).then_inc(counted, 1)
                        dve.wait_ge(counted, c.n + 1)
                        dve.tensor_scalar(cnt[u][:, 1:2], cnt[u][:, 0:1], 1.0, None, ALU.min).then_inc(clipped, 1)
                        dve.wait_ge(clipped, c.n + 1)
                        dve.wait_ge(gap, c.n + 1)
                        dve.scalar_tensor_tensor(out=cnt[u][:, 3:4], in0=cnt[u][:, 1:2], scalar=cnt[u][:, 2:3],
                                                 in1=ownb[u][:, 0:1], op0=ALU.mult, op1=ALU.add).then_inc(target, 1)
                        dve.wait_ge(target, c.n + 1)
                        if not first(c, 2):
                            dve.wait_ge(added, 16 * (c.n - 1))
                        dve.tensor_copy(goal[u][:], cnt[u][:, 3:4]).then_inc(target_i, 1)
                        dve.tensor_copy(i_acc[:, bass.ds(c.n, 1)], cnt[u][:, 3:4])

                    def copy_sums(c):
                        u = c.buf
                        dve.wait_ge(filled, c.n + 3)
                        if not first(c, 2):
                            dve.wait_ge(added, 16 * (c.n - 1))
                        dve.tensor_copy(tot[u][:], pM).then_inc(tot_ready, 1)

                    def mean_rows(c):
                        u = c.buf
                        dve.wait_ge(fetched[u], 16 * (c.turn + 1))
                        dve.tensor_scalar(rr[u][:, 0:GH], ag[u][:, GH * OD:MSG], GNN_EPS, None, ALU.max).then_inc(guard, 1)
                        dve.wait_ge(guard, c.n + 1)
                        dve.reciprocal(rr[u][:, GH:2 * GH], rr[u][:, 0:GH]).then_inc(recip, 1)
                        dve.wait_ge(recip, c.n + 1)
                        if not first(c, 2):
                            dve.wait_ge(placed, 16 * (c.n - 1))
                        v3 = gv[u][:].rearrange("p (h d) -> p h d", h=GH)
                        dve.tensor_tensor(v3, ag[u][:, 0:GH * OD].rearrange("p (h d) -> p h d", h=GH),
                                          rr[u][:, GH:2 * GH].unsqueeze(2).to_broadcast([P, GH, OD]), ALU.mult)\
                           .then_inc(mean_r, 1)
                        dve.wait_ge(mean_r, c.n + 1)
                        dve.tensor_tensor(v3, v3, gb_b[:].unsqueeze(1).to_broadcast([P, GH, OD]), ALU.add)\
                           .then_inc(biased, 1)

                    def elu_rows(c):
                        u = c.buf
                        dve.wait_ge(expd, c.n + 1)
                        dve.tensor_scalar(ge[u][:], ge[u][:], 1.0, -1.0, ALU.min, ALU.add).then_inc(mined, 1)
                        dve.wait_ge(mined, c.n + 1)
                        dve.tensor_tensor(gv[u][:], gv[u][:], ge[u][:], ALU.max).then_inc(elud, 1)

                    stats(At(0, 0, 0))
                    stats(At(1, 1, 0))

                    def edge_tile(c):
                        if first(c) and c.n == 0:
                            end_stats(At(0, 0, 0))
                        if c.inside(0, EC):
                            end_norm(c)
                        if (c + -1).inside(0, EC):
                            scores(c + -1)
                        if (c + 1).inside(0, EC):
                            end_stats(c + 1)
                        if (c + -2).inside(0, EC):
                            copy_sums(c + -2)
                        if (c + -1).inside(0, EC):
                            messages(c + -1)
                        if c.inside(0, EC):
                            shared_sources(c)

                    def node_tile(c):
                        if c.inside(0, EC):
                            mean_rows(c)
                        if (c + -1).inside(0, EC):
                            elu_rows(c + -1)

                    def step(g, part):
                        slots_b = b_slots(g, part)
                        slots_a = a_slots(g, part)
                        for c in slots_a[0:1]:
                            edge_tile(c)
                        for c in slots_b[0:2]:
                            node_tile(c)
                        if (g + 2).inside(0, NG):
                            stats(g + 2)
                        for c in slots_a[1:]:
                            edge_tile(c)
                        if g.inside(0, NG):
                            elu_k(g)
                        for c in slots_b[2:]:
                            node_tile(c)
                    go(dve, step)

                    for m in range(KB):
                        dve.wait_ge(gram, NG)
                        dve.tensor_copy(gsb[:, m, :], pGm[m][:, 0:D + 1]).then_inc(g_copy, 1)
                    dve.wait_ge(g_turn, 1)
                    dve.tensor_copy(gT[:], pT[:, :, 0:D]).then_inc(gT_rdy, 1)
                    dve.wait_ge(kv_rdy, 1)
                    for m in range(KB):
                        dve.tensor_tensor(kvT[:, m, :], pK[:, m, 0:P], headmask[:], ALU.mult).then_inc(kv_m, 1)
                    dve.wait_ge(g_copy, KB)
                    for m in range(KB):
                        dve.tensor_scalar(ks8[:, m, :], mask8[:, m, :], gsb[:, m, D:D + 1], None, ALU.mult)
                    dve.wait_ge(m_rdy, 1)
                    dve.tensor_copy(mix[:], pT[:, :, 0:D]).then_inc(m_copy, 1)

                @block.scalar
                def _(act):
                    def scale_x(g):
                        u = g.buf
                        act.wait_ge(x_in[u], 16 * (g.turn + 1))
                        act.wait_ge(s_rdy, g.n + 1)
                        act.wait_ge(sh_s, g.n + 1)
                        if not first(g, 2):
                            act.wait_ge(gram, g.n - 1)
                        for j in range(T):
                            act.activation(xs[u][:, j, 0:D], xin[u][:, j, :], ACT.Identity, bias=sh[u][:, j:j + 1],
                                           scale=sc[u][:, j:j + 1]).then_inc(scaled_x, 1)

                    def copy_x(g):
                        act.wait_ge(turned, g.n + 1)
                        if not first(g, 2):
                            act.wait_ge(k_rdy, 2 * (g.n - 1))
                        act.activation(xT[g.buf][:], pT[:], ACT.Copy).then_inc(copied, 1)

                    def exp_k(g):
                        u = g.buf
                        if not first(g, 2):
                            act.wait_ge(k_elu, 2 * (g.n - 1))
                        for h in range(2):
                            part = slice(HALF * h, HALF * h + HALF)
                            act.wait_ge(k_rdy, 2 * g.n + h + 1)
                            act.activation(ke[u][:, part, :], pK[:, part, :], ACT.Exp).then_inc(k_exp, 1)

                    def copy_ends(c):
                        u = c.buf
                        act.wait_ge(e_turned, c.n + 1)
                        if not first(c, 2):
                            act.wait_ge(filled, c.n)
                        act.activation(normT[u][:].rearrange("p a b -> p (a b)"), pE[:], ACT.Copy).then_inc(e_copied, 1)

                    def exp_scores(c):
                        u = c.buf
                        act.wait_ge(sc_lrelu, c.n + 1)
                        if not first(c, 2):
                            act.wait_ge(filled, c.n + 1)
                        act.activation(msg[u][:, GH * OD:MSG], ev[u][:, GH:2 * GH], ACT.Exp).then_inc(sc_exp, 1)

                    def exp_rows(c):
                        act.wait_ge(biased, c.n + 1)
                        if not first(c, 2):
                            act.wait_ge(elud, c.n - 1)
                        act.activation(ge[c.buf][:], gv[c.buf][:], ACT.Exp).then_inc(expd, 1)

                    scale_x(At(0, 0, 0))
                    copy_x(At(0, 0, 0))

                    def edge_tile(c):
                        if c.inside(0, EC):
                            copy_ends(c)
                        if (c + -1).inside(0, EC):
                            exp_scores(c + -1)

                    def step(g, part):
                        slots_a, slots_b = a_slots(g, part), b_slots(g, part)
                        for c in slots_a[0:1]:
                            edge_tile(c)
                        if (g + 1).inside(0, NG):
                            scale_x(g + 1)
                        for c in slots_b[0:2]:
                            if c.inside(0, EC):
                                exp_rows(c)
                        for c in slots_a[1:]:
                            edge_tile(c)
                        if g.inside(0, NG):
                            exp_k(g)
                        if (g + 1).inside(0, NG):
                            copy_x(g + 1)
                        for c in slots_b[2:]:
                            if c.inside(0, EC):
                                exp_rows(c)
                    go(act, step)

                @block.tensor
                def _(pe):
                    def turn(g):
                        pe.wait_ge(scaled_x, T * (g.n + 1))
                        if not first(g):
                            pe.wait_ge(copied, g.n)
                        for j in range(T):
                            for k in range(KB):
                                last = pe.transpose(pT[:, k, j * P:(j + 1) * P], xs[g.buf][:, j, k * P:(k + 1) * P], ident[:])
                        last.then_inc(turned, 1)

                    def project(g, h):
                        pe.wait_ge(copied, g.n + 1)
                        if not first(g):
                            pe.wait_ge(k_elu, 2 * (g.n - 1) + h + 1)
                        for j in range(HALF * h, HALF * h + HALF):
                            for k in range(KB):
                                last = pe.matmul(pK[:, j, :], xT[g.buf][:, k, j * P:(j + 1) * P],
                                                 wqkv[:, k, D:2 * D], start=(k == 0), stop=(k == KB - 1))
                        last.then_inc(k_rdy, 1)

                    def add_gram(g, h):
                        final = isinstance(g.n, int) and g.n == NG - 1
                        if final:
                            pe.wait_ge(k_mask, 1)
                        pe.wait_ge(k_elu, 2 * g.n + h + 1)
                        for j in range(HALF * h, HALF * h + HALF):
                            for m in range(KB):
                                last = pe.matmul(pGm[m][:, 0:D + 1], kk[g.buf][:, j, m * P:(m + 1) * P], xs[g.buf][:, j, :],
                                                 start=(first(g) and j == 0), stop=(final and j == T - 1),
                                                 skip_group_check=True)
                        if h:
                            last.then_inc(gram, 1)

                    def turn_ends(c):
                        u = c.buf
                        pe.wait_ge(normed, 2 * (c.n + 1))
                        if not first(c):
                            pe.wait_ge(e_copied, c.n)
                        for s in range(2):
                            for k in range(KB):
                                last = pe.transpose(pE[:, (KB * s + k) * P:(KB * s + k + 1) * P],
                                                    norm[u][:, s, k * P:(k + 1) * P], ident[:])
                        last.then_inc(e_turned, 1)

                    def turn_own(c):
                        return pe.transpose(pS, ownb[c.buf][:], ident[:])

                    def fill_shared(c):
                        if not first(c):
                            pe.wait_ge(msgs, c.n)
                        if c.inside(0, EC):
                            pe.wait_ge(eq, c.n + 1)
                        if not first(c, 2):
                            pe.wait_ge(tot_ready, c.n - 1)
                        if not first(c):
                            v = (c + 1).buf
                            last = pe.matmul(pM, same[v][:], msg[v][:], start=True, stop=True, skip_group_check=True)
                        if c.inside(0, EC):
                            u = c.buf
                            pe.wait_ge(e_copied, c.n + 1)
                            for k in range(KB):
                                pe.matmul(pX, normT[u][:, k, :], wD[:, k, :], start=(k == 0), stop=(k == KB - 1),
                                          skip_group_check=True)
                            for k in range(KB):
                                last = pe.matmul(pX[:, OD:OD + GH], normT[u][:, KB + k, :], wS[:, k, :], start=False,
                                                 stop=(k == KB - 1), skip_group_check=True)
                        if (c + 1).inside(0, EC):
                            pe.wait_ge(spread, c.n + 2)
                            last = turn_own(c + 1)
                        last.then_inc(filled, 1)

                    pe.wait_ge(one_col, 2)
                    turn(At(0, 0, 0))

                    def step(g, part):
                        slots_a = a_slots(g, part)
                        halves = [lambda: (g + -1).inside(0, NG) and add_gram(g + -1, 0),
                                  lambda: (g + -1).inside(0, NG) and add_gram(g + -1, 1),
                                  lambda: g.inside(0, NG) and project(g, 0),
                                  lambda: g.inside(0, NG) and project(g, 1)]
                        for k in range(2):
                            c = slots_a[k] if slots_a else None
                            halves[2 * k]()
                            if c is not None and c.inside(0, EC):
                                turn_ends(c)
                            halves[2 * k + 1]()
                            if c is not None and c.inside(0, EC + 1):
                                if first(c):
                                    pe.wait_ge(spread, 1)
                                    turn_own(c).then_inc(filled, 1)
                                fill_shared(c)
                        if (g + 1).inside(0, NG):
                            turn(g + 1)
                    go(pe, step)

                    pe.wait_ge(g_copy, KB)
                    for m in range(KB):
                        for k in range(KB):
                            last = pe.transpose(pT[:, k, m * P:(m + 1) * P], gsb[:, m, k * P:(k + 1) * P], ident[:])
                    last.then_inc(g_turn, 1)
                    pe.wait_ge(gT_rdy, 1)
                    for m in range(KB):
                        for k in range(KB):
                            last = pe.matmul(pK[:, m, 0:P], wqkv[:, k, 2 * D + m * P:2 * D + (m + 1) * P],
                                             gT[:, k, m * P:(m + 1) * P], start=(k == 0), stop=(k == KB - 1))
                    last.then_inc(kv_rdy, 1)
                    pe.wait_ge(kv_m, KB)
                    for m in range(KB):
                        last = pe.matmul(pT[:, m, 0:D], kvT[:, m, :], wout[:, m, :], start=True, stop=True)
                    last.then_inc(m_rdy, 1)
        early.close()

        with phase() as ph:
            def sb(name, shape, dt=F32):
                return ph.enter_context(nc.sbuf_tensor(name, shape, dt))

            def two(name, shape, dt=F32):
                return [sb(f"{name}{u}", shape, dt) for u in range(2)]
            xin, gin = two("x2in", [P, T, D]), two("g2in", [P, T, D])
            xg, xs, xb = two("xg", [P, T, D]), two("xs2", [P, T, D]), sb("xb", [P, T, D])
            xT = two("xT2", [P, KB, ROWS])
            qe, qq, qz = sb("qe", [P, KB, ROWS]), two("qq", [P, KB, ROWS]), sb("qz", [P, KB, ROWS])
            den, z = sb("den", [P, T * ATTN_HEADS]), two("z", [P, T * ATTN_HEADS])
            zT = sb("zT", [ATTN_HEADS, ROWS])
            hh = two("hh", [P, T, D])
            junk, junk2 = sb("junk2", [P, T, D]), sb("junk3", [P, T, D])
            ssq, r1, r2 = two("ssq", [P, T]), two("r1", [P, T]), two("r2", [P, T])
            t1, x2, base = sb("t1", [P, T, D]), two("x2_", [P, T, D]), two("base", [P, T, D])
            st, mv = sb("st2", [P, T, 6]), two("mv2", [P, T, 2])
            dots = two("dots", [P, T])
            a1, nb = two("a1", [P, T]), two("nb", [P, T])
            fa = two("fa", [P, T])
            aux = two("aux", [P, T, 4])
            wv = two("wv", [P, T])
            pT = ph.enter_context(nc.psum_tensor("p2T", [P, KB, ROWS], F32))
            pQ = ph.enter_context(nc.psum_tensor("p2Q", [P, KB, ROWS], F32))
            pZ = ph.enter_context(nc.psum_tensor("p2Z", [P, KB, ROWS], F32))
            pA = ph.enter_context(nc.psum_tensor("p2A", [P, T, D], F32))
            x_in = [sem(f"x2_loaded{u}") for u in range(2)]
            g_in = [sem(f"gnn_loaded{u}") for u in range(2)]
            xg_s, xs_s, xb_s = sem("x_plus_gnn"), sem("xs2_ready"), sem("xn_bias_ready")
            turned, copied = sem("xs2_turned"), sem("xT2_copied")
            q_rdy, q_exp, q_min, q_elu = sem("q_ready"), sem("q_exp"), sem("q_min"), sem("q_elu")
            den_rdy, den_c, z_rdy = sem("den_ready"), sem("den_copied"), sem("z_ready")
            zt_rdy, zt_c, zb_rdy, qz_s = sem("zT_ready"), sem("zT_copied"), sem("z_spread"), sem("q_normalised")
            at_rdy, h_s, sq_s = sem("attention_ready"), sem("h_ready"), sem("h_squares")
            ms_s, r_s = sem("h_mean_square"), sem("h_rms_ready")
            t1_s, t2_s, x2_s = sem("h_rms_normed"), sem("h_sum"), sem("x2_ready")
            st_s, ag_s, dt_s = sem("x2_stats"), sem("x2_aggregated"), sem("x2_router_dot")
            ve_s, rr_s, a1_s, nb_s = sem("x2_var_eps"), sem("x2_rstd"), sem("x2_plus_one"), sem("x2_shift")
            f_s, w_s, aux_s, wv_s = sem("x2_undo"), sem("router_scaled"), sem("aux_ready"), sem("router_ready")
            base_s = sem("base_ready")
            o_out = [sem(f"base_stored{u}") for u in range(2)]
            a_out = [sem(f"aux_stored{u}") for u in range(2)]
            auxz = sem("aux_blank")

            def fresh(g, k=2):
                return isinstance(g.n, int) and g.n < k

            with nc.Block() as block:
                @block.sync
                def _(sp):
                    def load(g):
                        if not fresh(g):
                            wait_apart(sp, xg_s, g.n - 1)
                            wait_apart(sp, xs_s, T * (g.n - 1))
                        sp.dma_start(xin[g.buf][:].rearrange("p j d -> p (j d)"), group_rows(x, g, D)).then_inc(x_in[g.buf], 16)
                        sp.dma_start(gin[g.buf][:].rearrange("p j d -> p (j d)"), group_rows(gnn_d, g, D)).then_inc(g_in[g.buf], 16)

                    def store(g):
                        wait_apart(sp, base_s, T * (g.n + 1))
                        if isinstance(g.n, int) and g.n == NG - 1:
                            sp.wait_ge(o_out[1 - g.buf], 16 * (NG // 2))
                            sp.wait_ge(a_out[1 - g.buf], 32 * (NG // 2))
                        sp.dma_start(group_rows(out, g, D), base[g.buf][:].rearrange("p j d -> p (j d)")).then_inc(o_out[g.buf], 16)
                        wait_apart(sp, aux_s, g.n + 1)
                        wait_apart(sp, wv_s, g.n + 1)
                        sp.dma_start(group_rows(aux_d, g, 4), aux[g.buf][:].rearrange("p j d -> p (j d)")).then_inc(a_out[g.buf], 16)
                        sp.dma_start(group_rows(wt_d, g, 1), wv[g.buf][:]).then_inc(a_out[g.buf], 16)
                    load(At(0, 0, 0))
                    load(At(1, 1, 0))

                    def step(g):
                        if (g + -3).inside(0, NG):
                            store(g + -3)
                        if (g + 2).inside(0, NG):
                            load(g + 2)
                    run_steps(sp, step, 4, NG - 4, NG + 3)
                    for u in range(2):
                        sp.wait_ge(o_out[u], 16 * (NG // 2))
                        sp.wait_ge(a_out[u], 32 * (NG // 2))

                @block.gpsimd
                def _(pool):
                    for u in range(2):
                        pool.memset(aux[u][:], 0.0).then_inc(auxz, 1)
                    pool.wait_ge(auxz, 2)

                    def add_gnn(g):
                        pool.wait_ge(x_in[g.buf], 16 * (g.turn + 1))
                        wait_apart(pool, g_in[g.buf], 16 * (g.turn + 1))
                        if not fresh(g):
                            wait_apart(pool, x2_s, g.n - 1)
                        pool.tensor_tensor(xg[g.buf][:], xin[g.buf][:], gin[g.buf][:], ALU.add).then_inc(xg_s, 1)

                    def rms(g):
                        u = g.buf
                        wait_apart(pool, sq_s, T * (g.n + 1))
                        if not fresh(g):
                            wait_apart(pool, t1_s, T * (g.n - 1))
                        pool.tensor_scalar(r1[u][:], ssq[u][:], 1.0 / D, RMS_EPS, ALU.mult, ALU.add).then_inc(ms_s, 1)
                        wait_apart(pool, ms_s, g.n + 1)
                        pool.tensor_tensor(r1[u][:], r1[u][:], halfneg[:, 0:T], ALU.pow).then_inc(r_s, 1)

                    def second_norm(g):
                        u = g.buf
                        wait_apart(pool, ag_s, T * (g.n + 1))
                        if not fresh(g):
                            pool.wait_ge(base_s, T * (g.n - 1))
                            pool.wait_ge(f_s, g.n - 1)
                            wait_apart(pool, a_out[u], 32 * g.turn)
                        pool.tensor_scalar(r2[u][:], mv[u][:, :, 1], LN_EPS, 1.0, ALU.add, ALU.mult).then_inc(ve_s, 1)
                        wait_apart(pool, ve_s, g.n + 1)
                        pool.tensor_tensor(r2[u][:], r2[u][:], halfneg[:, 0:T], ALU.pow).then_inc(rr_s, 1)
                        wait_apart(pool, rr_s, g.n + 1)
                        pool.tensor_scalar(a1[u][:], r2[u][:], 1.0, 1.0, ALU.add, ALU.mult).then_inc(a1_s, 1)
                        pool.tensor_tensor(nb[u][:], mv[u][:, :, 0], r2[u][:], ALU.mult).then_inc(nb_s, 1)
                        wait_apart(pool, nb_s, 2 * g.n + 1)
                        pool.tensor_scalar(nb[u][:], nb[u][:], -1.0, 1.0, ALU.mult, ALU.mult).then_inc(nb_s, 1)
                        wait_apart(pool, dt_s, T * (g.n + 1))
                        pool.tensor_tensor(dots[u][:], dots[u][:], r2[u][:], ALU.mult).then_inc(w_s, 1)
                        wait_apart(pool, w_s, g.n + 1)
                        pool.tensor_scalar(wv[u][:], dots[u][:], br_b[:, 0:1], 1.0, ALU.add, ALU.mult).then_inc(wv_s, 1)

                    def step(g):
                        if (g + -1).inside(0, NG):
                            rms(g + -1)
                        if g.inside(0, NG):
                            add_gnn(g)
                        if (g + -2).inside(0, NG):
                            second_norm(g + -2)
                    run_steps(pool, step, 4, NG - 4, NG + 2)

                @block.vector
                def _(dve):
                    def elu_q(g):
                        dve.wait_ge(q_exp, g.n + 1)
                        dve.tensor_scalar(qe[:], qe[:], 1.0, None, ALU.min).then_inc(q_min, 1)
                        dve.wait_ge(q_min, g.n + 1)
                        if not fresh(g):
                            dve.wait_ge(qz_s, g.n - 1)
                        dve.scalar_tensor_tensor(out=qq[g.buf][:], in0=pQ[:], scalar=1.0, in1=qe[:],
                                                 op0=ALU.add, op1=ALU.max).then_inc(q_elu, 1)

                    def norm_q(g):
                        dve.wait_ge(zb_rdy, g.n + 1)
                        if not fresh(g, 1):
                            dve.wait_ge(at_rdy, g.n)
                        dve.tensor_tensor(qz[:], pZ[:], qq[g.buf][:], ALU.mult).then_inc(qz_s, 1)

                    def bias_x(g):
                        if not fresh(g, 1):
                            dve.wait_ge(h_s, g.n)
                        for j in range(T):
                            dve.scalar_tensor_tensor(out=xb[:, j, :], in0=xs[g.buf][:, j, :],
                                                     scalar=back_a[:, bass.ds(T * g.n + j, 1)], in1=bout_b[:],
                                                     op0=ALU.mult, op1=ALU.add).then_inc(xb_s, 1)

                    def scale_x(g):
                        dve.wait_ge(x_in[g.buf], 16 * (g.turn + 1))
                        if not fresh(g):
                            dve.wait_ge(turned, g.n - 1)
                            dve.wait_ge(xb_s, T * (g.n - 1))
                        for j in range(T):
                            dve.tensor_scalar(xs[g.buf][:, j, :], xin[g.buf][:, j, :],
                                              scale_a[:, bass.ds(T * g.n + j, 1)], shift_a[:, bass.ds(T * g.n + j, 1)],
                                              ALU.mult, ALU.add).then_inc(xs_s, 1)

                    def residual(g):
                        dve.wait_ge(at_rdy, g.n + 1)
                        dve.wait_ge(xb_s, T * (g.n + 1))
                        if not fresh(g):
                            dve.wait_ge(t2_s, g.n - 1)
                        dve.tensor_tensor(hh[g.buf][:], pA[:], xb[:], ALU.add).then_inc(h_s, 1)

                    def recip_den(g):
                        dve.wait_ge(den_rdy, g.n + 1)
                        dve.tensor_scalar(den[:], pZ[:, 1, 0:T * ATTN_HEADS], ATTN_EPS, None, ALU.add).then_inc(den_c, 1)
                        dve.wait_ge(den_c, g.n + 1)
                        if not fresh(g):
                            dve.wait_ge(zt_rdy, g.n - 1)
                        dve.reciprocal(z[g.buf][:], den[:]).then_inc(z_rdy, 1)

                    def finish_x2(g):
                        u = g.buf
                        dve.wait_ge(r_s, g.n + 1)
                        for j in range(T):
                            dve.scalar_tensor_tensor(out=t1[:, j, :], in0=hh[u][:, j, :], scalar=r1[u][:, j:j + 1],
                                                     in1=wn2_b[:], op0=ALU.mult, op1=ALU.mult).then_inc(t1_s, 1)
                        dve.wait_ge(t1_s, T * (g.n + 1))
                        dve.tensor_tensor(t1[:], t1[:], hh[u][:], ALU.add).then_inc(t2_s, 1)
                        dve.wait_ge(t2_s, g.n + 1)
                        dve.wait_ge(xg_s, g.n + 1)
                        if not fresh(g):
                            dve.wait_ge(base_s, T * (g.n - 1))
                            dve.wait_ge(nb_s, 2 * (g.n - 1))
                        dve.tensor_tensor(x2[u][:], t1[:], xg[u][:], ALU.add).then_inc(x2_s, 1)
                        dve.wait_ge(x2_s, g.n + 1)
                        for j in range(T):
                            dve.bn_stats(st[:, j, :], x2[u][:, j, :]).then_inc(st_s, 1)
                        dve.wait_ge(st_s, T * (g.n + 1))
                        if not fresh(g):
                            wait_apart(dve, aux_s, g.n - 1)
                        for j in range(T):
                            dve.bn_aggr(mv[u][:, j, :], st[:, j, :]).then_inc(ag_s, 1)
                        if not fresh(g):
                            dve.wait_ge(wv_s, g.n - 1)
                        if not fresh(g, 1):
                            dve.wait_ge(dt_s, T * g.n)
                        for j in range(T):
                            dve.tensor_tensor_reduce(junk[:, j, :], x2[u][:, j, :], wr_b[:], 1.0, 0.0, ALU.mult, ALU.add,
                                                     dots[u][:, j:j + 1]).then_inc(dt_s, 1)

                    def make_aux(g):
                        u = g.buf
                        dve.wait_ge(a1_s, g.n + 1)
                        dve.wait_ge(wv_s, g.n + 1)
                        dve.reciprocal(fa[u][:], a1[u][:]).then_inc(f_s, 1)
                        dve.wait_ge(f_s, g.n + 1)
                        if not fresh(g):
                            dve.wait_ge(a_out[u], 32 * g.turn)
                        dve.tensor_copy(aux[u][:, :, 0], mv[u][:, :, 0])
                        dve.tensor_tensor(aux[u][:, :, 1], fa[u][:], r2[u][:], ALU.mult)
                        dve.tensor_copy(aux[u][:, :, 2], wv[u][:]).then_inc(aux_s, 1)

                    dve.wait_ge(auxz, 2)
                    scale_x(At(0, 0, 0))

                    def step(g):
                        if g.inside(0, NG):
                            elu_q(g)
                        if (g + -1).inside(0, NG):
                            norm_q(g + -1)
                            bias_x(g + -1)
                        if (g + 1).inside(0, NG):
                            scale_x(g + 1)
                        if (g + -1).inside(0, NG):
                            residual(g + -1)
                        if g.inside(0, NG):
                            recip_den(g)
                        if (g + -3).inside(0, NG):
                            make_aux(g + -3)
                        if (g + -2).inside(0, NG):
                            finish_x2(g + -2)
                    run_steps(dve, step, 4, NG - 4, NG + 3)

                @block.scalar
                def _(act):
                    def exp_q(g):
                        act.wait_ge(q_rdy, g.n + 1)
                        if not fresh(g, 1):
                            act.wait_ge(q_elu, g.n)
                        act.activation(qe[:], pQ[:], ACT.Exp).then_inc(q_exp, 1)

                    def copy_z(g):
                        act.wait_ge(zt_rdy, g.n + 1)
                        if not fresh(g, 1):
                            act.wait_ge(zb_rdy, g.n)
                        act.activation(zT[:], pZ[0:ATTN_HEADS, 0, :], ACT.Copy).then_inc(zt_c, 1)

                    def make_base(g):
                        u = g.buf
                        act.wait_ge(a1_s, g.n + 1)
                        act.wait_ge(nb_s, 2 * (g.n + 1))
                        act.wait_ge(x2_s, g.n + 1)
                        if not fresh(g):
                            act.wait_ge(o_out[u], 16 * g.turn)
                        for j in range(T):
                            act.activation(base[u][:, j, :], x2[u][:, j, :], ACT.Identity, bias=nb[u][:, j:j + 1],
                                           scale=a1[u][:, j:j + 1]).then_inc(base_s, 1)

                    def copy_x(g):
                        act.wait_ge(turned, g.n + 1)
                        if not fresh(g):
                            act.wait_ge(q_rdy, g.n - 1)
                        act.activation(xT[g.buf][:], pT[:], ACT.Copy).then_inc(copied, 1)

                    def squares(g):
                        act.wait_ge(h_s, g.n + 1)
                        if not fresh(g):
                            act.wait_ge(ms_s, g.n - 1)
                        if not fresh(g, 1):
                            act.wait_ge(sq_s, T * g.n)
                        for j in range(T):
                            act.activation(junk2[:, j, :], hh[g.buf][:, j, :], ACT.Square, accum_out=ssq[g.buf][:, j:j + 1])\
                               .then_inc(sq_s, 1)
                    copy_x(At(0, 0, 0))

                    def step(g):
                        if g.inside(0, NG):
                            exp_q(g)
                        if (g + -1).inside(0, NG):
                            copy_z(g + -1)
                        if (g + -3).inside(0, NG):
                            make_base(g + -3)
                        if (g + 1).inside(0, NG):
                            copy_x(g + 1)
                        if (g + -1).inside(0, NG):
                            squares(g + -1)
                    run_steps(act, step, 4, NG - 4, NG + 3)

                @block.tensor
                def _(pe):
                    def turn(g):
                        pe.wait_ge(xs_s, T * (g.n + 1))
                        if not fresh(g, 1):
                            pe.wait_ge(copied, g.n)
                        for j in range(T):
                            for k in range(KB):
                                last = pe.transpose(pT[:, k, j * P:(j + 1) * P], xs[g.buf][:, j, k * P:(k + 1) * P], ident[:])
                        last.then_inc(turned, 1)

                    def project(g):
                        pe.wait_ge(copied, g.n + 1)
                        if not fresh(g, 1):
                            pe.wait_ge(q_elu, g.n)
                        for m in range(KB):
                            for k in range(KB):
                                last = pe.matmul(pQ[:, m, :], wqkv[:, k, m * P:(m + 1) * P], xT[g.buf][:, k, :],
                                                 start=(k == 0), stop=(k == KB - 1))
                        last.then_inc(q_rdy, 1)

                    def turn_z(g):
                        pe.wait_ge(z_rdy, g.n + 1)
                        for j in range(T):
                            last = pe.transpose(pZ[0:ATTN_HEADS, 0, j * P:(j + 1) * P],
                                                z[g.buf][:, ATTN_HEADS * j:ATTN_HEADS * (j + 1)], ident[:])
                        last.then_inc(zt_rdy, 1)

                    def spread_z(g):
                        pe.wait_ge(zt_c, g.n + 1)
                        for m in range(KB):
                            last = pe.matmul(pZ[:, m, :], spread8[:, m, :], zT[:], start=True, stop=True)
                        last.then_inc(zb_rdy, 1)

                    def attend(g):
                        pe.wait_ge(qz_s, g.n + 1)
                        if not fresh(g, 1):
                            pe.wait_ge(h_s, g.n)
                        for j in range(T):
                            for k in range(KB):
                                last = pe.matmul(pA[:, j, :], qz[:, k, j * P:(j + 1) * P], mix[:, k, :],
                                                 start=(k == 0), stop=(k == KB - 1))
                        last.then_inc(at_rdy, 1)

                    def denominators(g):
                        pe.wait_ge(q_elu, g.n + 1)
                        if not fresh(g, 1):
                            pe.wait_ge(qz_s, g.n)
                        for j in range(T):
                            for k in range(KB):
                                last = pe.matmul(pZ[:, 1, ATTN_HEADS * j:ATTN_HEADS * (j + 1)],
                                                 qq[g.buf][:, k, j * P:(j + 1) * P], ks8[:, k, :],
                                                 start=(k == 0), stop=(k == KB - 1))
                        last.then_inc(den_rdy, 1)

                    turn(At(0, 0, 0))

                    def step(g):
                        if g.inside(0, NG):
                            project(g)
                        if (g + -1).inside(0, NG):
                            turn_z(g + -1)
                            spread_z(g + -1)
                            attend(g + -1)
                        if (g + 1).inside(0, NG):
                            turn(g + 1)
                        if g.inside(0, NG):
                            denominators(g)
                    run_steps(pe, step, 4, NG - 4, NG + 1)

        w1s = keep("w1s", [P, KB, H])
        w2s = keep("w2s", [P, FB, D])
        ctab = keep("ctab", [TP, TC + 3], F16)
        bounds = keep("bounds", [TP, 2])
        with phase() as ph:
            def sb(name, shape, dt=F32):
                return ph.enter_context(nc.sbuf_tensor(name, shape, dt))
            w = sb("w", [TP, TC])
            sgn = sb("sgn", [TP, TC], I32)
            key = sb("key", [TP, TC], I32)
            half_i = sb("half_i", [TP, 2, TC], I32)
            hi = sb("hi", [TP, TC])
            lo = sb("lo", [TP, TC])
            m1 = sb("m1", [TP, TC])
            m2 = sb("m2", [TP, TC])
            m3 = sb("m3", [TP, TC])
            fill1 = sb("fill1", [TP, TC])
            scr = sb("scr", [TP, TC])
            thr = sb("thr", [TP, 2])
            bit = sb("bit", [TP, 2])
            cand = sb("cand", [TP, 1])
            cnt = sb("cntp", [TP, 1])
            hit = sb("hit", [TP, 1])
            tot = sb("totp", [TP, 2])
            need = sb("need", [TP, 1])
            offi = sb("offi", [TP, 3], I32)
            pC = ph.enter_context(nc.psum_tensor("pC", [P, 512], F32))
            pc = sem("selection_loaded")
            c_ = sem("selection_chain")
            total = sem("count_total")
            cnts = sem("count_ready")
            pid = sem("partition_ids")
            with nc.Block() as block:
                @block.sync
                def _(sp):
                    sp.dma_start(w[:], wt_d.rearrange("(p c) o -> p (c o)", c=TC)).then_inc(pc, 16)
                    sp.dma_start(w1s[:], w1.rearrange("(k p) n -> p k n", p=P)).then_inc(pc, 16)
                    sp.dma_start(w2s[:], w2.rearrange("(k p) n -> p k n", p=P)).then_inc(pc, 16)
                    sp.wait_ge(pc, 48)

                @block.gpsimd
                def _(pool):
                    pool.iota(offi[:, 2:3], pattern=[[0, 1]], base=0, channel_multiplier=1).then_inc(pid, 1)

                @block.tensor
                def _(pe):
                    with pe.Fori(0, 32) as i:
                        pe.wait_ge(cnts, i + 1)
                        pe.matmul(pC[0:TP, 0:1], ones[0:TP, 0:TP], cnt[:], start=True, stop=True).then_inc(total, 1)
                    pe.wait_ge(cnts, 33)
                    pe.matmul(pC[0:TP, 0:1], ones[0:TP, 0:TP], cnt[:], start=True, stop=True).then_inc(total, 1)
                    for i in range(2):
                        pe.wait_ge(cnts, 34 + i)
                        pe.matmul(pC[0:TP, 0:1], after[0:TP, 0:TP], tot[:, i:i + 1], start=True, stop=True).then_inc(total, 1)

                @block.vector
                def _(dve):
                    done = [0]

                    def link(ins):
                        done[0] += 1
                        ins.then_inc(c_, 1)
                        dve.wait_ge(c_, done[0])
                    dve.memset(fill1[:], 1.0)
                    dve.memset(thr[:], 0.0)
                    link(dve.memset(bit[:], 32768.0))
                    dve.wait_ge(pc, 48)
                    wi = w[:].bitcast(I32)
                    link(dve.tensor_scalar(sgn[:], wi, 31, None, ALU.arith_shift_right))
                    link(dve.tensor_scalar(sgn[:], sgn[:], -2147483648, None, ALU.bitwise_or))
                    link(dve.tensor_tensor(key[:], sgn[:], wi, ALU.bitwise_xor))
                    link(dve.tensor_scalar(half_i[:, 0, :], key[:], 16, None, ALU.logical_shift_right))
                    link(dve.tensor_scalar(half_i[:, 1, :], key[:], 65535, None, ALU.bitwise_and))
                    link(dve.tensor_copy(hi[:], half_i[:, 0, :]))
                    link(dve.tensor_copy(lo[:], half_i[:, 1, :]))

                    def search(vals, col, base_n):
                        per = 5
                        c0 = done[0]
                        with dve.Fori(0, 16) as i:
                            dve.tensor_tensor(cand[:], thr[:, col:col + 1], bit[:, col:col + 1], ALU.add).then_inc(c_, 1)
                            dve.wait_ge(c_, c0 + per * i + 1)
                            dve.tensor_scalar(scr[:], vals[:], cand[:, 0:1], None, ALU.is_ge, ALU.add,
                                              accum_out=cnt[:]).then_inc(cnts, 1)
                            dve.wait_ge(total, base_n + i + 1)
                            dve.tensor_scalar(hit[:], pC[0:TP, 0:1], float(CAP), None, ALU.is_ge).then_inc(c_, 1)
                            dve.wait_ge(c_, c0 + per * i + 2)
                            dve.tensor_tensor(hit[:], hit[:], bit[:, col:col + 1], ALU.mult).then_inc(c_, 1)
                            dve.wait_ge(c_, c0 + per * i + 3)
                            dve.tensor_tensor(thr[:, col:col + 1], thr[:, col:col + 1], hit[:], ALU.add).then_inc(c_, 1)
                            dve.tensor_scalar(bit[:, col:col + 1], bit[:, col:col + 1], 0.5, None, ALU.mult).then_inc(c_, 1)
                            dve.wait_ge(c_, c0 + per * i + 5)
                        done[0] += per * 16
                    search(hi, 0, 0)
                    link(dve.tensor_scalar(m1[:], hi[:], thr[:, 0:1], 70000.0, ALU.is_gt, ALU.mult))
                    link(dve.tensor_scalar(m2[:], hi[:], thr[:, 0:1], None, ALU.is_equal))
                    link(dve.scalar_tensor_tensor(out=m2[:], in0=lo[:], scalar=1.0, in1=m2[:], op0=ALU.add, op1=ALU.mult))
                    link(dve.scalar_tensor_tensor(out=lo[:], in0=m2[:], scalar=-1.0, in1=m1[:], op0=ALU.add, op1=ALU.add))
                    search(lo, 1, 16)
                    dve.tensor_scalar(m1[:], lo[:], thr[:, 1:2], None, ALU.is_gt, ALU.add, accum_out=cnt[:]).then_inc(cnts, 1)
                    link(dve.tensor_scalar(m2[:], lo[:], thr[:, 1:2], None, ALU.is_equal))
                    dve.wait_ge(total, 33)
                    link(dve.tensor_scalar(need[:], pC[0:TP, 0:1], -1.0, float(CAP), ALU.mult, ALU.add))
                    link(dve.tensor_tensor_scan(m3[:], fill1[:], m2[:], 0.0, ALU.mult, ALU.add))
                    dve.tensor_copy(tot[:, 0:1], m3[:, TC - 1:TC]).then_inc(cnts, 1)
                    dve.wait_ge(total, 34)
                    link(dve.tensor_scalar(m3[:], m3[:], pC[0:TP, 0:1], need[:, 0:1], ALU.add, ALU.is_le))
                    link(dve.tensor_tensor(m2[:], m2[:], m3[:], ALU.mult))
                    link(dve.tensor_tensor(m1[:], m1[:], m2[:], ALU.add))
                    link(dve.tensor_tensor_scan(m3[:], fill1[:], m1[:], 0.0, ALU.mult, ALU.add))
                    dve.tensor_copy(tot[:, 1:2], m3[:, TC - 1:TC]).then_inc(cnts, 1)
                    dve.wait_ge(total, 35)
                    link(dve.tensor_copy(bounds[:, 0:1], pC[0:TP, 0:1]))
                    link(dve.tensor_tensor(bounds[:, 1:2], bounds[:, 0:1], tot[:, 1:2], ALU.add))
                    link(dve.tensor_copy(offi[:, 0:1], bounds[:, 0:1]))
                    link(dve.tensor_scalar(offi[:, 1:2], offi[:, 0:1], 63, None, ALU.bitwise_and))
                    link(dve.tensor_copy(cand[:], offi[:, 1:2]))
                    dve.wait_ge(pid, 1)
                    link(dve.tensor_copy(ctab[:, 0:TC], m3[:]))
                    link(dve.tensor_tensor(ctab[:, TC:TC + 1], bounds[:, 0:1], cand[:], ALU.subtract))
                    link(dve.tensor_copy(ctab[:, TC + 1:TC + 2], cand[:]))
                    link(dve.tensor_copy(ctab[:, TC + 2:TC + 3], offi[:, 2:3]))

        with phase() as ph:
            def sb(name, shape, dt=F32):
                return ph.enter_context(nc.sbuf_tensor(name, shape, dt))

            def two(name, shape, dt=F32):
                return [sb(f"{name}{u}", shape, dt) for u in range(2)]
            rank0 = sb("rank0", [TP, ROWS])
            rank0i = sb("rank0i", [TP, ROWS], I32)
            slot_i = sb("slot_i", [P, T], I32)
            slot = sb("slot", [P, T])
            below = sb("below", [TP, ROWS], F16)
            pick = sb("pick", [TP, ROWS], F16)
            rk = sb("rk", [P, 2 * T])
            cntj = sb("cntj", [P, 3 * T])
            past = sb("past", [P, T])
            scr = sb("scr2", [P, TC])
            tok = two("tok", [P, T], I32)
            brow = two("brow", [P, T, D])
            axr = two("axr", [P, T, 4])
            yn = sb("yn", [P, T, D])
            yT = two("yT", [P, KB, ROWS])
            hT = two("hT", [P, FB, ROWS])
            res = two("res", [P, T, D])
            o1 = sb("o1", [P, T, D])
            pC = [ph.enter_context(nc.psum_tensor(f"pC{u}", [P, 512], F32)) for u in range(2)]
            pT = ph.enter_context(nc.psum_tensor("p3T", [P, KB, ROWS], F32))
            pH = [ph.enter_context(nc.psum_tensor(f"p3H{u}", [P, 512], F32)) for u in range(2)]
            pY = ph.enter_context(nc.psum_tensor("p3Y", [P, T, D], F32))
            ini, ini_f, blank2 = sem("ranks_made"), sem("ranks_float"), sem("row_buffers_blank")
            bl_s, pk_s, bd_s, pa_s, sl_s = sem("below_ready"), sem("pick_ready"), sem("bounds_moved"), sem("past_end"), sem("slots_moved")
            ct_s, rk_s, cj_s = sem("rows_looked_up"), sem("ranks_ready"), sem("tokens_counted")
            tk_s, tf_s = sem("token_parts"), sem("token_ready")
            fetch = [sem(f"rows_fetched{u}") for u in range(2)]
            yn_s, yt_s, yc_s = sem("yn_ready"), sem("yn_turned"), sem("yT_copied")
            h_s, g_s, y_s = sem("hidden_ready"), sem("gelu_ready"), sem("y_ready")
            o_s, r_s = sem("y_biased"), sem("result_ready")
            put = [sem(f"rows_put{u}") for u in range(2)]

            def fresh(g, k=2):
                return isinstance(g.n, int) and g.n < k

            with nc.Block() as block:
                @block.gpsimd
                def _(pool):
                    pool.iota(rank0i[:], pattern=[[1, ROWS]], base=0, channel_multiplier=0).then_inc(ini, 1)
                    pool.iota(slot_i[:], pattern=[[P, T]], base=0, channel_multiplier=1).then_inc(ini, 1)
                    pool.wait_ge(blank2, 4)

                    def fetch_rows(g):
                        wait_apart(pool, tf_s, g.n + 1)
                        if not fresh(g):
                            pool.wait_ge(yn_s, T * (g.n - 1))
                            wait_apart(pool, r_s, T * (g.n - 1))
                        for j in range(T):
                            for t, table in ((brow, out), (axr, aux_d)):
                                pool.indirect_dma_start(
                                    out=t[g.buf][:, j, :], out_offset=None, in_=table,
                                    in_offset=bass.IndirectOffsetOnAxis(ap=tok[g.buf][:, j:j + 1], axis=0),
                                    bounds_check=N - 1, oob_is_err=False).then_inc(fetch[g.buf], 16)

                    def put_rows(g):
                        for j in range(T):
                            wait_apart(pool, r_s, T * g.n + j + 1)
                            pool.indirect_dma_start(
                                out=out, out_offset=bass.IndirectOffsetOnAxis(ap=tok[g.buf][:, j:j + 1], axis=0),
                                in_=res[g.buf][:, j, :], in_offset=None,
                                bounds_check=N - 1, oob_is_err=False).then_inc(put[g.buf], 16)
                    fetch_rows(At(0, 0, 0))

                    def step(g):
                        if (g + -1).inside(0, NF):
                            put_rows(g + -1)
                        if (g + 1).inside(0, NF):
                            fetch_rows(g + 1)
                    run_steps(pool, step, 2, NF - 3, NF + 1)
                    for u in range(2):
                        pool.wait_ge(put[u], 16 * T * ((NF + 1 - u) // 2))

                @block.vector
                def _(dve):
                    for u in range(2):
                        dve.memset(brow[u][:], 0.0).then_inc(blank2, 1)
                        dve.memset(axr[u][:], 0.0).then_inc(blank2, 1)
                    dve.wait_ge(ini, 2)
                    dve.tensor_copy(rank0[:], rank0i[:]).then_inc(ini_f, 1)
                    dve.tensor_copy(slot[:], slot_i[:]).then_inc(ini_f, 1)
                    dve.wait_ge(ini_f, 2)

                    def pick_ranks(g):
                        if not fresh(g, 1):
                            dve.wait_ge(bd_s, g.n)
                            dve.wait_ge(ct_s, T * g.n)
                        dve.tensor_scalar(below[:], rank0[:], bounds[:, 0:1], None, ALU.is_ge).then_inc(bl_s, 1)
                        dve.wait_ge(bl_s, g.n + 1)
                        dve.scalar_tensor_tensor(out=pick[:], in0=rank0[:], scalar=bounds[:, 1:2], in1=below[:],
                                                 op0=ALU.is_lt, op1=ALU.mult).then_inc(pk_s, 1)
                        dve.wait_ge(pk_s, g.n + 1)
                        dve.tensor_scalar(bounds[:], bounds[:], -float(ROWS), None, ALU.add).then_inc(bd_s, 1)

                    def find_tokens(g):
                        u = g.buf
                        if not fresh(g, 1):
                            dve.wait_ge(sl_s, g.n)
                        dve.tensor_scalar(past[:], slot[:], float(CAP), SKIP, ALU.is_ge, ALU.mult).then_inc(pa_s, 1)
                        for j in range(T):
                            c = pC[j % 2]
                            dve.wait_ge(ct_s, T * g.n + j + 1)
                            dve.tensor_tensor(rk[:, j:j + 1], slot[:, j:j + 1], c[:, TC:TC + 1], ALU.subtract).then_inc(rk_s, 1)
                            dve.wait_ge(rk_s, 2 * (T * g.n + j) + 1)
                            dve.tensor_tensor(rk[:, T + j:T + j + 1], rk[:, j:j + 1], c[:, TC + 1:TC + 2], ALU.subtract)\
                               .then_inc(rk_s, 1)
                            dve.wait_ge(rk_s, 2 * (T * g.n + j) + 2)
                            dve.tensor_scalar(cntj[:, T + j:T + j + 1], c[:, TC + 2:TC + 3], float(TC), None, ALU.mult)\
                               .then_inc(tk_s, 1)
                            if not (fresh(g, 1) and j == 0):
                                dve.wait_ge(cj_s, T * g.n + j)
                            dve.tensor_scalar(scr[:], c[:, 0:TC], rk[:, T + j:T + j + 1], None, ALU.is_le, ALU.add,
                                              accum_out=cntj[:, j:j + 1]).then_inc(cj_s, 1)
                        dve.wait_ge(cj_s, T * (g.n + 1))
                        dve.wait_ge(tk_s, T * (g.n + 1) + g.n)
                        dve.wait_ge(pa_s, g.n + 1)
                        dve.tensor_tensor(cntj[:, 2 * T:3 * T], cntj[:, 0:T], cntj[:, T:2 * T], ALU.add).then_inc(tk_s, 1)
                        dve.wait_ge(tk_s, (T + 1) * (g.n + 1))
                        if not fresh(g):
                            dve.wait_ge(put[u], 16 * T * g.turn)
                        dve.tensor_tensor(tok[u][:], cntj[:, 2 * T:3 * T], past[:], ALU.add).then_inc(tf_s, 1)
                        dve.tensor_scalar(slot[:], slot[:], float(ROWS), None, ALU.add).then_inc(sl_s, 1)

                    def norm_rows(g):
                        u = g.buf
                        dve.wait_ge(fetch[u], 32 * T * (g.turn + 1))
                        if not fresh(g, 1):
                            dve.wait_ge(yt_s, g.n)
                        for j in range(T):
                            dve.tensor_scalar(yn[:, j, :], brow[u][:, j, :], axr[u][:, j, 0:1], axr[u][:, j, 1:2],
                                              ALU.subtract, ALU.mult).then_inc(yn_s, 1)

                    def finish_rows(g):
                        u = g.buf
                        for h in range(2):
                            dve.wait_ge(y_s, 2 * g.n + h + 1)
                            if not fresh(g, 1) and h == 0:
                                dve.wait_ge(r_s, T * g.n)
                            dve.tensor_tensor(o1[:, 2 * h:2 * h + 2, :], pY[:, 2 * h:2 * h + 2, :],
                                              b2_b[:].unsqueeze(1).to_broadcast([P, 2, D]), ALU.add).then_inc(o_s, 1)
                        if not fresh(g):
                            dve.wait_ge(put[u], 16 * T * g.turn)
                        dve.wait_ge(o_s, 2 * (g.n + 1))
                        for j in range(T):
                            dve.scalar_tensor_tensor(out=res[u][:, j, :], in0=o1[:, j, :], scalar=axr[u][:, j, 2:3],
                                                     in1=brow[u][:, j, :], op0=ALU.mult, op1=ALU.add).then_inc(r_s, 1)
                    pick_ranks(At(0, 0, 0))
                    find_tokens(At(0, 0, 0))
                    norm_rows(At(0, 0, 0))

                    def step(g):
                        if (g + 1).inside(0, NF):
                            pick_ranks(g + 1)
                        if (g + -1).inside(0, NF):
                            finish_rows(g + -1)
                        if (g + 1).inside(0, NF):
                            find_tokens(g + 1)
                            norm_rows(g + 1)
                    run_steps(dve, step, 2, NF - 3, NF + 1)

                @block.scalar
                def _(act):
                    def copy_y(g):
                        act.wait_ge(yt_s, g.n + 1)
                        if not fresh(g):
                            act.wait_ge(h_s, FB * (g.n - 1))
                        act.activation(yT[g.buf][:], pT[:], ACT.Copy).then_inc(yc_s, 1)

                    def gelu(g):
                        if not fresh(g):
                            act.wait_ge(y_s, 2 * (g.n - 1))
                        for f in range(FB):
                            act.wait_ge(h_s, FB * g.n + f + 1)
                            act.activation(hT[g.buf][:, f, :], pH[f % 2][:], ACT.Gelu_apprx_tanh, bias=b1c[:, f:f + 1])\
                               .then_inc(g_s, 1)
                    copy_y(At(0, 0, 0))

                    def step(g):
                        if g.inside(0, NF):
                            gelu(g)
                        if (g + 1).inside(0, NF):
                            copy_y(g + 1)
                    run_steps(act, step, 2, NF - 3, NF)

                @block.tensor
                def _(pe):
                    def look_up(g):
                        pe.wait_ge(pk_s, g.n + 1)
                        for j in range(T):
                            if not (fresh(g, 1) and j < 2):
                                pe.wait_ge(cj_s, T * g.n + j - 1)
                            pe.matmul(pC[j % 2][:, 0:TC + 3], pick[:, j * P:(j + 1) * P], ctab[:], start=True, stop=True)\
                              .then_inc(ct_s, 1)

                    def turn(g):
                        pe.wait_ge(yn_s, T * (g.n + 1))
                        if not fresh(g, 1):
                            pe.wait_ge(yc_s, g.n)
                        for j in range(T):
                            for k in range(KB):
                                last = pe.transpose(pT[:, k, j * P:(j + 1) * P], yn[:, j, k * P:(k + 1) * P], ident[:])
                        last.then_inc(yt_s, 1)

                    def up(g):
                        pe.wait_ge(yc_s, g.n + 1)
                        for f in range(FB):
                            if not (fresh(g, 1) and f < 2):
                                pe.wait_ge(g_s, FB * g.n + f - 1)
                            for k in range(KB):
                                last = pe.matmul(pH[f % 2][:], w1s[:, k, f * P:(f + 1) * P], yT[g.buf][:, k, :],
                                                 start=(k == 0), stop=(k == KB - 1))
                            last.then_inc(h_s, 1)

                    def down(g):
                        pe.wait_ge(g_s, FB * (g.n + 1))
                        for j in range(T):
                            if not fresh(g, 1) and j % 2 == 0:
                                pe.wait_ge(o_s, 2 * (g.n - 1) + j // 2 + 1)
                            for f in range(FB):
                                last = pe.matmul(pY[:, j, :], hT[g.buf][:, f, j * P:(j + 1) * P], w2s[:, f, :],
                                                 start=(f == 0), stop=(f == FB - 1))
                            if j % 2:
                                last.then_inc(y_s, 1)
                    look_up(At(0, 0, 0))
                    turn(At(0, 0, 0))

                    def step(g):
                        if (g + -1).inside(0, NF):
                            down(g + -1)
                        if (g + 1).inside(0, NF):
                            look_up(g + 1)
                        if g.inside(0, NF):
                            up(g)
                        if (g + 1).inside(0, NF):
                            turn(g + 1)
                    run_steps(pe, step, 2, NF - 3, NF + 1)


_INS = ["x", "src", "dst", "L0_gnn_W", "L0_gnn_Wl", "L0_gnn_Wr", "L0_gnn_b", "L0_mix_w_norm1", "L0_mix_w_qkv",
        "L0_mix_w_out", "L0_mix_b_out", "L0_mix_w_norm2", "L0_ffn_wr", "L0_ffn_br", "L0_ffn_w1", "L0_ffn_b1",
        "L0_ffn_w2", "L0_ffn_b2"]


def kernel(**inputs):
    import numpy as np
    import concourse.bacc as bacc
    from concourse.bass_utils import run_bass_kernel_spmd

    nc = bacc.Bacc("TRN2", target_bir_lowering=False, num_devices=1)
    arrays, args = {}, []
    for name in _INS:
        a = np.ascontiguousarray(inputs[name])
        arrays[f"in_{name}"] = a
        args.append(nc.dram_tensor(f"in_{name}", a.shape, mybir.dt.from_np(a.dtype), kind="ExternalInput").ap())
    out = nc.dram_tensor("out_0", inputs["x"].shape, F32, kind="ExternalOutput").ap()
    gps_layer(nc, *args, out)
    r = run_bass_kernel_spmd(nc, [arrays], core_ids=[0])
    return r.results[0]["out_0"]
```

```python
from contextlib import ExitStack, contextmanager

import concourse.bass as bass
from concourse import mybir

ALU = mybir.AluOpType
ACT = mybir.ActivationFunctionType
AX = mybir.AxisListType
F32 = mybir.dt.float32
F16 = mybir.dt.float16
F32R = mybir.dt.float32r
I32 = mybir.dt.int32

P = 128
LN_EPS = 1e-5
RMS_EPS = 1e-6
ATTN_EPS = 1e-6
GNN_EPS = 1e-12
ATTN_HEADS = 8


class At:

    def __init__(self, n, buf, turn, mod=2):
        self.n, self.buf, self.turn, self.mod = n, buf, turn, mod

    def __add__(self, k):
        return At(self.n + k, (self.buf + k) % self.mod, self.turn + (self.buf + k) // self.mod, self.mod)

    def inside(self, lo, hi):
        return not isinstance(self.n, int) or lo <= self.n < hi

    @property
    def pair(self):
        return At(self.n, self.buf % 2, self.turn * (self.mod // 2) + self.buf // 2)


def at_step(n, mod=2):
    return At(n, n % mod, n // mod, mod)


def run_steps(eng, body, peeled, loop_end, end, mod=2):
    run_plan(eng, body, ((False, 0, peeled), (True, peeled, loop_end), (False, loop_end, end)), mod)


def run_plan(eng, body, plan, mod=2):
    for looped, lo, hi in plan:
        if looped:
            assert lo % mod == 0 and hi % mod == 0
            with eng.Fori(lo // mod, hi // mod) as i:
                for k in range(mod):
                    body(At(mod * i + k if k else mod * i, k, i, mod))
        else:
            for n in range(lo, hi):
                body(at_step(n, mod))


def gps_layer(nc, x, src, dst, gnn_W, gnn_Wl, gnn_Wr, gnn_b, w_norm1, w_qkv, w_out, b_out, w_norm2,
              wr, br, w1, b1, w2, b2, out):
    N, D = x.shape
    E = src.shape[0]
    OD = gnn_W.shape[1]
    GH = gnn_Wl.shape[0]
    H = w1.shape[1]
    KB = D // P
    FB = H // P
    T = 4
    ROWS = T * P
    NG = -(-N // ROWS)
    LAST0 = N - ROWS
    SEEN = (NG - 1) * ROWS - LAST0
    SEEN_P = SEEN // T
    EP, EC = 125, 100
    assert EP * EC == E and SEEN_P * T == SEEN and NG % 2 == 0
    PADN = 400 * P
    MSG = GH * OD + GH
    TP, TC = 125, 400
    assert TP * TC == N
    CAP = N // 2 - 1
    NF = -(-CAP // ROWS)
    SKIP = 100000.0

    xg_v = x[0:(NG - 1) * ROWS, :].rearrange("(g p j) d -> g p (j d)", p=P, j=T)
    x_last = x[LAST0:N, :].rearrange("(p j) d -> p (j d)", j=T)

    def group_rows(table, at, d):
        if isinstance(at.n, int) and at.n == NG - 1:
            return table[LAST0:N, :].rearrange("(p j) d -> p (j d)", j=T)
        return table[0:(NG - 1) * ROWS, :].rearrange("(g p j) d -> g p (j d)", p=P, j=T)[at.n]

    acc_d = nc.dram_tensor("gnn_acc", (PADN, MSG), F32, kind="Internal").ap()
    gnn_d = nc.dram_tensor("gnn_rows", (PADN, D), F32, kind="Internal").ap()
    aux_d = nc.dram_tensor("aux_rows", (N, 4), F32, kind="Internal").ap()
    wt_d = nc.dram_tensor("router_rows", (N, 1), F32, kind="Internal").ap()

    with ExitStack() as whole:
        def keep(name, shape, dt=F32):
            return whole.enter_context(nc.sbuf_tensor(name, shape, dt))

        held = []

        def sem(name):
            held.append(nc.alloc_semaphore(name=name))
            return held[-1]

        def wait_apart(eng, signal, value):
            eng.wait_ge(signal, value)
            if not isinstance(value, int):
                eng.sem_inc(passed[0], 1)

        passed, phases = [], []

        @contextmanager
        def phase():
            phases.append(1)
            passed[:] = [sem(f"waits_passed{len(phases)}")]
            with ExitStack() as stack:
                yield stack
            nc.clear_and_free_semaphores(held)
            held.clear()
            nc.all_engine_barrier()

        ident = keep("ident", [P, P])
        before = keep("before", [P, P])
        after = keep("after", [P, P])
        ones = keep("ones", [P, P])
        headmask = keep("headmask", [P, P])
        mask8 = keep("mask8", [P, KB, ATTN_HEADS])
        spread8 = keep("spread8", [ATTN_HEADS, KB, P])
        wqkv = keep("wqkv", [P, KB, 3 * D])
        wout = keep("wout", [P, KB, D])
        mix = keep("mix", [P, KB, D])
        ks8 = keep("ks8", [P, KB, ATTN_HEADS])
        bout_b = keep("bout_b", [P, D])
        wn2_b = keep("wn2_b", [P, D])
        wr_b = keep("wr_b", [P, D])
        br_b = keep("br_b", [P, 1])
        b2_b = keep("b2_b", [P, D])
        gb_b = keep("gb_b", [P, OD])
        b1c = keep("b1c", [P, FB])
        shift_a = keep("shift_a", [P, NG * T])
        scale_a = keep("scale_a", [P, NG * T])
        back_a = keep("back_a", [P, NG * T])
        rw_a = keep("rw_a", [P, 4])
        wD = keep("wD", [P, KB, OD + GH])
        wS = keep("wS", [P, KB, GH])
        halfneg = keep("halfneg", [P, 8])

        early = whole.enter_context(ExitStack())
        zero = early.enter_context(nc.sbuf_tensor("zero", [P, 8 * MSG], F32))
        ebrow = early.enter_context(nc.sbuf_tensor("ebrow", [P, 8 * GH, OD], F32))

        with phase() as ph:
            def sb(name, shape, dt=F32):
                return ph.enter_context(nc.sbuf_tensor(name, shape, dt))
            gw = sb("gw", [P, KB, OD])
            wlr = sb("wlr", [2 * GH, OD])
            wlrT = sb("wlrT", [OD, 2 * GH])
            gwT = sb("gwT", [OD, KB, P])
            wn1c = sb("wn1c", [P, KB])
            wrsum = sb("wrsum", [P, 1])
            wr_raw = sb("wr_raw", [P, D])
            eb = sb("eb", [P, OD])
            eb1 = sb("eb1", [P, OD])
            pT = ph.enter_context(nc.psum_tensor("pT", [P, 512], F32))
            pW = ph.enter_context(nc.psum_tensor("pW", [P, 512], F32))
            loaded = sem("weights_loaded")
            made = sem("pool_masks_made")
            blank = sem("blank_masks_ready")
            dve_masks = sem("dve_masks_made")
            scaled = sem("weights_scaled")
            wrmean = sem("router_sum_ready")
            eb_exp = sem("bias_exp_ready")
            eb_min = sem("bias_min_ready")
            eb_elu = sem("bias_elu_ready")
            eb_rows = sem("bias_rows_ready")
            zero_ready = sem("zero_ready")
            fold_t = sem("fold_transposed")
            fold_c = sem("fold_copied")
            fold_m = sem("fold_product_ready")
            fold_d = sem("fold_done")
            with nc.Block() as block:
                @block.sync
                def _(sp):
                    loads = 0
                    with nc.allow_non_contiguous_dma(reason="a few small weight columns"):
                        for dst_ap, src_ap in (
                            (gw[:], gnn_W.rearrange("(k p) n -> p k n", p=P)),
                            (wlr[0:GH, :], gnn_Wl), (wlr[GH:2 * GH, :], gnn_Wr),
                            (gb_b[:], gnn_b.partition_broadcast(P)),
                            (wn1c[:], w_norm1.rearrange("(k p) -> p k", p=P)),
                            (wqkv[:], w_qkv.rearrange("(k p) n -> p k n", p=P)),
                            (wout[:], w_out.rearrange("(k p) n -> p k n", p=P)),
                            (bout_b[:], b_out.partition_broadcast(P)),
                            (wn2_b[:], w_norm2.partition_broadcast(P)),
                            (wr_raw[:], wr.rearrange("d o -> (d o)").partition_broadcast(P)),
                            (br_b[:], br.partition_broadcast(P)),
                            (b2_b[:], b2.partition_broadcast(P)),
                            (b1c[:], b1.rearrange("(k p) -> p k", p=P)),
                        ):
                            sp.dma_start(dst_ap, src_ap).then_inc(loaded, 16)
                            loads += 1
                    assert loads == 13
                    sp.wait_ge(eb_rows, 1)

                @block.gpsimd
                def _(pool):
                    pool.wait_ge(blank, 5)
                    pool.affine_select(out=ident[:], in_=ident[:], compare_op=ALU.not_equal, fill=1.0, base=0,
                                       pattern=[[-1, P]], channel_multiplier=1).then_inc(made, 1)
                    pool.affine_select(out=before[:], in_=ones[:], compare_op=ALU.is_gt, fill=0.0, base=0,
                                       pattern=[[-1, P]], channel_multiplier=1).then_inc(made, 1)
                    pool.affine_select(out=after[:], in_=ones[:], compare_op=ALU.is_gt, fill=0.0, base=0,
                                       pattern=[[1, P]], channel_multiplier=-1).then_inc(made, 1)
                    pool.affine_select(out=spread8[:].rearrange("h k (q e) -> h k q e", e=32),
                                       in_=spread8[:].rearrange("h k (q e) -> h k q e", e=32),
                                       compare_op=ALU.not_equal, fill=1.0, base=0,
                                       pattern=[[-4, KB], [-1, 4], [0, 32]], channel_multiplier=1).then_inc(made, 1)

                @block.vector
                def _(dve):
                    dve.memset(ident[:], 0.0).then_inc(blank, 1)
                    dve.memset(ones[:], 1.0).then_inc(blank, 1)
                    dve.memset(spread8[:], 0.0).then_inc(blank, 1)
                    dve.memset(headmask[:], 0.0).then_inc(blank, 1)
                    dve.memset(mask8[:], 0.0).then_inc(blank, 1)
                    dve.memset(halfneg[:], -0.5)
                    dve.memset(zero[:], 0.0).then_inc(zero_ready, 1)
                    dve.wait_ge(blank, 5)
                    for q in range(4):
                        dve.memset(headmask[32 * q:32 * q + 32, 32 * q:32 * q + 32], 1.0)
                        for k in range(KB):
                            last = dve.memset(mask8[32 * q:32 * q + 32, k, 4 * k + q:4 * k + q + 1], 1.0)
                    last.then_inc(dve_masks, 1)
                    dve.wait_ge(loaded, 13 * 16)
                    for k in range(KB):
                        dve.tensor_scalar(wqkv[:, k, :], wqkv[:, k, :], wn1c[:, k:k + 1], None, ALU.mult)\
                           .then_inc(scaled, 1)
                    dve.tensor_reduce(wrsum[:], wr_raw[:], AX.X, ALU.add).then_inc(wrmean, 1)
                    dve.wait_ge(wrmean, 1)
                    dve.tensor_scalar(wrsum[:], wrsum[:], 1.0 / D, None, ALU.mult).then_inc(wrmean, 1)
                    dve.wait_ge(wrmean, 2)
                    dve.tensor_scalar(wr_b[:], wr_raw[:], wrsum[:, 0:1], None, ALU.subtract).then_inc(wrmean, 1)
                    dve.wait_ge(eb_exp, 1)
                    dve.tensor_scalar(eb1[:], eb[:], 1.0, -1.0, ALU.min, ALU.add).then_inc(eb_min, 1)
                    dve.wait_ge(eb_min, 1)
                    dve.tensor_tensor(eb[:], eb1[:], gb_b[:], ALU.max).then_inc(eb_elu, 1)
                    dve.wait_ge(eb_elu, 1)
                    dve.tensor_copy(ebrow[:], eb[:].unsqueeze(1).to_broadcast([P, 8 * GH, OD])).then_inc(eb_rows, 1)
                    dve.wait_ge(fold_t, 1)
                    dve.tensor_copy(gwT[:], pT[0:OD, 0:KB * P].rearrange("p (k n) -> p k n", k=KB)).then_inc(fold_c, 1)
                    dve.tensor_copy(wlrT[:], pT[0:OD, KB * P:KB * P + 2 * GH]).then_inc(fold_c, 1)
                    dve.tensor_copy(wD[:, :, 0:OD], gw[:]).then_inc(fold_d, 1)
                    dve.wait_ge(fold_m, 1)
                    pv = pW[:, 0:KB * 2 * GH].rearrange("p (k n) -> p k n", k=KB)
                    dve.tensor_copy(wS[:], pv[:, :, 0:GH]).then_inc(fold_d, 1)
                    dve.tensor_copy(wD[:, :, OD:OD + GH], pv[:, :, GH:2 * GH]).then_inc(fold_d, 1)

                @block.scalar
                def _(act):
                    act.wait_ge(loaded, 13 * 16)
                    act.activation(eb[:], gb_b[:], ACT.Exp).then_inc(eb_exp, 1)

                @block.tensor
                def _(pe):
                    pe.wait_ge(loaded, 13 * 16)
                    pe.wait_ge(made, 4)
                    for k in range(KB):
                        pe.transpose(pT[0:OD, k * P:(k + 1) * P], gw[:, k, :], ident[:])
                    pe.transpose(pT[0:OD, KB * P:KB * P + 2 * GH], wlr[:], ident[0:2 * GH, 0:2 * GH]).then_inc(fold_t, 1)
                    pe.wait_ge(fold_c, 2)
                    for k in range(KB):
                        last = pe.matmul(pW[:, 2 * GH * k:2 * GH * (k + 1)], gwT[:, k, :], wlrT[:], start=True, stop=True)
                    last.then_inc(fold_m, 1)

        A_STEPS, B_STEPS = (24, 74), (76, 96)
        A_PER, B_PER = 2, 5
        assert (A_STEPS[1] - A_STEPS[0]) * A_PER == EC and (B_STEPS[1] - B_STEPS[0]) * B_PER == EC
        PLAN = ((False, 0, 2), (True, 2, 24), (False, 24, 26), (True, 26, 72), (False, 72, 78), (True, 78, 94),
                (False, 94, NG + 1))

        with phase() as ph:
            def sb(name, shape, dt=F32):
                return ph.enter_context(nc.sbuf_tensor(name, shape, dt))

            def two(name, shape, dt=F32):
                return [sb(f"{name}{u}", shape, dt) for u in range(2)]

            i_dst, i_src, i_own = sb("i_dst", [P, EC], I32), sb("i_src", [P, EC], I32), sb("i_own", [P, EC], I32)
            i_acc, i_dump = sb("i_acc", [P, EC], I32), sb("i_dump", [P, 1], I32)
            pair, goal, put_ix = two("pair", [P, 2], I32), two("goal", [P, 1], I32), two("put_ix", [P, 1], I32)
            dump, own = sb("dump", [P, 1]), sb("own", [P, EC])
            ends = two("ends", [P, 2, D])
            est, emv, ers = two("est", [P, 2, 6]), two("emv", [P, 2, 2]), two("ers", [P, 2])
            norm, normT = two("norm", [P, 2, D]), two("normT", [P, 2 * KB, P])
            ownb, same, junk = two("ownb", [P, P]), two("same", [P, P]), two("junk", [P, P])
            cnt, ev = two("cnt", [P, 4]), two("ev", [P, 2 * GH])
            msg, tot = two("msg", [P, MSG]), two("tot", [P, MSG])
            ag, rr, gv, ge = two("ag", [P, MSG]), two("rr", [P, 2 * GH]), two("gv", [P, D]), two("ge", [P, D])
            xin, xs, xT = two("xin", [P, T, D]), two("xs", [P, T, D + 1]), two("xT", [P, KB, ROWS])
            st, mv = two("pst", [P, T, 6]), two("pmv", [P, T, 2])
            sc, sv, rq, sh = two("psc", [P, T]), two("psv", [P, T]), two("prq", [P, T]), two("psh", [P, T])
            ke, kk = two("ke", [P, T, D]), two("kk", [P, T, D])
            gsb, gT, kvT = sb("gsb", [P, KB, D + 1]), sb("gT", [P, KB, D]), sb("kvT", [P, KB, P])
            pT = ph.enter_context(nc.psum_tensor("p1T", [P, KB, ROWS], F32))
            pK = ph.enter_context(nc.psum_tensor("p1K", [P, T, D], F32))
            pGm = [ph.enter_context(nc.psum_tensor(f"p1G{m}", [P, 512], F32)) for m in range(KB)]
            pE = ph.enter_context(nc.psum_tensor("pE", [P, 2 * KB * P], F32))
            pF = ph.enter_context(nc.psum_tensor("pF", [P, 512], F32))
            pX = pF[:, 0:OD + GH]
            pS = pF[:, OD + GH:OD + GH + P]
            pM = pF[:, OD + GH + P:OD + GH + P + MSG]

            idx_init, idx_load, idx_float = sem("index_blank"), sem("index_loaded"), sem("index_float")
            ix_col, ix_col2, ix_col3 = sem("edge_columns_ready"), sem("sum_columns_ready"), sem("goal_columns_ready")
            got = [sem(f"ends_gathered{u}") for u in range(2)]
            e_stat, e_aggr, e_veps, e_rstd = sem("ends_stats"), sem("ends_aggregated"), sem("ends_var_eps"), sem("ends_rstd")
            normed, e_turned, e_copied = sem("ends_normed"), sem("ends_turned"), sem("ends_copied")
            filled, spread, eq = sem("shared_bank_filled"), sem("own_spread"), sem("same_ready")
            counted, clipped, gap = sem("earlier_counted"), sem("earlier_clipped"), sem("dump_gap")
            target, target_i = sem("target_float"), sem("target_ready")
            sc_copy, sc_lrelu, sc_exp = sem("score_copied"), sem("score_lrelu"), sem("score_exp")
            msgs, tot_ready, added = sem("messages_ready"), sem("sums_copied"), sem("sums_added")
            cleared, prefilled = sem("accumulators_zero"), sem("default_rows_written")
            fetched = [sem(f"sums_fetched{u}") for u in range(2)]
            guard, recip, mean_r, biased = sem("rowsum_guarded"), sem("rowsum_reciprocal"), sem("rows_normalised"), sem("rows_biased")
            expd, mined, elud, placed = sem("rows_exp"), sem("rows_min"), sem("rows_elu"), sem("rows_placed")
            x_in = [sem(f"x_loaded{u}") for u in range(2)]
            stat, aggr, vs, s_rdy = sem("x_stats"), sem("x_aggregated"), sem("x_scale_var"), sem("x_scale_ready")
            v_e, r_rdy, iv, bk = sem("x_var_eps"), sem("x_rstd_ready"), sem("x_root_ready"), sem("x_back_ready")
            mm_s, sh_s, kept = sem("x_mean_scaled"), sem("x_shift_ready"), sem("x_stats_kept")
            one_col, scaled_x = sem("one_column_ready"), sem("xs_ready")
            turned, copied = sem("xs_turned"), sem("xT_copied")
            k_rdy, k_exp, k_min, k_elu, k_mask = sem("k_ready"), sem("k_exp_ready"), sem("k_min_ready"), sem("k_elu_ready"), sem("k_seen_rows_cleared")
            gram, g_copy, g_turn, gT_rdy = sem("gram_added"), sem("gram_copied"), sem("gram_turned"), sem("gramT_copied")
            kv_rdy, kv_m, m_rdy, m_copy = sem("kvT_ready"), sem("kvT_masked"), sem("mix_ready"), sem("mix_copied")
            HALF = T // 2

            def first(c, k=1):
                return isinstance(c.n, int) and c.n < k

            def slots(g, per, lo, hi):
                if isinstance(g.n, int):
                    return [At(c, c % 2, c // 2) for c in range((g.n - lo) * per, (g.n - lo + 1) * per)]
                return [At((g.n - lo) * per + k, (g.buf * per + k) % 2, (g.turn - lo // 2) * per + (g.buf * per + k) // 2)
                        for k in range(per)]

            def a_slots(g, looped):
                if looped not in (None, "A") or (looped is None and not A_STEPS[0] <= g.n <= A_STEPS[1]):
                    return []
                return slots(g, A_PER, *A_STEPS)

            def b_slots(g, looped):
                if looped not in (None, "B") or (looped is None and not B_STEPS[0] <= g.n <= B_STEPS[1]):
                    return []
                return slots(g, B_PER, *B_STEPS)

            def go(eng, body):
                for part, entry in zip((None, "Z", None, "A", None, "B", None), PLAN):
                    run_plan(eng, lambda g: body(g, part), (entry,))

            with nc.Block() as block:
                @block.sync
                def _(sp):
                    wait_apart(sp, idx_init, 3)
                    for t, a in ((i_dst, dst), (i_src, src), (i_own, src)):
                        sp.dma_start(t[0:EP, :], a.rearrange("(p c) -> p c", c=EC)).then_inc(idx_load, 16)
                    za = acc_d.rearrange("r c -> (r c)").rearrange("(g p c) -> g p c", p=P, c=8 * MSG)
                    ga = gnn_d.rearrange("(g p j) d -> g p (j d)", p=P, j=8)

                    def step(g, part):
                        if g.inside(0, NG):
                            if not first(g, 2):
                                wait_apart(sp, scaled_x, T * (g.n - 1))
                            sp.dma_start(xin[g.buf][:].rearrange("p j d -> p (j d)"), group_rows(x, g, D))\
                              .then_inc(x_in[g.buf], 16)
                        if part == "Z" or (part is None and g.n < A_STEPS[0]):
                            if isinstance(g.n, int):
                                blocks = [3 * g.n, 3 * g.n + 1, 3 * g.n + 2]
                            else:
                                blocks = [2 * g.n + 2, 2 * g.n + 3]
                            for b in blocks:
                                sp.dma_start(za[b], zero[:]).then_inc(cleared, 16)
                        elif part == "A" or (part is None and g.n < A_STEPS[1]):
                            sp.dma_start(ga[g.n - A_STEPS[0]], ebrow[:].rearrange("p a b -> p (a b)")).then_inc(prefilled, 16)
                    go(sp, step)

                @block.gpsimd
                def _(pool):
                    pool.iota(i_own[:], pattern=[[0, EC]], base=N, channel_multiplier=1).then_inc(idx_init, 1)
                    pool.iota(i_dst[:], pattern=[[0, EC]], base=0, channel_multiplier=0).then_inc(idx_init, 1)
                    pool.iota(i_src[:], pattern=[[0, EC]], base=0, channel_multiplier=0).then_inc(idx_init, 1)
                    pool.iota(i_dump[:], pattern=[[0, 1]], base=N, channel_multiplier=1).then_inc(idx_init, 1)
                    pool.wait_ge(idx_load, 48)

                    def scales(g):
                        u = g.buf
                        if not first(g, 2):
                            wait_apart(pool, scaled_x, T * (g.n - 1))
                        wait_apart(pool, aggr, T * (g.n + 1))
                        pool.tensor_scalar(sv[u][:], mv[u][:, :, 1], 1.0 + RMS_EPS, LN_EPS * RMS_EPS, ALU.mult, ALU.add)\
                            .then_inc(vs, 1)
                        pool.tensor_scalar(rq[u][:], mv[u][:, :, 1], LN_EPS, 1.0, ALU.add, ALU.mult).then_inc(v_e, 1)
                        pool.tensor_scalar(sh[u][:], mv[u][:, :, 0], -1.0, 1.0, ALU.mult, ALU.mult).then_inc(mm_s, 1)
                        pool.wait_ge(vs, g.n + 1)
                        pool.tensor_tensor(sc[u][:], sv[u][:], halfneg[:, 0:T], ALU.pow).then_inc(s_rdy, 1)
                        pool.wait_ge(v_e, g.n + 1)
                        pool.tensor_tensor(rq[u][:], rq[u][:], halfneg[:, 0:T], ALU.pow).then_inc(r_rdy, 1)
                        pool.wait_ge(s_rdy, g.n + 1)
                        pool.wait_ge(mm_s, g.n + 1)
                        pool.tensor_tensor(sh[u][:], sh[u][:], sc[u][:], ALU.mult).then_inc(sh_s, 1)
                        pool.tensor_tensor(sv[u][:], sv[u][:], sc[u][:], ALU.mult).then_inc(iv, 1)
                        pool.wait_ge(iv, g.n + 1)
                        pool.wait_ge(r_rdy, g.n + 1)
                        pool.tensor_tensor(back_a[:, bass.ds(g.n * T, T)], rq[u][:], sv[u][:], ALU.mult).then_inc(bk, 1)
                        pool.tensor_copy(scale_a[:, bass.ds(g.n * T, T)], sc[u][:]).then_inc(kept, 1)
                        wait_apart(pool, sh_s, g.n + 1)
                        pool.tensor_copy(shift_a[:, bass.ds(g.n * T, T)], sh[u][:]).then_inc(kept, 1)

                    def gather(c):
                        if not first(c, 2):
                            wait_apart(pool, normed, 2 * (c.n - 1))
                        for side, idx in enumerate((i_dst, i_src)):
                            pool.tensor_copy(pair[c.buf][:, side:side + 1], idx[:, bass.ds(c.n, 1)]).then_inc(ix_col, 1)
                        wait_apart(pool, ix_col, 2 * (c.n + 1))
                        for side in range(2):
                            pool.indirect_dma_start(
                                out=ends[c.buf][:, side, :], out_offset=None, in_=x,
                                in_offset=bass.IndirectOffsetOnAxis(ap=pair[c.buf][:, side:side + 1], axis=0)
                            ).then_inc(got[c.buf], 16)

                    def end_scale(c):
                        wait_apart(pool, e_aggr, 2 * (c.n + 1))
                        if not first(c, 2):
                            wait_apart(pool, normed, 2 * (c.n - 1))
                        pool.tensor_scalar(ers[c.buf][:], emv[c.buf][:, :, 1], LN_EPS, 1.0, ALU.add, ALU.mult)\
                            .then_inc(e_veps, 1)
                        pool.wait_ge(e_veps, c.n + 1)
                        pool.tensor_tensor(ers[c.buf][:], ers[c.buf][:], halfneg[:, 0:2], ALU.pow).then_inc(e_rstd, 1)

                    def add_sums(c):
                        pool.wait_ge(tot_ready, c.n + 1)
                        wait_apart(pool, target_i, c.n + 1)
                        if first(c):
                            pool.wait_ge(cleared, 16 * (PADN // (8 * P)))
                        else:
                            wait_apart(pool, added, 16 * c.n)
                        pool.indirect_dma_start(
                            out=acc_d, out_offset=bass.IndirectOffsetOnAxis(ap=goal[c.buf][:], axis=0),
                            in_=tot[c.buf][:], in_offset=None, compute_op=ALU.add).then_inc(added, 16)

                    def fetch_sums(c):
                        if not first(c, 2):
                            wait_apart(pool, mean_r, c.n - 1)
                        if first(c):
                            pool.wait_ge(added, 16 * EC)
                        pool.tensor_copy(goal[c.buf][:], i_acc[:, bass.ds(c.n, 1)]).then_inc(ix_col2, 1)
                        wait_apart(pool, ix_col2, c.n + 1)
                        pool.indirect_dma_start(
                            out=ag[c.buf][:], out_offset=None, in_=acc_d,
                            in_offset=bass.IndirectOffsetOnAxis(ap=goal[c.buf][:], axis=0)).then_inc(fetched[c.buf], 16)

                    def place(c):
                        wait_apart(pool, elud, c.n + 1)
                        if first(c):
                            pool.wait_ge(prefilled, 16 * (PADN // (8 * P)))
                        else:
                            wait_apart(pool, placed, 16 * c.n)
                        pool.tensor_copy(put_ix[c.buf][:], i_acc[:, bass.ds(c.n, 1)]).then_inc(ix_col3, 1)
                        wait_apart(pool, ix_col3, c.n + 1)
                        pool.indirect_dma_start(
                            out=gnn_d, out_offset=bass.IndirectOffsetOnAxis(ap=put_ix[c.buf][:], axis=0),
                            in_=gv[c.buf][:], in_offset=None).then_inc(placed, 16)

                    def node_tile(c):
                        if first(c) and c.n == 0:
                            fetch_sums(At(0, 0, 0))
                            fetch_sums(At(1, 1, 0))
                        if (c + 2).inside(0, EC):
                            fetch_sums(c + 2)
                        if (c + -1).inside(0, EC):
                            place(c + -1)

                    scales(At(0, 0, 0))
                    scales(At(1, 1, 0))

                    def step(g, part):
                        slots_b = b_slots(g, part)
                        for c in a_slots(g, part):
                            if first(c) and c.n == 0:
                                gather(At(0, 0, 0))
                                gather(At(1, 1, 0))
                                end_scale(At(0, 0, 0))
                            if (c + 2).inside(0, EC):
                                gather(c + 2)
                            if (c + 1).inside(0, EC):
                                end_scale(c + 1)
                            if (c + -2).inside(0, EC):
                                add_sums(c + -2)
                        for c in slots_b[0:2]:
                            node_tile(c)
                        if (g + 2).inside(0, NG):
                            scales(g + 2)
                        for c in slots_b[2:]:
                            node_tile(c)
                    go(pool, step)
                    pool.wait_ge(placed, 16 * EC)

                @block.vector
                def _(dve):
                    for u in range(2):
                        dve.memset(xs[u][:, :, D:D + 1], 1.0).then_inc(one_col, 1)
                    dve.wait_ge(idx_init, 4)
                    dve.wait_ge(idx_load, 48)
                    dve.tensor_copy(own[:], i_own[:]).then_inc(idx_float, 1)
                    dve.tensor_copy(dump[:], i_dump[:]).then_inc(idx_float, 1)
                    dve.wait_ge(idx_float, 2)

                    def stats(g):
                        u = g.buf
                        dve.wait_ge(x_in[u], 16 * (g.turn + 1))
                        if not first(g, 2):
                            dve.wait_ge(mm_s, g.n - 1)
                            dve.wait_ge(vs, g.n - 1)
                            dve.wait_ge(v_e, g.n - 1)
                        for j in range(T):
                            dve.bn_stats(st[u][:, j, :], xin[u][:, j, :]).then_inc(stat, 1)
                        for j in range(T):
                            wait_apart(dve, stat, T * g.n + j + 1)
                            dve.bn_aggr(mv[u][:, j, :], st[u][:, j, :]).then_inc(aggr, 1)

                    def elu_k(g):
                        u = g.buf
                        if not first(g, 2):
                            dve.wait_ge(gram, g.n - 1)
                        for h in range(2):
                            part = slice(HALF * h, HALF * h + HALF)
                            dve.wait_ge(k_exp, 2 * g.n + h + 1)
                            dve.tensor_scalar(ke[u][:, part, :], ke[u][:, part, :], 1.0, None, ALU.min).then_inc(k_min, 1)
                            dve.wait_ge(k_min, 2 * g.n + h + 1)
                            dve.scalar_tensor_tensor(out=kk[u][:, part, :], in0=pK[:, part, :], scalar=1.0,
                                                     in1=ke[u][:, part, :], op0=ALU.add, op1=ALU.max).then_inc(k_elu, 1)
                        if isinstance(g.n, int) and g.n == NG - 1:
                            dve.wait_ge(k_elu, 2 * NG)
                            dve.memset(kk[u][0:SEEN_P, :, :], 0.0).then_inc(k_mask, 1)

                    def end_stats(c):
                        u = c.buf
                        dve.wait_ge(got[u], 32 * (c.turn + 1))
                        if not first(c, 2):
                            dve.wait_ge(normed, 2 * (c.n - 1))
                        for s in range(2):
                            dve.bn_stats(est[u][:, s, :], ends[u][:, s, :]).then_inc(e_stat, 1)
                        if not first(c, 2):
                            dve.wait_ge(e_veps, c.n - 1)
                            dve.wait_ge(filled, c.n - 1)
                            dve.wait_ge(target, c.n - 1)
                        dve.tensor_copy(ownb[u][:], own[:, bass.ds(c.n, 1)].to_broadcast([P, P])).then_inc(spread, 1)
                        wait_apart(dve, e_stat, 2 * (c.n + 1))
                        for s in range(2):
                            dve.bn_aggr(emv[u][:, s, :], est[u][:, s, :]).then_inc(e_aggr, 1)

                    def end_norm(c):
                        u = c.buf
                        dve.wait_ge(e_rstd, c.n + 1)
                        if not first(c, 2):
                            dve.wait_ge(e_turned, c.n - 1)
                        for s in range(2):
                            dve.tensor_scalar(norm[u][:, s, :], ends[u][:, s, :], emv[u][:, s, 0:1], ers[u][:, s:s + 1],
                                              ALU.subtract, ALU.mult).then_inc(normed, 1)

                    def scores(c):
                        u = c.buf
                        dve.wait_ge(filled, c.n + 2)
                        dve.tensor_copy(ev[u][:, 0:GH], pX[:, OD:OD + GH]).then_inc(sc_copy, 1)
                        dve.wait_ge(sc_copy, c.n + 1)
                        if not first(c, 2):
                            dve.wait_ge(sc_exp, c.n - 1)
                        dve.scalar_tensor_tensor(out=ev[u][:, GH:2 * GH], in0=pX[:, OD:OD + GH], scalar=0.2,
                                                 in1=ev[u][:, 0:GH], op0=ALU.mult, op1=ALU.max).then_inc(sc_lrelu, 1)

                    def messages(c):
                        u = c.buf
                        dve.wait_ge(sc_exp, c.n + 1)
                        dve.tensor_tensor(msg[u][:, 0:GH * OD].rearrange("p (h d) -> p h d", h=GH),
                                          pX[:, 0:OD].unsqueeze(1).to_broadcast([P, GH, OD]),
                                          msg[u][:, GH * OD:MSG].unsqueeze(2).to_broadcast([P, GH, OD]), ALU.mult)\
                           .then_inc(msgs, 1)

                    def shared_sources(c):
                        u = c.buf
                        dve.wait_ge(filled, c.n + 1)
                        dve.wait_ge(spread, c.n + 1)
                        dve.tensor_scalar(same[u][:], pS, ownb[u][:, 0:1], None, ALU.is_equal).then_inc(eq, 1)
                        dve.tensor_scalar(cnt[u][:, 2:3], dump[:], ownb[u][:, 0:1], None, ALU.subtract).then_inc(gap, 1)
                        dve.wait_ge(eq, c.n + 1)
                        dve.tensor_tensor_reduce(junk[u][:], same[u][:], before[:], 1.0, 0.0, ALU.mult, ALU.add,
                                                 cnt[u][:, 0:1]).then_inc(counted, 1)
                        dve.wait_ge(counted, c.n + 1)
                        dve.tensor_scalar(cnt[u][:, 1:2], cnt[u][:, 0:1], 1.0, None, ALU.min).then_inc(clipped, 1)
                        dve.wait_ge(clipped, c.n + 1)
                        dve.wait_ge(gap, c.n + 1)
                        dve.scalar_tensor_tensor(out=cnt[u][:, 3:4], in0=cnt[u][:, 1:2], scalar=cnt[u][:, 2:3],
                                                 in1=ownb[u][:, 0:1], op0=ALU.mult, op1=ALU.add).then_inc(target, 1)
                        dve.wait_ge(target, c.n + 1)
                        if not first(c, 2):
                            dve.wait_ge(added, 16 * (c.n - 1))
                        dve.tensor_copy(goal[u][:], cnt[u][:, 3:4]).then_inc(target_i, 1)
                        dve.tensor_copy(i_acc[:, bass.ds(c.n, 1)], cnt[u][:, 3:4])

                    def copy_sums(c):
                        u = c.buf
                        dve.wait_ge(filled, c.n + 3)
                        if not first(c, 2):
                            dve.wait_ge(added, 16 * (c.n - 1))
                        dve.tensor_copy(tot[u][:], pM).then_inc(tot_ready, 1)

                    def mean_rows(c):
                        u = c.buf
                        dve.wait_ge(fetched[u], 16 * (c.turn + 1))
                        dve.tensor_scalar(rr[u][:, 0:GH], ag[u][:, GH * OD:MSG], GNN_EPS, None, ALU.max).then_inc(guard, 1)
                        dve.wait_ge(guard, c.n + 1)
                        dve.reciprocal(rr[u][:, GH:2 * GH], rr[u][:, 0:GH]).then_inc(recip, 1)
                        dve.wait_ge(recip, c.n + 1)
                        if not first(c, 2):
                            dve.wait_ge(placed, 16 * (c.n - 1))
                        v3 = gv[u][:].rearrange("p (h d) -> p h d", h=GH)
                        dve.tensor_tensor(v3, ag[u][:, 0:GH * OD].rearrange("p (h d) -> p h d", h=GH),
                                          rr[u][:, GH:2 * GH].unsqueeze(2).to_broadcast([P, GH, OD]), ALU.mult)\
                           .then_inc(mean_r, 1)
                        dve.wait_ge(mean_r, c.n + 1)
                        dve.tensor_tensor(v3, v3, gb_b[:].unsqueeze(1).to_broadcast([P, GH, OD]), ALU.add)\
                           .then_inc(biased, 1)

                    def elu_rows(c):
                        u = c.buf
                        dve.wait_ge(expd, c.n + 1)
                        dve.tensor_scalar(ge[u][:], ge[u][:], 1.0, -1.0, ALU.min, ALU.add).then_inc(mined, 1)
                        dve.wait_ge(mined, c.n + 1)
                        dve.tensor_tensor(gv[u][:], gv[u][:], ge[u][:], ALU.max).then_inc(elud, 1)

                    stats(At(0, 0, 0))
                    stats(At(1, 1, 0))

                    def edge_tile(c):
                        if first(c) and c.n == 0:
                            end_stats(At(0, 0, 0))
                        if c.inside(0, EC):
                            end_norm(c)
                        if (c + -1).inside(0, EC):
                            scores(c + -1)
                        if (c + 1).inside(0, EC):
                            end_stats(c + 1)
                        if (c + -2).inside(0, EC):
                            copy_sums(c + -2)
                        if (c + -1).inside(0, EC):
                            messages(c + -1)
                        if c.inside(0, EC):
                            shared_sources(c)

                    def node_tile(c):
                        if c.inside(0, EC):
                            mean_rows(c)
                        if (c + -1).inside(0, EC):
                            elu_rows(c + -1)

                    def step(g, part):
                        slots_b = b_slots(g, part)
                        slots_a = a_slots(g, part)
                        for c in slots_a[0:1]:
                            edge_tile(c)
                        for c in slots_b[0:2]:
                            node_tile(c)
                        if (g + 2).inside(0, NG):
                            stats(g + 2)
                        for c in slots_a[1:]:
                            edge_tile(c)
                        if g.inside(0, NG):
                            elu_k(g)
                        for c in slots_b[2:]:
                            node_tile(c)
                    go(dve, step)

                    for m in range(KB):
                        dve.wait_ge(gram, NG)
                        dve.tensor_copy(gsb[:, m, :], pGm[m][:, 0:D + 1]).then_inc(g_copy, 1)
                    dve.wait_ge(g_turn, 1)
                    dve.tensor_copy(gT[:], pT[:, :, 0:D]).then_inc(gT_rdy, 1)
                    dve.wait_ge(kv_rdy, 1)
                    for m in range(KB):
                        dve.tensor_tensor(kvT[:, m, :], pK[:, m, 0:P], headmask[:], ALU.mult).then_inc(kv_m, 1)
                    dve.wait_ge(g_copy, KB)
                    for m in range(KB):
                        dve.tensor_scalar(ks8[:, m, :], mask8[:, m, :], gsb[:, m, D:D + 1], None, ALU.mult)
                    dve.wait_ge(m_rdy, 1)
                    dve.tensor_copy(mix[:], pT[:, :, 0:D]).then_inc(m_copy, 1)

                @block.scalar
                def _(act):
                    def scale_x(g):
                        u = g.buf
                        act.wait_ge(x_in[u], 16 * (g.turn + 1))
                        act.wait_ge(s_rdy, g.n + 1)
                        act.wait_ge(sh_s, g.n + 1)
                        if not first(g, 2):
                            act.wait_ge(gram, g.n - 1)
                        for j in range(T):
                            act.activation(xs[u][:, j, 0:D], xin[u][:, j, :], ACT.Identity, bias=sh[u][:, j:j + 1],
                                           scale=sc[u][:, j:j + 1]).then_inc(scaled_x, 1)

                    def copy_x(g):
                        act.wait_ge(turned, g.n + 1)
                        if not first(g, 2):
                            act.wait_ge(k_rdy, 2 * (g.n - 1))
                        act.activation(xT[g.buf][:], pT[:], ACT.Copy).then_inc(copied, 1)

                    def exp_k(g):
                        u = g.buf
                        if not first(g, 2):
                            act.wait_ge(k_elu, 2 * (g.n - 1))
                        for h in range(2):
                            part = slice(HALF * h, HALF * h + HALF)
                            act.wait_ge(k_rdy, 2 * g.n + h + 1)
                            act.activation(ke[u][:, part, :], pK[:, part, :], ACT.Exp).then_inc(k_exp, 1)

                    def copy_ends(c):
                        u = c.buf
                        act.wait_ge(e_turned, c.n + 1)
                        if not first(c, 2):
                            act.wait_ge(filled, c.n)
                        act.activation(normT[u][:].rearrange("p a b -> p (a b)"), pE[:], ACT.Copy).then_inc(e_copied, 1)

                    def exp_scores(c):
                        u = c.buf
                        act.wait_ge(sc_lrelu, c.n + 1)
                        if not first(c, 2):
                            act.wait_ge(filled, c.n + 1)
                        act.activation(msg[u][:, GH * OD:MSG], ev[u][:, GH:2 * GH], ACT.Exp).then_inc(sc_exp, 1)

                    def exp_rows(c):
                        act.wait_ge(biased, c.n + 1)
                        if not first(c, 2):
                            act.wait_ge(elud, c.n - 1)
                        act.activation(ge[c.buf][:], gv[c.buf][:], ACT.Exp).then_inc(expd, 1)

                    scale_x(At(0, 0, 0))
                    copy_x(At(0, 0, 0))

                    def edge_tile(c):
                        if c.inside(0, EC):
                            copy_ends(c)
                        if (c + -1).inside(0, EC):
                            exp_scores(c + -1)

                    def step(g, part):
                        slots_a, slots_b = a_slots(g, part), b_slots(g, part)
                        for c in slots_a[0:1]:
                            edge_tile(c)
                        if (g + 1).inside(0, NG):
                            scale_x(g + 1)
                        for c in slots_b[0:2]:
                            if c.inside(0, EC):
                                exp_rows(c)
                        for c in slots_a[1:]:
                            edge_tile(c)
                        if g.inside(0, NG):
                            exp_k(g)
                        if (g + 1).inside(0, NG):
                            copy_x(g + 1)
                        for c in slots_b[2:]:
                            if c.inside(0, EC):
                                exp_rows(c)
                    go(act, step)

                @block.tensor
                def _(pe):
                    def turn(g):
                        pe.wait_ge(scaled_x, T * (g.n + 1))
                        if not first(g):
                            pe.wait_ge(copied, g.n)
                        for j in range(T):
                            for k in range(KB):
                                last = pe.transpose(pT[:, k, j * P:(j + 1) * P], xs[g.buf][:, j, k * P:(k + 1) * P], ident[:])
                        last.then_inc(turned, 1)

                    def project(g, h):
                        pe.wait_ge(copied, g.n + 1)
                        if not first(g):
                            pe.wait_ge(k_elu, 2 * (g.n - 1) + h + 1)
                        for j in range(HALF * h, HALF * h + HALF):
                            for k in range(KB):
                                last = pe.matmul(pK[:, j, :], xT[g.buf][:, k, j * P:(j + 1) * P],
                                                 wqkv[:, k, D:2 * D], start=(k == 0), stop=(k == KB - 1))
                        last.then_inc(k_rdy, 1)

                    def add_gram(g, h):
                        final = isinstance(g.n, int) and g.n == NG - 1
                        if final:
                            pe.wait_ge(k_mask, 1)
                        pe.wait_ge(k_elu, 2 * g.n + h + 1)
                        for j in range(HALF * h, HALF * h + HALF):
                            for m in range(KB):
                                last = pe.matmul(pGm[m][:, 0:D + 1], kk[g.buf][:, j, m * P:(m + 1) * P], xs[g.buf][:, j, :],
                                                 start=(first(g) and j == 0), stop=(final and j == T - 1),
                                                 skip_group_check=True)
                        if h:
                            last.then_inc(gram, 1)

                    def turn_ends(c):
                        u = c.buf
                        pe.wait_ge(normed, 2 * (c.n + 1))
                        if not first(c):
                            pe.wait_ge(e_copied, c.n)
                        for s in range(2):
                            for k in range(KB):
                                last = pe.transpose(pE[:, (KB * s + k) * P:(KB * s + k + 1) * P],
                                                    norm[u][:, s, k * P:(k + 1) * P], ident[:])
                        last.then_inc(e_turned, 1)

                    def turn_own(c):
                        return pe.transpose(pS, ownb[c.buf][:], ident[:])

                    def fill_shared(c):
                        if not first(c):
                            pe.wait_ge(msgs, c.n)
                        if c.inside(0, EC):
                            pe.wait_ge(eq, c.n + 1)
                        if not first(c, 2):
                            pe.wait_ge(tot_ready, c.n - 1)
                        if not first(c):
                            v = (c + 1).buf
                            last = pe.matmul(pM, same[v][:], msg[v][:], start=True, stop=True, skip_group_check=True)
                        if c.inside(0, EC):
                            u = c.buf
                            pe.wait_ge(e_copied, c.n + 1)
                            for k in range(KB):
                                pe.matmul(pX, normT[u][:, k, :], wD[:, k, :], start=(k == 0), stop=(k == KB - 1),
                                          skip_group_check=True)
                            for k in range(KB):
                                last = pe.matmul(pX[:, OD:OD + GH], normT[u][:, KB + k, :], wS[:, k, :], start=False,
                                                 stop=(k == KB - 1), skip_group_check=True)
                        if (c + 1).inside(0, EC):
                            pe.wait_ge(spread, c.n + 2)
                            last = turn_own(c + 1)
                        last.then_inc(filled, 1)

                    pe.wait_ge(one_col, 2)
                    turn(At(0, 0, 0))

                    def step(g, part):
                        slots_a = a_slots(g, part)
                        halves = [lambda: (g + -1).inside(0, NG) and add_gram(g + -1, 0),
                                  lambda: (g + -1).inside(0, NG) and add_gram(g + -1, 1),
                                  lambda: g.inside(0, NG) and project(g, 0),
                                  lambda: g.inside(0, NG) and project(g, 1)]
                        for k in range(2):
                            c = slots_a[k] if slots_a else None
                            halves[2 * k]()
                            if c is not None and c.inside(0, EC):
                                turn_ends(c)
                            halves[2 * k + 1]()
                            if c is not None and c.inside(0, EC + 1):
                                if first(c):
                                    pe.wait_ge(spread, 1)
                                    turn_own(c).then_inc(filled, 1)
                                fill_shared(c)
                        if (g + 1).inside(0, NG):
                            turn(g + 1)
                    go(pe, step)

                    pe.wait_ge(g_copy, KB)
                    for m in range(KB):
                        for k in range(KB):
                            last = pe.transpose(pT[:, k, m * P:(m + 1) * P], gsb[:, m, k * P:(k + 1) * P], ident[:])
                    last.then_inc(g_turn, 1)
                    pe.wait_ge(gT_rdy, 1)
                    for m in range(KB):
                        for k in range(KB):
                            last = pe.matmul(pK[:, m, 0:P], wqkv[:, k, 2 * D + m * P:2 * D + (m + 1) * P],
                                             gT[:, k, m * P:(m + 1) * P], start=(k == 0), stop=(k == KB - 1))
                    last.then_inc(kv_rdy, 1)
                    pe.wait_ge(kv_m, KB)
                    for m in range(KB):
                        last = pe.matmul(pT[:, m, 0:D], kvT[:, m, :], wout[:, m, :], start=True, stop=True)
                    last.then_inc(m_rdy, 1)
        early.close()

        with phase() as ph:
            def sb(name, shape, dt=F32):
                return ph.enter_context(nc.sbuf_tensor(name, shape, dt))

            def two(name, shape, dt=F32):
                return [sb(f"{name}{u}", shape, dt) for u in range(2)]
            RING = 4
            xin, gin, xg = ([sb(f"{name}{u}", [P, T, D]) for u in range(RING)] for name in ("x2in", "g2in", "xg"))
            xs, xb = two("xs2", [P, T, D]), two("xb", [P, T, D])
            xT = two("xT2", [P, KB, ROWS])
            qn, qe = sb("qn", [P, KB, ROWS]), sb("qe", [P, KB, ROWS])
            qq, qz = two("qq", [P, KB, ROWS]), two("qz", [P, KB, ROWS])
            den, z = sb("den", [P, T * ATTN_HEADS]), two("z", [P, T * ATTN_HEADS])
            zT = sb("zT", [ATTN_HEADS, ROWS])
            hh = two("hh", [P, T, D])
            junk, junk2 = sb("junk2", [P, T, D]), sb("junk3", [P, T, D])
            ssq, r1, r2 = two("ssq", [P, T]), two("r1", [P, T]), two("r2", [P, T])
            t1, x2, base = sb("t1", [P, T, D]), two("x2_", [P, T, D]), two("base", [P, T, D])
            st, mv = sb("st2", [P, T, 6]), two("mv2", [P, T, 2])
            dots = two("dots", [P, T])
            a1, nb = two("a1", [P, T]), two("nb", [P, T])
            fa = two("fa", [P, T])
            aux = two("aux", [P, T, 4])
            wv = two("wv", [P, T])
            pT = ph.enter_context(nc.psum_tensor("p2T", [P, KB, ROWS], F32))
            pQ = ph.enter_context(nc.psum_tensor("p2Q", [P, KB, ROWS], F32))
            pZ = ph.enter_context(nc.psum_tensor("p2Z", [P, KB, ROWS], F32))
            pA = ph.enter_context(nc.psum_tensor("p2A", [P, T, D], F32))
            x_in = [sem(f"x2_loaded{u}") for u in range(RING)]
            g_in = [sem(f"gnn_loaded{u}") for u in range(RING)]
            xg_s, xs_s, xb_s = sem("x_plus_gnn"), sem("xs2_ready"), sem("xn_bias_ready")
            turned, copied = sem("xs2_turned"), sem("xT2_copied")
            q_rdy, q_neg, q_exp, q_elu = sem("q_ready"), sem("q_negative_part"), sem("q_exp"), sem("q_elu")
            den_rdy, den_c, z_rdy = sem("den_ready"), sem("den_copied"), sem("z_ready")
            zt_rdy, zt_c, zb_rdy, qz_s = sem("zT_ready"), sem("zT_copied"), sem("z_spread"), sem("q_normalised")
            at_rdy, h_s, sq_s = sem("attention_ready"), sem("h_ready"), sem("h_squares")
            ms_s, r_s = sem("h_mean_square"), sem("h_rms_ready")
            t1_s, t2_s, x2_s = sem("h_rms_normed"), sem("h_sum"), sem("x2_ready")
            st_s, ag_s, dt_s = sem("x2_stats"), sem("x2_aggregated"), sem("x2_router_dot")
            ve_s, rr_s, a1_s, nb_s = sem("x2_var_eps"), sem("x2_rstd"), sem("x2_plus_one"), sem("x2_shift")
            f_s, w_s, aux_s, wv_s = sem("x2_undo"), sem("router_scaled"), sem("aux_ready"), sem("router_ready")
            base_s = sem("base_ready")
            o_out = [sem(f"base_stored{u}") for u in range(2)]
            a_out = [sem(f"aux_stored{u}") for u in range(2)]
            auxz = sem("aux_blank")

            def fresh(g, k=2):
                return isinstance(g.n, int) and g.n < k

            def run(eng, step, end):
                run_steps(eng, step, RING, NG - 2 - (NG - 2) % RING - RING, end, mod=RING)

            with nc.Block() as block:
                @block.sync
                def _(sp):
                    def load(g):
                        if not fresh(g, RING):
                            wait_apart(sp, xg_s, g.n + 1 - RING)
                            wait_apart(sp, xs_s, T * (g.n + 1 - RING))
                        sp.dma_start(xin[g.buf][:].rearrange("p j d -> p (j d)"), group_rows(x, g, D)).then_inc(x_in[g.buf], 16)
                        sp.dma_start(gin[g.buf][:].rearrange("p j d -> p (j d)"), group_rows(gnn_d, g, D)).then_inc(g_in[g.buf], 16)

                    def store(g):
                        u = g.pair.buf
                        wait_apart(sp, base_s, T * (g.n + 1))
                        if isinstance(g.n, int) and g.n == NG - 1:
                            sp.wait_ge(o_out[1 - u], 16 * (NG // 2))
                            sp.wait_ge(a_out[1 - u], 32 * (NG // 2))
                        sp.dma_start(group_rows(out, g, D), base[u][:].rearrange("p j d -> p (j d)")).then_inc(o_out[u], 16)
                        wait_apart(sp, aux_s, g.n + 1)
                        wait_apart(sp, wv_s, g.n + 1)
                        sp.dma_start(group_rows(aux_d, g, 4), aux[u][:].rearrange("p j d -> p (j d)")).then_inc(a_out[u], 16)
                        sp.dma_start(group_rows(wt_d, g, 1), wv[u][:]).then_inc(a_out[u], 16)
                    load(at_step(0, RING))
                    load(at_step(1, RING))

                    def step(g):
                        if (g + 2).inside(0, NG):
                            load(g + 2)
                        if (g + -4).inside(0, NG):
                            store(g + -4)
                    run(sp, step, NG + 4)
                    for u in range(2):
                        sp.wait_ge(o_out[u], 16 * (NG // 2))
                        sp.wait_ge(a_out[u], 32 * (NG // 2))

                @block.gpsimd
                def _(pool):
                    for u in range(2):
                        pool.memset(aux[u][:], 0.0).then_inc(auxz, 1)
                    pool.wait_ge(auxz, 2)

                    def add_gnn(g):
                        pool.wait_ge(x_in[g.buf], 16 * (g.turn + 1))
                        wait_apart(pool, g_in[g.buf], 16 * (g.turn + 1))
                        if not fresh(g, RING):
                            wait_apart(pool, x2_s, g.n + 1 - RING)
                        pool.tensor_tensor(xg[g.buf][:], xin[g.buf][:], gin[g.buf][:], ALU.add).then_inc(xg_s, 1)

                    def rms(g):
                        u = g.pair.buf
                        wait_apart(pool, sq_s, T * (g.n + 1))
                        if not fresh(g):
                            wait_apart(pool, t1_s, T * (g.n - 1))
                        pool.tensor_scalar(r1[u][:], ssq[u][:], 1.0 / D, RMS_EPS, ALU.mult, ALU.add).then_inc(ms_s, 1)
                        wait_apart(pool, ms_s, g.n + 1)
                        pool.tensor_tensor(r1[u][:], r1[u][:], halfneg[:, 0:T], ALU.pow).then_inc(r_s, 1)

                    def second_norm(g):
                        u = g.pair.buf
                        wait_apart(pool, ag_s, T * (g.n + 1))
                        if not fresh(g):
                            pool.wait_ge(base_s, T * (g.n - 1))
                            pool.wait_ge(f_s, g.n - 1)
                            wait_apart(pool, a_out[u], 32 * g.pair.turn)
                        pool.tensor_scalar(r2[u][:], mv[u][:, :, 1], LN_EPS, 1.0, ALU.add, ALU.mult).then_inc(ve_s, 1)
                        wait_apart(pool, ve_s, g.n + 1)
                        pool.tensor_tensor(r2[u][:], r2[u][:], halfneg[:, 0:T], ALU.pow).then_inc(rr_s, 1)
                        wait_apart(pool, rr_s, g.n + 1)
                        pool.tensor_scalar(a1[u][:], r2[u][:], 1.0, 1.0, ALU.add, ALU.mult).then_inc(a1_s, 1)
                        pool.tensor_tensor(nb[u][:], mv[u][:, :, 0], r2[u][:], ALU.mult).then_inc(nb_s, 1)
                        wait_apart(pool, nb_s, 2 * g.n + 1)
                        pool.tensor_scalar(nb[u][:], nb[u][:], -1.0, 1.0, ALU.mult, ALU.mult).then_inc(nb_s, 1)
                        wait_apart(pool, dt_s, T * (g.n + 1))
                        pool.tensor_tensor(dots[u][:], dots[u][:], r2[u][:], ALU.mult).then_inc(w_s, 1)
                        wait_apart(pool, w_s, g.n + 1)
                        pool.tensor_scalar(wv[u][:], dots[u][:], br_b[:, 0:1], 1.0, ALU.add, ALU.mult).then_inc(wv_s, 1)

                    def step(g):
                        if g.inside(0, NG):
                            add_gnn(g)
                        if (g + -3).inside(0, NG):
                            second_norm(g + -3)
                        if (g + -2).inside(0, NG):
                            rms(g + -2)
                    run(pool, step, NG + 3)

                @block.vector
                def _(dve):
                    def elu_q(g):
                        dve.wait_ge(q_exp, g.n + 1)
                        if not fresh(g):
                            dve.wait_ge(qz_s, g.n - 1)
                        dve.scalar_tensor_tensor(out=qq[g.pair.buf][:], in0=pQ[:], scalar=0.0, in1=qe[:],
                                                 op0=ALU.max, op1=ALU.add).then_inc(q_elu, 1)

                    def norm_q(g):
                        u = g.pair.buf
                        dve.wait_ge(zb_rdy, g.n + 1)
                        if not fresh(g):
                            dve.wait_ge(at_rdy, g.n - 1)
                        dve.tensor_tensor(qz[u][:], pZ[:], qq[u][:], ALU.mult).then_inc(qz_s, 1)

                    def bias_x(g):
                        u = g.pair.buf
                        dve.wait_ge(xs_s, T * (g.n + 1))
                        if not fresh(g):
                            dve.wait_ge(h_s, g.n - 1)
                        for j in range(T):
                            dve.scalar_tensor_tensor(out=xb[u][:, j, :], in0=xs[u][:, j, :],
                                                     scalar=back_a[:, bass.ds(T * g.n + j, 1)], in1=bout_b[:],
                                                     op0=ALU.mult, op1=ALU.add).then_inc(xb_s, 1)

                    def residual(g):
                        u = g.pair.buf
                        dve.wait_ge(at_rdy, g.n + 1)
                        dve.wait_ge(xb_s, T * (g.n + 1))
                        if not fresh(g):
                            dve.wait_ge(t2_s, g.n - 1)
                        dve.tensor_tensor(hh[u][:], pA[:], xb[u][:], ALU.add).then_inc(h_s, 1)

                    def recip_den(g):
                        dve.wait_ge(den_rdy, g.n + 1)
                        dve.tensor_scalar(den[:], pZ[:, 1, 0:T * ATTN_HEADS], ATTN_EPS, None, ALU.add).then_inc(den_c, 1)
                        dve.wait_ge(den_c, g.n + 1)
                        if not fresh(g):
                            dve.wait_ge(zt_rdy, g.n - 1)
                        dve.reciprocal(z[g.pair.buf][:], den[:]).then_inc(z_rdy, 1)

                    def finish_x2(g):
                        u = g.pair.buf
                        dve.wait_ge(r_s, g.n + 1)
                        for j in range(T):
                            dve.scalar_tensor_tensor(out=t1[:, j, :], in0=hh[u][:, j, :], scalar=r1[u][:, j:j + 1],
                                                     in1=wn2_b[:], op0=ALU.mult, op1=ALU.mult).then_inc(t1_s, 1)
                        dve.wait_ge(t1_s, T * (g.n + 1))
                        dve.tensor_tensor(t1[:], t1[:], hh[u][:], ALU.add).then_inc(t2_s, 1)
                        dve.wait_ge(t2_s, g.n + 1)
                        dve.wait_ge(xg_s, g.n + 1)
                        if not fresh(g):
                            dve.wait_ge(base_s, T * (g.n - 1))
                            dve.wait_ge(nb_s, 2 * (g.n - 1))
                        dve.tensor_tensor(x2[u][:], t1[:], xg[g.buf][:], ALU.add).then_inc(x2_s, 1)
                        dve.wait_ge(x2_s, g.n + 1)
                        for j in range(T):
                            dve.bn_stats(st[:, j, :], x2[u][:, j, :]).then_inc(st_s, 1)
                        if not fresh(g):
                            wait_apart(dve, aux_s, g.n - 1)
                        for j in range(T):
                            wait_apart(dve, st_s, T * g.n + j + 1)
                            dve.bn_aggr(mv[u][:, j, :], st[:, j, :]).then_inc(ag_s, 1)
                        if not fresh(g):
                            dve.wait_ge(wv_s, g.n - 1)
                        if not fresh(g, 1):
                            dve.wait_ge(dt_s, T * g.n)
                        for j in range(T):
                            dve.tensor_tensor_reduce(junk[:, j, :], x2[u][:, j, :], wr_b[:], 1.0, 0.0, ALU.mult, ALU.add,
                                                     dots[u][:, j:j + 1]).then_inc(dt_s, 1)

                    def make_aux(g):
                        u = g.pair.buf
                        dve.wait_ge(a1_s, g.n + 1)
                        dve.wait_ge(wv_s, g.n + 1)
                        dve.reciprocal(fa[u][:], a1[u][:]).then_inc(f_s, 1)
                        dve.wait_ge(f_s, g.n + 1)
                        if not fresh(g):
                            dve.wait_ge(a_out[u], 32 * g.pair.turn)
                        dve.tensor_copy(aux[u][:, :, 0], mv[u][:, :, 0])
                        dve.tensor_tensor(aux[u][:, :, 1], fa[u][:], r2[u][:], ALU.mult)
                        dve.tensor_copy(aux[u][:, :, 2], wv[u][:]).then_inc(aux_s, 1)

                    dve.wait_ge(auxz, 2)

                    def step(g):
                        if (g + -1).inside(0, NG):
                            recip_den(g + -1)
                        if (g + -3).inside(0, NG):
                            finish_x2(g + -3)
                        if g.inside(0, NG):
                            elu_q(g)
                        if (g + -2).inside(0, NG):
                            residual(g + -2)
                        if (g + -1).inside(0, NG):
                            norm_q(g + -1)
                        if g.inside(0, NG):
                            bias_x(g)
                        if (g + -4).inside(0, NG):
                            make_aux(g + -4)
                    run(dve, step, NG + 4)

                @block.scalar
                def _(act):
                    def scale_x(g):
                        u = g.pair.buf
                        act.wait_ge(x_in[g.buf], 16 * (g.turn + 1))
                        if not fresh(g):
                            act.wait_ge(turned, g.n - 1)
                            act.wait_ge(xb_s, T * (g.n - 1))
                        for j in range(T):
                            act.activation(xs[u][:, j, :], xin[g.buf][:, j, :], ACT.Identity,
                                           bias=shift_a[:, bass.ds(T * g.n + j, 1)],
                                           scale=scale_a[:, bass.ds(T * g.n + j, 1)]).then_inc(xs_s, 1)

                    def exp_q(g):
                        act.wait_ge(q_rdy, g.n + 1)
                        if not fresh(g, 1):
                            act.wait_ge(q_exp, g.n)
                        act.activation(qn[:], pQ[:], ACT.Relu, scale=-1.0).then_inc(q_neg, 1)
                        act.wait_ge(q_neg, g.n + 1)
                        if not fresh(g, 1):
                            act.wait_ge(q_elu, g.n)
                        act.activation(qe[:], qn[:], ACT.Exp, scale=-1.0).then_inc(q_exp, 1)

                    def copy_z(g):
                        act.wait_ge(zt_rdy, g.n + 1)
                        if not fresh(g, 1):
                            act.wait_ge(zb_rdy, g.n)
                        act.activation(zT[:], pZ[0:ATTN_HEADS, 0, :], ACT.Copy).then_inc(zt_c, 1)

                    def make_base(g):
                        u = g.pair.buf
                        act.wait_ge(a1_s, g.n + 1)
                        act.wait_ge(nb_s, 2 * (g.n + 1))
                        act.wait_ge(x2_s, g.n + 1)
                        if not fresh(g):
                            act.wait_ge(o_out[u], 16 * g.pair.turn)
                        for j in range(T):
                            act.activation(base[u][:, j, :], x2[u][:, j, :], ACT.Identity, bias=nb[u][:, j:j + 1],
                                           scale=a1[u][:, j:j + 1]).then_inc(base_s, 1)

                    def copy_x(g):
                        act.wait_ge(turned, g.n + 1)
                        if not fresh(g):
                            act.wait_ge(q_rdy, g.n - 1)
                        act.activation(xT[g.pair.buf][:], pT[:], ACT.Copy).then_inc(copied, 1)

                    def squares(g):
                        u = g.pair.buf
                        act.wait_ge(h_s, g.n + 1)
                        if not fresh(g):
                            act.wait_ge(ms_s, g.n - 1)
                        if not fresh(g, 1):
                            act.wait_ge(sq_s, T * g.n)
                        for j in range(T):
                            act.activation(junk2[:, j, :], hh[u][:, j, :], ACT.Square, accum_out=ssq[u][:, j:j + 1])\
                               .then_inc(sq_s, 1)
                    scale_x(at_step(0, RING))
                    copy_x(at_step(0, RING))

                    def step(g):
                        if (g + 1).inside(0, NG):
                            scale_x(g + 1)
                        if (g + -4).inside(0, NG):
                            make_base(g + -4)
                        if g.inside(0, NG):
                            exp_q(g)
                        if (g + -1).inside(0, NG):
                            copy_z(g + -1)
                        if (g + -2).inside(0, NG):
                            squares(g + -2)
                        if (g + 1).inside(0, NG):
                            copy_x(g + 1)
                    run(act, step, NG + 4)

                @block.tensor
                def _(pe):
                    def turn(g):
                        pe.wait_ge(xs_s, T * (g.n + 1))
                        if not fresh(g, 1):
                            pe.wait_ge(copied, g.n)
                        for j in range(T):
                            for k in range(KB):
                                last = pe.transpose(pT[:, k, j * P:(j + 1) * P], xs[g.pair.buf][:, j, k * P:(k + 1) * P],
                                                    ident[:])
                        last.then_inc(turned, 1)

                    def project(g):
                        pe.wait_ge(copied, g.n + 1)
                        if not fresh(g, 1):
                            pe.wait_ge(q_elu, g.n)
                        for m in range(KB):
                            for k in range(KB):
                                last = pe.matmul(pQ[:, m, :], wqkv[:, k, m * P:(m + 1) * P], xT[g.pair.buf][:, k, :],
                                                 start=(k == 0), stop=(k == KB - 1))
                        last.then_inc(q_rdy, 1)

                    def turn_z(g):
                        pe.wait_ge(z_rdy, g.n + 1)
                        if not fresh(g, 1):
                            pe.wait_ge(qz_s, g.n)
                        for j in range(T):
                            last = pe.transpose(pZ[0:ATTN_HEADS, 0, j * P:(j + 1) * P],
                                                z[g.pair.buf][:, ATTN_HEADS * j:ATTN_HEADS * (j + 1)], ident[:])
                        last.then_inc(zt_rdy, 1)

                    def spread_z(g):
                        pe.wait_ge(zt_c, g.n + 1)
                        for m in range(KB):
                            last = pe.matmul(pZ[:, m, :], spread8[:, m, :], zT[:], start=True, stop=True)
                        last.then_inc(zb_rdy, 1)

                    def attend(g):
                        pe.wait_ge(qz_s, g.n + 1)
                        if not fresh(g, 1):
                            pe.wait_ge(h_s, g.n)
                        for j in range(T):
                            for k in range(KB):
                                last = pe.matmul(pA[:, j, :], qz[g.pair.buf][:, k, j * P:(j + 1) * P], mix[:, k, :],
                                                 start=(k == 0), stop=(k == KB - 1))
                        last.then_inc(at_rdy, 1)

                    def denominators(g):
                        pe.wait_ge(q_elu, g.n + 1)
                        if not fresh(g, 1):
                            pe.wait_ge(qz_s, g.n)
                        for j in range(T):
                            for k in range(KB):
                                last = pe.matmul(pZ[:, 1, ATTN_HEADS * j:ATTN_HEADS * (j + 1)],
                                                 qq[g.pair.buf][:, k, j * P:(j + 1) * P], ks8[:, k, :],
                                                 start=(k == 0), stop=(k == KB - 1))
                        last.then_inc(den_rdy, 1)

                    turn(at_step(0, RING))

                    def step(g):
                        if g.inside(0, NG):
                            project(g)
                        if (g + -1).inside(0, NG):
                            turn_z(g + -1)
                        if (g + -2).inside(0, NG):
                            attend(g + -2)
                        if (g + -1).inside(0, NG):
                            spread_z(g + -1)
                        if (g + 1).inside(0, NG):
                            turn(g + 1)
                        if g.inside(0, NG):
                            denominators(g)
                    run(pe, step, NG + 2)

        w1h, w1l = keep("w1h", [P, KB, H], F32R), keep("w1l", [P, KB, H], F32R)
        w2h, w2l = keep("w2h", [P, FB, D], F32R), keep("w2l", [P, FB, D], F32R)
        ctab = keep("ctab", [TP, TC + 3], F16)
        bounds = keep("bounds", [TP, 2])
        with phase() as ph:
            def sb(name, shape, dt=F32):
                return ph.enter_context(nc.sbuf_tensor(name, shape, dt))
            w1s, w2s = sb("w1s", [P, KB, H]), sb("w2s", [P, FB, D])
            w = sb("w", [TP, TC])
            sgn = sb("sgn", [TP, TC], I32)
            key = sb("key", [TP, TC], I32)
            half_i = sb("half_i", [TP, 2, TC], I32)
            hi = sb("hi", [TP, TC])
            lo = sb("lo", [TP, TC])
            m1 = sb("m1", [TP, TC])
            m2 = sb("m2", [TP, TC])
            m3 = sb("m3", [TP, TC])
            fill1 = sb("fill1", [TP, TC])
            scr = sb("scr", [TP, TC])
            thr = sb("thr", [TP, 2])
            bit = sb("bit", [TP, 2])
            cand = sb("cand", [TP, 1])
            cnt = sb("cntp", [TP, 1])
            hit = sb("hit", [TP, 1])
            tot = sb("totp", [TP, 2])
            need = sb("need", [TP, 1])
            offi = sb("offi", [TP, 3], I32)
            pC = ph.enter_context(nc.psum_tensor("pC", [P, 512], F32))
            pc = sem("selection_loaded")
            c_ = sem("selection_chain")
            total = sem("count_total")
            cnts = sem("count_ready")
            pid = sem("partition_ids")
            wh_s, wl_s = sem("weights_high"), sem("weights_low")
            with nc.Block() as block:
                @block.sync
                def _(sp):
                    sp.dma_start(w[:], wt_d.rearrange("(p c) o -> p (c o)", c=TC)).then_inc(pc, 16)
                    sp.dma_start(w1s[:], w1.rearrange("(k p) n -> p k n", p=P)).then_inc(pc, 16)
                    sp.dma_start(w2s[:], w2.rearrange("(k p) n -> p k n", p=P)).then_inc(pc, 16)
                    sp.wait_ge(pc, 48)

                @block.gpsimd
                def _(pool):
                    pool.iota(offi[:, 2:3], pattern=[[0, 1]], base=0, channel_multiplier=1).then_inc(pid, 1)
                    for n, (low, w32, high) in enumerate(((w1l, w1s, w1h), (w2l, w2s, w2h))):
                        pool.wait_ge(wh_s, n + 1)
                        pool.tensor_tensor(low[:], w32[:], high[:].bitcast(F32), ALU.subtract).then_inc(wl_s, 1)

                @block.scalar
                def _(act):
                    act.wait_ge(pc, 48)
                    act.activation(w1h[:], w1s[:], ACT.Copy).then_inc(wh_s, 1)
                    act.activation(w2h[:], w2s[:], ACT.Copy).then_inc(wh_s, 1)

                @block.tensor
                def _(pe):
                    with pe.Fori(0, 32) as i:
                        pe.wait_ge(cnts, i + 1)
                        pe.matmul(pC[0:TP, 0:1], ones[0:TP, 0:TP], cnt[:], start=True, stop=True).then_inc(total, 1)
                    pe.wait_ge(cnts, 33)
                    pe.matmul(pC[0:TP, 0:1], ones[0:TP, 0:TP], cnt[:], start=True, stop=True).then_inc(total, 1)
                    for i in range(2):
                        pe.wait_ge(cnts, 34 + i)
                        pe.matmul(pC[0:TP, 0:1], after[0:TP, 0:TP], tot[:, i:i + 1], start=True, stop=True).then_inc(total, 1)

                @block.vector
                def _(dve):
                    done = [0]

                    def link(ins):
                        done[0] += 1
                        ins.then_inc(c_, 1)
                        dve.wait_ge(c_, done[0])
                    dve.memset(fill1[:], 1.0)
                    dve.memset(thr[:], 0.0)
                    link(dve.memset(bit[:], 32768.0))
                    dve.wait_ge(pc, 48)
                    wi = w[:].bitcast(I32)
                    link(dve.tensor_scalar(sgn[:], wi, 31, None, ALU.arith_shift_right))
                    link(dve.tensor_scalar(sgn[:], sgn[:], -2147483648, None, ALU.bitwise_or))
                    link(dve.tensor_tensor(key[:], sgn[:], wi, ALU.bitwise_xor))
                    link(dve.tensor_scalar(half_i[:, 0, :], key[:], 16, None, ALU.logical_shift_right))
                    link(dve.tensor_scalar(half_i[:, 1, :], key[:], 65535, None, ALU.bitwise_and))
                    link(dve.tensor_copy(hi[:], half_i[:, 0, :]))
                    link(dve.tensor_copy(lo[:], half_i[:, 1, :]))

                    def search(vals, col, base_n):
                        per = 5
                        c0 = done[0]
                        with dve.Fori(0, 16) as i:
                            dve.tensor_tensor(cand[:], thr[:, col:col + 1], bit[:, col:col + 1], ALU.add).then_inc(c_, 1)
                            dve.wait_ge(c_, c0 + per * i + 1)
                            dve.tensor_scalar(scr[:], vals[:], cand[:, 0:1], None, ALU.is_ge, ALU.add,
                                              accum_out=cnt[:]).then_inc(cnts, 1)
                            dve.wait_ge(total, base_n + i + 1)
                            dve.tensor_scalar(hit[:], pC[0:TP, 0:1], float(CAP), None, ALU.is_ge).then_inc(c_, 1)
                            dve.wait_ge(c_, c0 + per * i + 2)
                            dve.tensor_tensor(hit[:], hit[:], bit[:, col:col + 1], ALU.mult).then_inc(c_, 1)
                            dve.wait_ge(c_, c0 + per * i + 3)
                            dve.tensor_tensor(thr[:, col:col + 1], thr[:, col:col + 1], hit[:], ALU.add).then_inc(c_, 1)
                            dve.tensor_scalar(bit[:, col:col + 1], bit[:, col:col + 1], 0.5, None, ALU.mult).then_inc(c_, 1)
                            dve.wait_ge(c_, c0 + per * i + 5)
                        done[0] += per * 16
                    search(hi, 0, 0)
                    link(dve.tensor_scalar(m1[:], hi[:], thr[:, 0:1], 70000.0, ALU.is_gt, ALU.mult))
                    link(dve.tensor_scalar(m2[:], hi[:], thr[:, 0:1], None, ALU.is_equal))
                    link(dve.scalar_tensor_tensor(out=m2[:], in0=lo[:], scalar=1.0, in1=m2[:], op0=ALU.add, op1=ALU.mult))
                    link(dve.scalar_tensor_tensor(out=lo[:], in0=m2[:], scalar=-1.0, in1=m1[:], op0=ALU.add, op1=ALU.add))
                    search(lo, 1, 16)
                    dve.tensor_scalar(m1[:], lo[:], thr[:, 1:2], None, ALU.is_gt, ALU.add, accum_out=cnt[:]).then_inc(cnts, 1)
                    link(dve.tensor_scalar(m2[:], lo[:], thr[:, 1:2], None, ALU.is_equal))
                    dve.wait_ge(total, 33)
                    link(dve.tensor_scalar(need[:], pC[0:TP, 0:1], -1.0, float(CAP), ALU.mult, ALU.add))
                    link(dve.tensor_tensor_scan(m3[:], fill1[:], m2[:], 0.0, ALU.mult, ALU.add))
                    dve.tensor_copy(tot[:, 0:1], m3[:, TC - 1:TC]).then_inc(cnts, 1)
                    dve.wait_ge(total, 34)
                    link(dve.tensor_scalar(m3[:], m3[:], pC[0:TP, 0:1], need[:, 0:1], ALU.add, ALU.is_le))
                    link(dve.tensor_tensor(m2[:], m2[:], m3[:], ALU.mult))
                    link(dve.tensor_tensor(m1[:], m1[:], m2[:], ALU.add))
                    link(dve.tensor_tensor_scan(m3[:], fill1[:], m1[:], 0.0, ALU.mult, ALU.add))
                    dve.tensor_copy(tot[:, 1:2], m3[:, TC - 1:TC]).then_inc(cnts, 1)
                    dve.wait_ge(total, 35)
                    link(dve.tensor_copy(bounds[:, 0:1], pC[0:TP, 0:1]))
                    link(dve.tensor_tensor(bounds[:, 1:2], bounds[:, 0:1], tot[:, 1:2], ALU.add))
                    link(dve.tensor_copy(offi[:, 0:1], bounds[:, 0:1]))
                    link(dve.tensor_scalar(offi[:, 1:2], offi[:, 0:1], 63, None, ALU.bitwise_and))
                    link(dve.tensor_copy(cand[:], offi[:, 1:2]))
                    dve.wait_ge(pid, 1)
                    link(dve.tensor_copy(ctab[:, 0:TC], m3[:]))
                    link(dve.tensor_tensor(ctab[:, TC:TC + 1], bounds[:, 0:1], cand[:], ALU.subtract))
                    link(dve.tensor_copy(ctab[:, TC + 1:TC + 2], cand[:]))
                    link(dve.tensor_copy(ctab[:, TC + 2:TC + 3], offi[:, 2:3]))

        with phase() as ph:
            def sb(name, shape, dt=F32):
                return ph.enter_context(nc.sbuf_tensor(name, shape, dt))

            def two(name, shape, dt=F32):
                return [sb(f"{name}{u}", shape, dt) for u in range(2)]
            def some(k, name, shape, dt=F32):
                return [sb(f"{name}{u}", shape, dt) for u in range(k)]
            RING = 4
            rank0 = sb("rank0", [TP, ROWS])
            rank0i = sb("rank0i", [TP, ROWS], I32)
            slot_i = sb("slot_i", [P, T], I32)
            slot = sb("slot", [P, T])
            below = sb("below", [TP, ROWS], F16)
            pick = sb("pick", [TP, ROWS], F16)
            rk = sb("rk", [P, 2 * T])
            cntj = sb("cntj", [P, 3 * T])
            past = sb("past", [P, T])
            scr = sb("scr2", [P, TC])
            tok = some(RING, "tok", [P, T], I32)
            brow = some(RING, "brow", [P, T, D])
            axr = some(RING, "axr", [P, T, 4])
            yn = sb("yn", [P, T, D])
            yTh, yTl = sb("yTh", [P, KB, ROWS], F32R), sb("yTl", [P, KB, ROWS], F32R)
            act32 = some(4, "act32", [P, ROWS])
            hTh, hTl = sb("hTh", [P, FB, ROWS], F32R), sb("hTl", [P, FB, ROWS], F32R)
            res = some(2, "res", [P, T, D])
            o1 = sb("o1", [P, T, D])
            pC = [ph.enter_context(nc.psum_tensor(f"pC{u}", [P, 512], F32)) for u in range(2)]
            pT = ph.enter_context(nc.psum_tensor("p3T", [P, KB, ROWS], F32))
            pH = [ph.enter_context(nc.psum_tensor(f"p3H{u}", [P, 512], F32)) for u in range(2)]
            pY = ph.enter_context(nc.psum_tensor("p3Y", [P, T, D], F32))
            ini, ini_f, blank2 = sem("ranks_made"), sem("ranks_float"), sem("row_buffers_blank")
            bl_s, pk_s, bd_s, pa_s, sl_s = sem("below_ready"), sem("pick_ready"), sem("bounds_moved"), sem("past_end"), sem("slots_moved")
            ct_s, rk_s, cj_s = sem("rows_looked_up"), sem("ranks_ready"), sem("tokens_counted")
            tk_s, tf_s = sem("token_parts"), sem("token_ready")
            fetch = [sem(f"rows_fetched{u}") for u in range(RING)]
            yn_s, yt_s, yh_s, yl_s = sem("yn_ready"), sem("yn_turned"), sem("yT_high_ready"), sem("yT_low_ready")
            h_s, ge_s, g_s, gl_s, y_s = sem("hidden_ready"), sem("gelu_ready"), sem("hT_high_ready"), sem("hT_low_ready"), sem("y_ready")
            o_s, r_s = sem("y_biased"), sem("result_ready")
            put = [sem(f"rows_put{u}") for u in range(RING)]

            def fresh(g, k=2):
                return isinstance(g.n, int) and g.n < k

            def run(eng, step, end):
                run_steps(eng, step, 4, NF - 1 - (NF - 1) % 4 - 4, end, mod=RING)

            with nc.Block() as block:
                @block.gpsimd
                def _(pool):
                    pool.iota(rank0i[:], pattern=[[1, ROWS]], base=0, channel_multiplier=0).then_inc(ini, 1)
                    pool.iota(slot_i[:], pattern=[[P, T]], base=0, channel_multiplier=1).then_inc(ini, 1)
                    pool.wait_ge(blank2, 2 * RING)

                    def fetch_rows(g):
                        wait_apart(pool, tf_s, g.n + 1)
                        if not fresh(g, RING):
                            wait_apart(pool, r_s, T * (g.n + 1 - RING))
                        for j in range(T):
                            for t, table in ((brow, out), (axr, aux_d)):
                                pool.indirect_dma_start(
                                    out=t[g.buf][:, j, :], out_offset=None, in_=table,
                                    in_offset=bass.IndirectOffsetOnAxis(ap=tok[g.buf][:, j:j + 1], axis=0),
                                    bounds_check=N - 1, oob_is_err=False).then_inc(fetch[g.buf], 16)

                    def put_rows(g):
                        for j in range(T):
                            wait_apart(pool, r_s, T * g.n + j + 1)
                            pool.indirect_dma_start(
                                out=out, out_offset=bass.IndirectOffsetOnAxis(ap=tok[g.buf][:, j:j + 1], axis=0),
                                in_=res[g.buf % 2][:, j, :], in_offset=None,
                                bounds_check=N - 1, oob_is_err=False).then_inc(put[g.buf], 16)
                    fetch_rows(at_step(0, RING))
                    fetch_rows(at_step(1, RING))

                    def step(g):
                        if (g + 2).inside(0, NF):
                            fetch_rows(g + 2)
                        if (g + -1).inside(0, NF):
                            put_rows(g + -1)
                    run(pool, step, NF + 1)
                    for u in range(RING):
                        pool.wait_ge(put[u], 16 * T * ((NF + RING - 1 - u) // RING))

                @block.vector
                def _(dve):
                    for u in range(RING):
                        dve.memset(brow[u][:], 0.0).then_inc(blank2, 1)
                        dve.memset(axr[u][:], 0.0).then_inc(blank2, 1)
                    dve.wait_ge(ini, 2)
                    dve.tensor_copy(rank0[:], rank0i[:]).then_inc(ini_f, 1)
                    dve.tensor_copy(slot[:], slot_i[:]).then_inc(ini_f, 1)
                    dve.wait_ge(ini_f, 2)

                    def pick_ranks(g):
                        if not fresh(g, 1):
                            dve.wait_ge(bd_s, g.n)
                            dve.wait_ge(ct_s, T * g.n)
                        dve.tensor_scalar(below[:], rank0[:], bounds[:, 0:1], None, ALU.is_ge).then_inc(bl_s, 1)
                        dve.wait_ge(bl_s, g.n + 1)
                        dve.scalar_tensor_tensor(out=pick[:], in0=rank0[:], scalar=bounds[:, 1:2], in1=below[:],
                                                 op0=ALU.is_lt, op1=ALU.mult).then_inc(pk_s, 1)
                        dve.wait_ge(pk_s, g.n + 1)
                        dve.tensor_scalar(bounds[:], bounds[:], -float(ROWS), None, ALU.add).then_inc(bd_s, 1)

                    def find_tokens(g):
                        if not fresh(g, 1):
                            dve.wait_ge(sl_s, g.n)
                        dve.tensor_scalar(past[:], slot[:], float(CAP), SKIP, ALU.is_ge, ALU.mult).then_inc(pa_s, 1)
                        for j in range(T):
                            c = pC[j % 2]
                            dve.wait_ge(ct_s, T * g.n + j + 1)
                            dve.tensor_tensor(rk[:, j:j + 1], slot[:, j:j + 1], c[:, TC:TC + 1], ALU.subtract).then_inc(rk_s, 1)
                            dve.wait_ge(rk_s, 2 * (T * g.n + j) + 1)
                            dve.tensor_tensor(rk[:, T + j:T + j + 1], rk[:, j:j + 1], c[:, TC + 1:TC + 2], ALU.subtract)\
                               .then_inc(rk_s, 1)
                            dve.wait_ge(rk_s, 2 * (T * g.n + j) + 2)
                            dve.tensor_scalar(cntj[:, T + j:T + j + 1], c[:, TC + 2:TC + 3], float(TC), None, ALU.mult)\
                               .then_inc(tk_s, 1)
                            if not (fresh(g, 1) and j == 0):
                                dve.wait_ge(cj_s, T * g.n + j)
                            dve.tensor_scalar(scr[:], c[:, 0:TC], rk[:, T + j:T + j + 1], None, ALU.is_le, ALU.add,
                                              accum_out=cntj[:, j:j + 1]).then_inc(cj_s, 1)
                        dve.wait_ge(cj_s, T * (g.n + 1))
                        dve.wait_ge(tk_s, T * (g.n + 1) + g.n)
                        dve.wait_ge(pa_s, g.n + 1)
                        dve.tensor_tensor(cntj[:, 2 * T:3 * T], cntj[:, 0:T], cntj[:, T:2 * T], ALU.add).then_inc(tk_s, 1)
                        dve.wait_ge(tk_s, (T + 1) * (g.n + 1))
                        if not fresh(g, RING):
                            dve.wait_ge(put[g.buf], 16 * T * g.turn)
                        dve.tensor_tensor(tok[g.buf][:], cntj[:, 2 * T:3 * T], past[:], ALU.add).then_inc(tf_s, 1)
                        dve.tensor_scalar(slot[:], slot[:], float(ROWS), None, ALU.add).then_inc(sl_s, 1)

                    def norm_rows(g):
                        u = g.buf
                        dve.wait_ge(fetch[u], 32 * T * (g.turn + 1))
                        if not fresh(g, 1):
                            dve.wait_ge(yt_s, g.n)
                        for j in range(T):
                            dve.tensor_scalar(yn[:, j, :], brow[u][:, j, :], axr[u][:, j, 0:1], axr[u][:, j, 1:2],
                                              ALU.subtract, ALU.mult).then_inc(yn_s, 1)

                    def low_y(g):
                        dve.wait_ge(yh_s, g.n + 1)
                        dve.tensor_tensor(yTl[:], pT[:], yTh[:].bitcast(F32), ALU.subtract).then_inc(yl_s, 1)

                    def low_hidden(g):
                        for f in range(FB):
                            dve.wait_ge(g_s, FB * g.n + f + 1)
                            dve.tensor_tensor(hTl[:, f, :], act32[f % 4][:], hTh[:, f, :].bitcast(F32), ALU.subtract)\
                               .then_inc(gl_s, 1)

                    def finish_rows(g):
                        u = g.buf
                        for h in range(2):
                            dve.wait_ge(y_s, 2 * g.n + h + 1)
                            if not fresh(g, 1) and h == 0:
                                dve.wait_ge(r_s, T * g.n)
                            dve.tensor_tensor(o1[:, 2 * h:2 * h + 2, :], pY[:, 2 * h:2 * h + 2, :],
                                              b2_b[:].unsqueeze(1).to_broadcast([P, 2, D]), ALU.add).then_inc(o_s, 1)
                        if not fresh(g, 2):
                            before_g = g + -2
                            dve.wait_ge(put[before_g.buf], 16 * T * (before_g.turn + 1))
                        dve.wait_ge(o_s, 2 * (g.n + 1))
                        for j in range(T):
                            dve.scalar_tensor_tensor(out=res[u % 2][:, j, :], in0=o1[:, j, :], scalar=axr[u][:, j, 2:3],
                                                     in1=brow[u][:, j, :], op0=ALU.mult, op1=ALU.add).then_inc(r_s, 1)
                    for n in range(3):
                        pick_ranks(at_step(n, RING))
                        find_tokens(at_step(n, RING))
                    norm_rows(at_step(0, RING))
                    low_y(at_step(0, RING))

                    def step(g):
                        if (g + 3).inside(0, NF):
                            pick_ranks(g + 3)
                        if (g + 1).inside(0, NF):
                            norm_rows(g + 1)
                        if (g + -1).inside(0, NF):
                            finish_rows(g + -1)
                        if g.inside(0, NF):
                            low_hidden(g)
                        if (g + 1).inside(0, NF):
                            low_y(g + 1)
                        if (g + 3).inside(0, NF):
                            find_tokens(g + 3)
                    run(dve, step, NF + 1)

                @block.scalar
                def _(act):
                    def high_y(g):
                        act.wait_ge(yt_s, g.n + 1)
                        act.activation(yTh[:], pT[:], ACT.Copy).then_inc(yh_s, 1)

                    def gelu(g, f):
                        act.wait_ge(h_s, FB * g.n + f + 1)
                        if not (fresh(g, 1) and f < 4):
                            act.wait_ge(gl_s, FB * g.n + f - 3)
                        act.activation(act32[f % 4][:], pH[f % 2][:], ACT.Gelu_apprx_tanh, bias=b1c[:, f:f + 1])\
                            .then_inc(ge_s, 1)

                    def high_hidden(g, f):
                        act.wait_ge(ge_s, FB * g.n + f + 1)
                        act.activation(hTh[:, f, :], act32[f % 4][:], ACT.Copy).then_inc(g_s, 1)
                    high_y(at_step(0, RING))

                    def step(g):
                        for f in range(FB):
                            gelu(g, f)
                            high_hidden(g, f)
                        if (g + 1).inside(0, NF):
                            high_y(g + 1)
                    run(act, step, NF)

                @block.tensor
                def _(pe):
                    def look_up(g, js):
                        pe.wait_ge(pk_s, g.n + 1)
                        for j in js:
                            if not (fresh(g, 1) and j < 2):
                                pe.wait_ge(cj_s, T * g.n + j - 1)
                            pe.matmul(pC[j % 2][:, 0:TC + 3], pick[:, j * P:(j + 1) * P], ctab[:], start=True, stop=True)\
                              .then_inc(ct_s, 1)

                    def turn(g):
                        pe.wait_ge(yn_s, T * (g.n + 1))
                        if not fresh(g, 1):
                            pe.wait_ge(yl_s, g.n)
                        for j in range(T):
                            for k in range(KB):
                                last = pe.transpose(pT[:, k, j * P:(j + 1) * P], yn[:, j, k * P:(k + 1) * P], ident[:])
                        last.then_inc(yt_s, 1)

                    def product(target, parts):
                        for n, (left, right) in enumerate(parts):
                            last = pe.matmul(target, left, right, start=(n == 0), stop=(n == len(parts) - 1))
                        return last

                    def up(g):
                        pe.wait_ge(yl_s, g.n + 1)
                        for f in range(FB):
                            if not (fresh(g, 1) and f < 2):
                                pe.wait_ge(ge_s, FB * g.n + f - 1)
                            cols = slice(f * P, (f + 1) * P)
                            product(pH[f % 2][:], [(a[:, k, cols], b[:, k, :]) for k in range(KB)
                                                   for a, b in ((w1h, yTh), (w1h, yTl), (w1l, yTh))]).then_inc(h_s, 1)

                    def down(g, js):
                        pe.wait_ge(gl_s, FB * (g.n + 1))
                        for j in js:
                            if not fresh(g, 1) and j % 2 == 0:
                                pe.wait_ge(o_s, 2 * (g.n - 1) + j // 2 + 1)
                            rows = slice(j * P, (j + 1) * P)
                            last = product(pY[:, j, :], [(a[:, f, rows], b[:, f, :]) for f in range(FB)
                                                         for a, b in ((hTh, w2h), (hTh, w2l), (hTl, w2h))])
                            if j % 2:
                                last.then_inc(y_s, 1)
                    for n in range(3):
                        look_up(at_step(n, RING), range(T))
                    turn(at_step(0, RING))

                    def step(g):
                        up(g)
                        if (g + 1).inside(0, NF):
                            turn(g + 1)
                        if (g + 3).inside(0, NF):
                            look_up(g + 3, range(2))
                        down(g, range(2))
                        if (g + 3).inside(0, NF):
                            look_up(g + 3, range(2, T))
                        down(g, range(2, T))
                    run(pe, step, NF)


_INS = ["x", "src", "dst", "L0_gnn_W", "L0_gnn_Wl", "L0_gnn_Wr", "L0_gnn_b", "L0_mix_w_norm1", "L0_mix_w_qkv",
        "L0_mix_w_out", "L0_mix_b_out", "L0_mix_w_norm2", "L0_ffn_wr", "L0_ffn_br", "L0_ffn_w1", "L0_ffn_b1",
        "L0_ffn_w2", "L0_ffn_b2"]


def kernel(**inputs):
    import numpy as np
    import concourse.bacc as bacc
    from concourse.bass_utils import run_bass_kernel_spmd

    nc = bacc.Bacc("TRN2", target_bir_lowering=False, num_devices=1)
    arrays, args = {}, []
    for name in _INS:
        a = np.ascontiguousarray(inputs[name])
        arrays[f"in_{name}"] = a
        args.append(nc.dram_tensor(f"in_{name}", a.shape, mybir.dt.from_np(a.dtype), kind="ExternalInput").ap())
    out = nc.dram_tensor("out_0", inputs["x"].shape, F32, kind="ExternalOutput").ap()
    gps_layer(nc, *args, out)
    r = run_bass_kernel_spmd(nc, [arrays], core_ids=[0])
    return r.results[0]["out_0"]
```
